# Optimizing a Trainium2 kernel written in Bass

```python
import numpy as np
import jax
import jax.numpy as jnp

def _softmax(x, axis=-1):
    return jax.nn.softmax(x, axis=axis)

def _gelu(x):
    return jax.nn.gelu(x, approximate=True)

def _silu(x):
    return jax.nn.silu(x)

def _sigmoid(x):
    return jax.nn.sigmoid(x)

def _layernorm(x, axis=-1, eps=1e-05):
    m = jnp.mean(x, axis=axis, keepdims=True)
    v = jnp.var(x, axis=axis, keepdims=True)
    return (x - m) / jnp.sqrt(v + eps)

def _scatter_add(tgt, idx, src, axis=0):
    return tgt.at[idx].add(src)

def _segment_sum(src, seg, n):
    return jax.ops.segment_sum(src, seg, n)
kernel_name = 'mk_flamingo_gated_d1_seqx_r4_d19e44'

def setup_inputs(seed: int=0):
    np.random.seed(seed)
    _w = jnp.asarray

    def _rec_inputs():
        import jax
        import jax.numpy as jnp
        _rk = jax.random.key(seed)
        x = 7.22e-05 + 1 * jax.random.normal(jax.random.fold_in(_rk, 1), (4, 512, 256), jnp.float32)
        _lenS = 512 - jax.random.randint(jax.random.fold_in(_rk, 7), (4,), 0, max(1, 512 // 4) + 1, jnp.int32)
        _lenS2 = 1024 - jax.random.randint(jax.random.fold_in(_rk, 8), (4,), 0, max(1, 1024 // 4) + 1, jnp.int32)
        _ctx_768P = jax.random.normal(jax.random.fold_in(_rk, 11), (4, 16, 192), jnp.float32)
        _ctx_768c = jax.random.dirichlet(jax.random.fold_in(_rk, 511), 0.3 * jnp.ones((16,), jnp.float32), (4, 1024))
        _ctx_768t = jnp.einsum('bsk,bkd->bsd', _ctx_768c, _ctx_768P)
        _ctx_768t = _ctx_768t * jax.lax.rsqrt(jnp.mean(jnp.square(_ctx_768t)) + 1e-12) * 0.953939
        ctx_768 = -0.000191848 + 0.999787 * (_ctx_768t + 0.3 * jax.random.normal(jax.random.fold_in(_rk, 611), (4, 1024, 192), jnp.float32))
        _g = jax.random.normal(jax.random.fold_in(_rk, 9001), (2, 1), jnp.float32)
        _g = jnp.sign(_g) * jnp.maximum(jnp.abs(_g), 1.0) + (_g == 0) * 1.0
        g_xattn = _g[0]
        g_ffn = _g[1]
        return (x, ctx_768, g_xattn, g_ffn)
    x, ctx_768, g_xattn, g_ffn = _rec_inputs()

    def _L0_xattn_setup():
        import jax, jax.numpy as jnp
        import numpy as np
        NUM_HEADS = 16
        CLAMP = 10000.0
        key = jax.random.key(seed)
        ks = jax.random.split(key, 8)
        B, Nq, Nkv, Cq, Ckv = (4, 512, 512, 256, 192)
        s_q = 1.0 / np.sqrt(Cq)
        s_kv = 1.0 / np.sqrt(Ckv)
        return {'query': jax.random.normal(ks[0], (B, Nq, Cq), jnp.float32), 'key_value': jax.random.normal(ks[1], (B, Nkv, Ckv), jnp.float32), 'Wq': jax.random.normal(ks[2], (Cq, Cq), jnp.float32) * s_q, 'bq': jnp.zeros((Cq,), jnp.float32), 'Wk': jax.random.normal(ks[3], (Ckv, Cq), jnp.float32) * s_kv, 'bk': jnp.zeros((Cq,), jnp.float32), 'Wv': jax.random.normal(ks[4], (Ckv, Cq), jnp.float32) * s_kv, 'bv': jnp.zeros((Cq,), jnp.float32), 'Wo': jax.random.normal(ks[5], (Cq, Cq), jnp.float32) * s_q, 'bo': jnp.zeros((Cq,), jnp.float32)}
    _L0_xattn_all = _L0_xattn_setup()
    _L0_xattn_in = {k: v for k, v in _L0_xattn_all.items() if k in ('Wq', 'bq', 'Wk', 'bk', 'Wv', 'bv', 'Wo', 'bo')}
    del _L0_xattn_all

    def _L0_ffn_setup():
        import jax, jax.numpy as jnp
        import numpy as np
        D, H, O, E, TOPK = (256, 1024, 256, 8, 2)
        B, S = (4, 256)
        key = jax.random.key(seed)
        ks = jax.random.split(key, 12)
        std = 0.02
        return {'hidden_states': jax.random.normal(ks[0], (B, S, D), dtype=jnp.float32), 'norm_weight': jnp.ones((D,), dtype=jnp.float32), 'router_w': jax.random.normal(ks[1], (E, D), dtype=jnp.float32) * std, 'sw1': jax.random.normal(ks[2], (D, H), dtype=jnp.float32) * (1.0 / np.sqrt(D)), 'sb1': jnp.zeros((H,), dtype=jnp.float32), 'sw2': jax.random.normal(ks[3], (H, O), dtype=jnp.float32) * (1.0 / np.sqrt(H)), 'sb2': jnp.zeros((O,), dtype=jnp.float32), 'ew1': jax.random.normal(ks[4], (E, D, H), dtype=jnp.float32) * (1.0 / np.sqrt(D)), 'eb1': jnp.zeros((E, H), dtype=jnp.float32), 'ew2': jax.random.normal(ks[5], (E, H, O), dtype=jnp.float32) * (1.0 / np.sqrt(H)), 'eb2': jnp.zeros((E, O), dtype=jnp.float32)}
    _L0_ffn_all = _L0_ffn_setup()
    _L0_ffn_in = {k: v for k, v in _L0_ffn_all.items() if k in ('norm_weight', 'router_w', 'sw1', 'sb1', 'sw2', 'sb2', 'ew1', 'eb1', 'ew2', 'eb2')}
    del _L0_ffn_all
    return {'x': x, 'ctx_768': ctx_768, 'g_xattn': g_xattn, 'g_ffn': g_ffn, 'L0_xattn_Wq': _L0_xattn_in['Wq'], 'L0_xattn_bq': _L0_xattn_in['bq'], 'L0_xattn_Wk': _L0_xattn_in['Wk'], 'L0_xattn_bk': _L0_xattn_in['bk'], 'L0_xattn_Wv': _L0_xattn_in['Wv'], 'L0_xattn_bv': _L0_xattn_in['bv'], 'L0_xattn_Wo': _L0_xattn_in['Wo'], 'L0_xattn_bo': _L0_xattn_in['bo'], 'L0_ffn_norm_weight': _L0_ffn_in['norm_weight'], 'L0_ffn_router_w': _L0_ffn_in['router_w'], 'L0_ffn_sw1': _L0_ffn_in['sw1'], 'L0_ffn_sb1': _L0_ffn_in['sb1'], 'L0_ffn_sw2': _L0_ffn_in['sw2'], 'L0_ffn_sb2': _L0_ffn_in['sb2'], 'L0_ffn_ew1': _L0_ffn_in['ew1'], 'L0_ffn_eb1': _L0_ffn_in['eb1'], 'L0_ffn_ew2': _L0_ffn_in['ew2'], 'L0_ffn_eb2': _L0_ffn_in['eb2']}

def reference(x, ctx_768, g_xattn, g_ffn, L0_xattn_Wq, L0_xattn_bq, L0_xattn_Wk, L0_xattn_bk, L0_xattn_Wv, L0_xattn_bv, L0_xattn_Wo, L0_xattn_bo, L0_ffn_norm_weight, L0_ffn_router_w, L0_ffn_sw1, L0_ffn_sb1, L0_ffn_sw2, L0_ffn_sb2, L0_ffn_ew1, L0_ffn_eb1, L0_ffn_ew2, L0_ffn_eb2):
    import jax
    import jax.numpy as jnp

    def _L0_xattn_ref(query, key_value, Wq, bq, Wk, bk, Wv, bv, Wo, bo):
        import jax, jax.numpy as jnp
        import numpy as np
        NUM_HEADS = 16
        CLAMP = 10000.0
        B, Nq, Cq = query.shape
        Nkv = key_value.shape[1]
        H = NUM_HEADS
        D = Cq // H
        scale = D ** (-0.5)
        q = (query @ Wq + bq).reshape(B, Nq, H, D).transpose(0, 2, 1, 3)
        k = (key_value @ Wk + bk).reshape(B, Nkv, H, D).transpose(0, 2, 1, 3)
        v = (key_value @ Wv + bv).reshape(B, Nkv, H, D).transpose(0, 2, 1, 3)
        attn = jnp.einsum('bhqd,bhkd->bhqk', q, k) * scale
        attn = jnp.clip(attn, -CLAMP, CLAMP)
        attn = jax.nn.softmax(attn, axis=-1)
        attn = jnp.where(jnp.any(jnp.isnan(attn)), jnp.asarray(1.0 / Nkv, attn.dtype), attn)
        x = jnp.einsum('bhqk,bhkd->bqhd', attn, v).reshape(B, Nq, Cq)
        return x @ Wo + bo

    def _L0_ffn_ref(hidden_states, norm_weight, router_w, sw1, sb1, sw2, sb2, ew1, eb1, ew2, eb2):
        import jax, jax.numpy as jnp
        import numpy as np
        D, H, O, E, TOPK = (256, 1024, 256, 8, 2)
        B, S = (4, 256)
        b, s, d = hidden_states.shape
        var = jnp.mean(jnp.square(hidden_states), axis=-1, keepdims=True)
        normed = hidden_states * jax.lax.rsqrt(var + 1e-08) * norm_weight
        shared = jnp.maximum(normed @ sw1 + sb1, 0.0) @ sw2 + sb2
        flat = normed.reshape(-1, d)
        T = flat.shape[0]
        probs = jax.nn.sigmoid(flat @ router_w.T)
        scores, idx = jax.lax.top_k(probs, TOPK)
        w = scores / (jnp.sum(scores, axis=-1, keepdims=True) + 1e-06)
        comb = jnp.zeros((T, E), dtype=flat.dtype)
        comb = comb.at[jnp.arange(T)[:, None], idx].add(w)
        h = jnp.maximum(jnp.einsum('td,edh->teh', flat, ew1) + eb1[None, :, :], 0.0)
        eo = jnp.einsum('teh,eho->teo', h, ew2) + eb2[None, :, :]
        routed = jnp.einsum('teo,te->to', eo, comb)
        return shared + routed.reshape(b, s, -1)
    x = x + jnp.tanh(g_xattn[0]) * _L0_xattn_ref(_layernorm(x, axis=-1), ctx_768, L0_xattn_Wq, L0_xattn_bq, L0_xattn_Wk, L0_xattn_bk, L0_xattn_Wv, L0_xattn_bv, L0_xattn_Wo, L0_xattn_bo)
    x = x + jnp.tanh(g_ffn[0]) * _L0_ffn_ref(_layernorm(x, axis=-1), L0_ffn_norm_weight, L0_ffn_router_w, L0_ffn_sw1, L0_ffn_sb1, L0_ffn_sw2, L0_ffn_sb2, L0_ffn_ew1, L0_ffn_eb1, L0_ffn_ew2, L0_ffn_eb2)
    return x

_drawn_inputs = setup_inputs


def setup_inputs(seed=0):
    import zlib

    import numpy as np

    out = dict(_drawn_inputs(seed))
    spreads = {'L0_xattn_bq': (0.0, 0.1),
     'L0_xattn_bk': (0.0, 0.1),
     'L0_xattn_bv': (0.0, 0.1),
     'L0_xattn_bo': (0.0, 0.1),
     'L0_ffn_norm_weight': (1.0, 0.2),
     'L0_ffn_sb1': (0.0, 0.1),
     'L0_ffn_sb2': (0.0, 0.1),
     'L0_ffn_eb1': (0.0, 0.1),
     'L0_ffn_eb2': (0.0, 0.1)}
    factors = {}
    for name, (base, spread) in spreads.items():
        noise = np.random.default_rng([zlib.crc32(name.encode()), seed]).standard_normal(out[name].shape)
        drawn = base * np.exp(spread * noise) if base else spread * noise
        out[name] = jnp.asarray(drawn.astype(out[name].dtype))
    for name, factor in factors.items():
        out[name] = (out[name] * factor).astype(out[name].dtype)
    return out
```

```python
from contextlib import ExitStack

import concourse.bass as bass
from concourse import mybir

ALU = mybir.AluOpType
ACT = mybir.ActivationFunctionType
AX = mybir.AxisListType
F32 = mybir.dt.float32
F32R = mybir.dt.float32r
I32 = mybir.dt.int32
U32 = mybir.dt.uint32

P = 128
LN_EPS, RMS_EPS, TOP_EPS = 1e-5, 1e-8, 1e-6
Z_LOW, Z_HIGH = -88.7, 16.635533
CLAMP = 10000.0
LOGIT_SAFE, V_SAFE = 40.0, 1e24


def flamingo_block(nc, x, ctx_kv, g_xattn, g_ffn, wq, bq, wk, bk, wv, bv, wo, bo,
                   norm_w, router_w, sw1, sb1, sw2, sb2, ew1, eb1, ew2, eb2, out):
    B, NQ, D = x.shape
    _, NK, CK = ctx_kv.shape
    E, _, H = ew1.shape
    HEADS, DH = 16, 16
    SCALE = float(DH) ** -0.5
    QT = NQ // P
    T = B * QT
    KT = NK // P
    KD = D // P
    CH = CK // 2
    HM = H // P
    GROUPS = HEADS // 4
    CHUNK = 2 * P
    SHARED = B * NQ // CHUNK
    SLOTS = (2 * B * NQ - E) // CHUNK + E
    CHUNKS = SHARED + SLOTS

    PASSES = ((0, 0), (0, 1), (1, 0))

    x_t = x.rearrange("b (t p) d -> b p t d", p=P)
    ctx_t = ctx_kv.rearrange("b (t p) c -> b p t c", p=P)
    out_t = out.rearrange("b (t p) d -> (b t) p d", p=P)

    k_rows = nc.dram_tensor("k_rows", (B, 2, D, NK), F32).ap()
    q_rows = nc.dram_tensor("q_rows", (B, 2, D, NQ), F32).ap()
    slot_x = nc.dram_tensor("slot_x", (SLOTS * CHUNK, D), F32).ap()
    slot_y = nc.dram_tensor("slot_y", (SLOTS * CHUNK, D), F32).ap()
    maxima = nc.dram_tensor("maxima", (B, HEADS // 2, P, 2 * NQ), F32).ap()
    b1_cols = nc.dram_tensor("b1_cols", (E + 1, P, HM), F32).ap()

    with ExitStack() as top:
        def sem(name):
            return top.enter_context(nc.semaphore(name))

        def sb(name, shape, dt=F32, scope=top):
            return scope.enter_context(nc.sbuf_tensor(name, shape, dt))

        x_sb = sb("x_sb", [P, T, D])
        normed = sb("normed", [P, T, D])
        ident = sb("ident", [P, P])
        before = sb("before", [P, P])
        ones = sb("ones", [P, P])
        bo_bc = sb("bo_bc", [P, D])
        nw_bc = sb("nw_bc", [P, D])
        tanh_g = sb("tanh_g", [P, 2])
        g_bc = sb("g_bc", [P, 2])
        logits = sb("logits", [P, T, E])
        rw_t = sb("rw_t", [P, KD, E])
        iota_e = sb("iota_e", [P, E])
        iota_s = sb("iota_s", [P, SLOTS])
        stat6 = sb("stat6", [P, QT, 6])
        mv = sb("mv", [P, 2, QT, 2])
        rs = sb("rs", [P, 3, QT])
        ra = sb("ra", [P, QT])
        rt = sb("rt", [P, QT])
        ssq = sb("ssq", [P, QT])
        half_neg = sb("half_neg", [P, QT])
        flag = sb("flag", [1, 1], I32)

        one = ExitStack()
        k_stack = sb("k_stack", [P, HEADS // 2, NK], F32R, one)
        q_stack = sb("q_stack", [P, HEADS // 2, NQ], F32R, one)
        v_sb = [sb(f"v{n}", [P, KT, HEADS, DH + 1], F32, one) for n in range(B)]
        wo_p = [sb(f"wo_p{i}", [P, KD, D], F32R, one) for i in range(2)]

        qkv = ExitStack()
        w_raw = sb("w_raw", [P, 4, 512], F32, qkv)
        ctx_raw = [sb(f"ctx_raw{i}", [P, KT, CK], F32, qkv) for i in range(2)]
        ctx_p = [sb(f"ctx_p{i}", [CH, 2, NK], F32R, qkv) for i in range(2)]
        xn_p = [sb(f"xn_p{i}", [P, KD, NQ], F32R, qkv) for i in range(2)]
        stage_f = [sb(f"stage_f{i}", [P, 512], F32, qkv) for i in range(2)]
        stage_s = [sb(f"stage_s{i}", [P, 512], F32R, qkv) for i in range(2)]
        stage_p = [[sb(f"stage_p{i}{j}", [P, 512], F32R, qkv) for j in range(2)] for i in range(2)]
        wq_p = [sb(f"wq_p{i}", [P, KD, D], F32R, qkv) for i in range(2)]
        wk_p = [sb(f"wk_p{i}", [CH, 2, D], F32R, qkv) for i in range(2)]
        wv_p = [sb(f"wv_p{i}", [CH, 2, D], F32R, qkv) for i in range(2)]
        bv_bc = sb("bv_bc", [P, D], F32, qkv)
        qk_col = sb("qk_col", [P, 2 * KD], F32, qkv)
        bq_col, bk_col = qk_col[:, 0:KD], qk_col[:, KD:2 * KD]
        bias_rows = sb("bias_rows", [P, P], F32, qkv)
        b1_all = sb("b1_all", [P, E + 1, HM], F32, qkv)
        rw_rows = sb("rw_rows", [E, D], F32, qkv)
        head_f = sb("head_f", [P, P], F32, qkv)
        head_of = sb("head_of", [P, P], F32R, qkv)
        junk = sb("junk", [P, 512], F32, qkv)
        v_ss = sb("v_ss", [P, B, KT // 2], F32, qkv)
        norm2 = sb("norm2", [8, B, 6], I32, qkv)
        k_max = sb("k_max", [8, B, KD], F32, qkv)
        qk_max = sb("qk_max", [8, B, KD], F32, qkv)
        checks = sb("checks", [P, 2], F32, qkv)
        v_ok = sb("v_ok", [P, B, KT // 2], F32, qkv)
        zero = normed[:, T - 2:T, :]
        qkv.close()

        prob = [[sb(f"prob{k}{i}", [P, 2, NQ], F32, one) for i in range(2)] for k in range(2)]
        o_t = sb("o_t", [P, GROUPS, NQ], F32, one)
        on = [sb(f"on{i}", [P, HEADS, DH], F32, one) for i in range(2)]
        on_p = [[sb(f"on_p{i}{j}", [P, KD, P], F32R, one) for j in range(2)] for i in range(2)]
        r_sum = sb("r_sum", [P, HEADS], F32, one)
        n_t = sb("n_t", [P, 2, KD, P], F32, one)
        stage_t = sb("stage_t", [P, D], F32, one)
        clip = [sb(f"clip{i}", [P, 2, NQ], F32, one) for i in range(2)]
        high = [sb(f"high{i}", [P, 2, NQ], F32, one) for i in range(2)]
        is_num = sb("is_num", [P, 2, NQ], F32, one)
        keep = sb("keep", [P, 2], F32, one)
        one.close()

        two = ExitStack()
        w1_raw = [sb(f"w1_raw{i}", [P, KD, H], F32, two) for i in range(2)]
        w2_raw = [sb(f"w2_raw{i}", [P, HM, D], F32, two) for i in range(2)]
        w1_p = [[sb(f"w1_p{i}{j}", [P, KD, H], F32R, two) for j in range(2)] for i in range(2)]
        w2_p = [[sb(f"w2_p{i}{j}", [P, HM, D], F32R, two) for j in range(2)] for i in range(2)]
        b1_sb = [sb(f"b1_sb{i}", [P, HM], F32, two) for i in range(3)]
        b2_sb = [sb(f"b2_sb{i}", [P, D], F32, two) for i in range(3)]
        x_in = [sb(f"x_in{i}", [P, 2, D], F32, two) for i in range(2)]
        xt_p = [[sb(f"xt_p{i}{j}", [P, KD, CHUNK], F32R, two) for j in range(2)] for i in range(2)]
        h_f = [sb(f"h_f{i}", [P, 2, CHUNK], F32, two) for i in range(2)]
        h_p = [[sb(f"h_p{i}{j}", [P, HM, CHUNK], F32R, two) for j in range(2)] for i in range(2)]
        y_sb = [sb(f"y_sb{i}", [P, 2, D], F32, two) for i in range(2)]
        z_c = sb("z_c", [P, T, E], F32, two)
        z_top = sb("z_top", [P, T, 8], F32, two)
        e_top = sb("e_top", [P, T, 8], U32, two)
        e_f = sb("e_f", [P, T, 2], F32, two)
        s_top = sb("s_top", [P, T, 2], F32, two)
        s_sum = sb("s_sum", [P, T], F32, two)
        w_top = sb("w_top", [P, T, 2], F32, two)
        mask = [sb(f"mask{i}", [P, T, E], F32, two) for i in range(2)]
        mask_s = sb("mask_s", [P, T, E], F32, two)
        upto = sb("upto", [P, T + 1, E], F32, two)
        pos = sb("pos", [P, T, E], F32, two)
        pick = sb("pick", [P, T, E], F32, two)
        dest_f = sb("dest_f", [P, 2, T], F32, two)
        dest = sb("dest", [P, 2, T], U32, two)
        n_i = sb("n_i", [P, E], I32, two)
        n_s = sb("n_s", [P, E], I32, two)
        n_slots = sb("n_slots", [P, E], F32, two)
        first = sb("first", [P, E + 1], F32, two)
        first_row = sb("first_row", [P, E], F32, two)
        slot_ef = sb("slot_ef", [P, SLOTS], F32, two)
        slot_e = sb("slot_e", [P, SLOTS], I32, two)
        y_in = [[sb(f"y_in{i}{j}", [P, D], F32, two) for j in range(2)] for i in range(4)]
        two.close()

        sc = [top.enter_context(nc.psum_tensor(f"sc{i}", [P, 2, 512], F32)) for i in range(2)]
        pv = [top.enter_context(nc.psum_tensor(f"pv{i}", [P, 512], F32)) for i in range(2)]
        mb = [top.enter_context(nc.psum_tensor(f"mb{i}", [P, 512], F32)) for i in range(2)]

        loaded_x = [sem(f"loaded_x{n}") for n in range(B)]
        loaded_w = sem("loaded_w")
        loaded_small = sem("loaded_small")
        loaded_ctx = [sem(f"loaded_ctx{i}") for i in range(2)]
        consts_set = sem("consts_set")
        zeros_out = sem("zeros_out")
        w_split = sem("w_split")
        tanh_done = sem("tanh_done")
        dve_step = sem("dve_step")
        pool_step = sem("pool_step")
        stats_done = sem("stats_done")
        rstd_done = sem("rstd_done")
        xn_done = sem("xn_done")
        normed_done = sem("normed_done")
        fill_done = sem("fill_done")
        act_read = sem("act_read")
        dve_read = sem("dve_read")
        low_done = sem("low_done")
        checks_done = sem("checks_done")
        checks_sum = sem("checks_sum")
        flag_done = sem("flag_done")
        post_done = sem("post_done")
        post_read = sem("post_read")
        slow_stack = sem("slow_stack")
        slow_scores = sem("slow_scores")
        slow_step = sem("slow_step")
        slow_high = sem("slow_high")
        slow_max = sem("slow_max")
        slow_max_out = sem("slow_max_out")
        slow_max_in = [sem(f"slow_max_in{i}") for i in range(2)]
        slow_num = sem("slow_num")
        slow_keep = sem("slow_keep")
        slow_logits = sem("slow_logits")
        stage_out = [sem(f"stage_out{i}") for i in range(2)]
        stack_in = [sem(f"stack_in{g}") for g in range(GROUPS)]
        scores_done = sem("scores_done")
        exp_done = sem("exp_done")
        pv_done = sem("pv_done")
        pv_read = sem("pv_read")
        b1_read = sem("b1_read")
        b1_out = sem("b1_out")
        masks_done = sem("masks_done")
        ztop_done = sem("ztop_done")
        exp_z = sem("exp_z")
        rank_done = sem("rank_done")
        rank_read = sem("rank_read")
        dest_done = sem("dest_done")
        scattered = sem("scattered")
        raw1_in = [sem(f"raw1_in{i}") for i in range(2)]
        raw2_in = [sem(f"raw2_in{i}") for i in range(2)]
        biases_in = [sem(f"biases_in{i}") for i in range(3)]
        w1_hi = sem("w1_hi")
        w1_lo = sem("w1_lo")
        w2_hi = sem("w2_hi")
        w2_lo = sem("w2_lo")
        x_in_done = [sem(f"x_in_done{i}") for i in range(2)]
        xt_done = sem("xt_done")
        xt_read = sem("xt_read")
        h_done = sem("h_done")
        relu_done = sem("relu_done")
        h_split = sem("h_split")
        y_done = sem("y_done")
        y_read = sem("y_read")
        y_out = [sem(f"y_out{i}") for i in range(2)]
        gathered = [sem(f"gathered{i}") for i in range(4)]
        combined = sem("combined")
        stored = sem("stored")

        TX, TC, Q, K, V, N = range(6)
        PREP = ([(TX, i) for i in range(KD)] + [(TC, i) for i in range(4)] + [(Q, i) for i in range(KD)]
                + [(K, i) for i in range(2 * KD)] + [(V, 0), (V, 1)] + [(N, i) for i in range(3 * KD)]
                + [(V, i) for i in range(2, KT // 2)])
        STAGES = 3 * KD
        FILLS = len(PREP)
        BY_ACT, BY_DVE = (TX, TC, Q, K, V), (TX, TC, V, N)

        def count_of(n, i, kinds):
            return (n * sum(k in kinds for k, _ in PREP) + sum(k in kinds for k, _ in PREP[:i + 1]))

        def prep_bank(n, i):
            f = (n * FILLS + i) % 8
            return sc[f // 2][:, f % 2, :] if f < 4 else pv[f - 4][:, :] if f < 6 else mb[f - 6][:, :]

        T1, T2, T3, T4, T5 = range(5)
        POST = ((T1, 0), (T1, 1), (T2, 0), (T1, 2), (T2, 1), (T3, 0), (T1, 3), (T2, 2),
                (T3, 1), (T2, 3), (T3, 2), (T3, 3), (T4, 0), (T5, 0), (T4, 1), (T5, 1))
        EARLY = 12
        LATE_AT = 24
        WS = GROUPS * KT

        def post_slot(b, s):
            if b == 0 or EARLY <= s < LATE_AT or s >= LATE_AT + len(POST) - EARLY:
                return None
            return s if s < EARLY else EARLY + s - LATE_AT

        def after(n, kind, t):
            return n * len(POST) + POST.index((kind, t)) + 1

        def norm_fill(s):
            return s // STAGES * FILLS + PREP.index((N, s % STAGES)) + 1

        CHECKS = 8 * B * KD + P * B * KT // 2

        def hps(f):
            return sc[f % 4 // 2][:, f % 2, :].rearrange("p (r n) -> p r n", r=2)

        block = top.enter_context(nc.Block())

        @block.sync
        def _(sp):
            sp.dma_start(x_sb[:, 0:QT, :], x_t[0]).then_inc(loaded_x[0], 16)
            sp.dma_start(w_raw[:, 0, :].rearrange("p (k n) -> p k n", k=KD),
                         wq.rearrange("(k p) n -> p k n", p=P)).then_inc(loaded_w, 16)
            sp.dma_start(w_raw[0:CH, 1, :].rearrange("p (k n) -> p k n", k=2),
                         wk.rearrange("(k p) n -> p k n", p=CH)).then_inc(loaded_w, 16)
            sp.dma_start(w_raw[0:CH, 2, :].rearrange("p (k n) -> p k n", k=2),
                         wv.rearrange("(k p) n -> p k n", p=CH)).then_inc(loaded_w, 16)
            sp.dma_start(w_raw[:, 3, :].rearrange("p (k n) -> p k n", k=KD),
                         wo.rearrange("(k p) n -> p k n", p=P)).then_inc(loaded_w, 16)
            for n in range(1, B):
                sp.dma_start(x_sb[:, n * QT:(n + 1) * QT, :], x_t[n]).then_inc(loaded_x[n], 16)

            def write_rows(n):
                for i in range(STAGES):
                    s = n * STAGES + i
                    sp.wait_ge(low_done, s + 1)
                    for part in range(2):
                        if i < KD:
                            dst = q_rows[n, part, i * P:(i + 1) * P, :]
                        else:
                            m, half = (i - KD) // 2, (i - KD) % 2
                            dst = k_rows[n, part, m * P:(m + 1) * P, half * 512:(half + 1) * 512]
                        sp.dma_start(dst, stage_p[s % 2][part][:, :].bitcast(F32)).then_inc(stage_out[s % 2], 16)

            def load_stacks(n, g, done):
                for a in range(2):
                    for blk in range(4):
                        at = 64 * a + 16 * blk
                        for rows, stack, part in ((k_rows, k_stack, blk // 2), (q_rows, q_stack, blk % 2)):
                            src = rows[n, part].rearrange("(pair a d) n -> a d pair n", a=2, d=DH)
                            sp.dma_start(stack[at:at + DH, 2 * g:2 * g + 2, :].bitcast(F32),
                                         src[a, :, 2 * g:2 * g + 2, :]).then_inc(done, 16)

            def next_stacks(n, g):
                sp.wait_ge(scores_done, 2 * KT * ((n - 1) * GROUPS + g + 1))
                load_stacks(n, g, stack_in[g])

            write_rows(0)
            sp.wait_ge(stage_out[0], 16 * STAGES)
            sp.wait_ge(stage_out[1], 16 * STAGES)
            for g in range(GROUPS):
                load_stacks(0, g, stack_in[g])
            for n in range(1, B):
                write_rows(n)
            sp.wait_ge(stage_out[0], 16 * STAGES * B)
            sp.wait_ge(stage_out[1], 16 * STAGES * B)
            sp.wait_ge(flag_done, 1)
            held = sp.value_load(flag[0:1, 0:1], min_val=0, max_val=CHECKS)
            with sp.If(held < CHECKS):
                pair = 0
                for n in range(B):
                    for g in range(GROUPS):
                        if n >= 1:
                            sp.wait_ge(slow_scores, 2 * KT * ((n - 1) * GROUPS + g + 1))
                            load_stacks(n, g, slow_stack)
                        for i in range(2):
                            pair += 1
                            sp.wait_ge(slow_max, pair)
                            sp.dma_start(maxima[n, 2 * g + i], high[i][:, :, :].rearrange("p a n -> p (a n)")
                                         ).then_inc(slow_max_out, 16)
                            sp.wait_ge(slow_max_out, 16 * pair)
                for g in range(GROUPS):
                    load_stacks(0, g, slow_stack)
                for n in range(B):
                    for g in range(GROUPS):
                        for i in range(2):
                            if n or g:
                                sp.wait_ge(slow_logits, 2 * KT * (n * GROUPS + g))
                            sp.dma_start(high[i][:, :, :].rearrange("p a n -> p (a n)"),
                                         maxima[n, 2 * g + i]).then_inc(slow_max_in[i], 16)
                        if n + 1 < B:
                            next_stacks(n + 1, g)
            with sp.Else():
                for n in range(1, B):
                    for g in range(GROUPS):
                        next_stacks(n, g)

            sp.wait_ge(post_read, B * len(POST))
            sp.wait_ge(b1_out, 16)

            def load_weights(s):
                if s == 0:
                    m1, m2, c1, c2 = sw1, sw2, b1_cols[0], sb2.rearrange("(a n) -> a n", a=1)
                else:
                    e = sp.value_load(slot_e[0:1, s - 1:s], min_val=0, max_val=E - 1)
                    m1 = ew1[bass.ds(e, 1)].rearrange("e d h -> (e d) h")
                    m2 = ew2[bass.ds(e, 1)].rearrange("e h d -> (e h) d")
                    c1 = b1_cols[1:E + 1][bass.ds(e, 1)].rearrange("e p m -> (e p) m")
                    c2 = eb2[bass.ds(e, 1), :]
                i = s % 2
                if s >= 2:
                    sp.wait_ge(w1_hi, s - 1)
                    sp.wait_ge(w1_lo, s - 1)
                sp.dma_start(w1_raw[i][:, :, :], m1.rearrange("(k p) h -> p k h", p=P)).then_inc(raw1_in[i], 16)
                if s >= 3:
                    sp.wait_ge(relu_done, HM // 2 * (SHARED + s - 3))
                    sp.wait_ge(y_read, SHARED + s - 3)
                sp.dma_start(b1_sb[s % 3][:, :], c1).then_inc(biases_in[s % 3], 16)
                sp.dma_start(b2_sb[s % 3][:, :], c2.to_broadcast([P, D])).then_inc(biases_in[s % 3], 16)
                if s >= 2:
                    sp.wait_ge(w2_hi, s - 1)
                    sp.wait_ge(w2_lo, s - 1)
                sp.dma_start(w2_raw[i][:, :, :], m2.rearrange("(k p) d -> p k d", p=P)).then_inc(raw2_in[i], 16)

            def load_slot(j):
                if j >= 2:
                    sp.wait_ge(xt_done, SHARED + j - 1)
                sp.dma_start(x_in[j % 2][:, :, :],
                             slot_x[j * CHUNK:(j + 1) * CHUNK, :].rearrange("(t p) d -> p t d", p=P)
                             ).then_inc(x_in_done[j % 2], 16)

            load_weights(0)
            sp.wait_ge(dest_done, 2)
            load_weights(1)
            sp.wait_ge(scattered, 16 * 2 * T)
            load_slot(0)
            load_slot(1)
            for j in range(SLOTS):
                if j + 2 <= SLOTS:
                    load_weights(j + 2)
                if j + 2 < SLOTS:
                    load_slot(j + 2)
            for t in range(T):
                sp.wait_ge(combined, t + 1)
                sp.dma_start(out_t[t], x_sb[:, t, :]).then_inc(stored, 16)
            sp.wait_ge(stored, 16 * T)

        @block.gpsimd
        def _(pool):
            count = [0]

            def step(ins):
                count[0] += 1
                ins.then_inc(pool_step, 1)
                pool.wait_ge(pool_step, count[0])

            def row(v):
                return v.rearrange("(a n) -> a n", a=1).to_broadcast([P, v.shape[0]])

            for n in range(2):
                pool.dma_start(ctx_raw[n][:, :, :], ctx_t[n]).then_inc(loaded_ctx[n], 16)
            for dst, src in ((bv_bc, bv), (bo_bc, bo), (nw_bc, norm_w)):
                pool.dma_start(dst[:, :], row(src)).then_inc(loaded_small, 16)
            pool.dma_start(g_bc[:, 0:1], row(g_xattn)).then_inc(loaded_small, 16)
            pool.dma_start(g_bc[:, 1:2], row(g_ffn)).then_inc(loaded_small, 16)
            nb = HM * (E + 1)
            pool.dma_start(bias_rows[nb:nb + KD, :], bq.rearrange("(k p) -> k p", p=P)).then_inc(loaded_small, 16)
            pool.dma_start(bias_rows[nb + KD:nb + 2 * KD, :],
                           bk.rearrange("(k p) -> k p", p=P)).then_inc(loaded_small, 16)
            pool.dma_start(bias_rows[0:HM, :], sb1.rearrange("(m p) -> m p", p=P)).then_inc(loaded_small, 16)
            pool.dma_start(bias_rows[HM:HM * (E + 1), :],
                           eb1.rearrange("e (m p) -> (e m) p", p=P)).then_inc(loaded_small, 16)
            pool.dma_start(rw_rows[:, :], router_w).then_inc(loaded_small, 16)

            step(nc.gpsimd.memset(ident[:, :], 0.0))
            step(nc.gpsimd.affine_select(out=ident[:, :], in_=ident[:, :], compare_op=ALU.not_equal,
                                         fill=1.0, base=0, pattern=[[-1, P]], channel_multiplier=1))
            step(nc.gpsimd.memset(before[:, :], 1.0))
            step(nc.gpsimd.affine_select(out=before[:, :], in_=before[:, :], compare_op=ALU.is_gt,
                                         fill=0.0, base=0, pattern=[[1, P]], channel_multiplier=-1))
            step(nc.gpsimd.memset(ones[:, :], 1.0))
            step(nc.gpsimd.memset(zero[:, :, :], 0.0))
            step(nc.gpsimd.memset(half_neg[:, :], -0.5))
            step(nc.gpsimd.iota(iota_e[:, :], pattern=[[1, E]], base=0, channel_multiplier=0,
                                allow_small_or_imprecise_dtypes=True))
            step(nc.gpsimd.iota(iota_s[:, :], pattern=[[1, SLOTS]], base=0, channel_multiplier=0,
                                allow_small_or_imprecise_dtypes=True))
            step(nc.gpsimd.memset(head_f[:, :], 1.0))
            step(nc.gpsimd.affine_select(out=head_f[:, :], in_=head_f[:, :], compare_op=ALU.is_ge,
                                         fill=0.0, base=0, pattern=[[-DH, P]], channel_multiplier=1))
            step(nc.gpsimd.affine_select(out=head_f[:, :], in_=head_f[:, :], compare_op=ALU.is_ge,
                                         fill=0.0, base=DH - 1, pattern=[[DH, P]], channel_multiplier=-1))
            step(nc.gpsimd.tensor_copy(head_of[:, :], head_f[:, :]))
            for v in v_sb:
                step(nc.gpsimd.memset(v[:, :, :, DH:DH + 1], 1.0))
            pool.nop().then_inc(consts_set, 1)
            for j in range(SLOTS):
                pool.dma_start(slot_x[j * CHUNK:(j + 1) * CHUNK, :].rearrange("(t p) d -> p t d", p=P),
                               zero[:, :, :]).then_inc(zeros_out, 16)

            def rsqrt(which, src, scale, eps):
                step(nc.gpsimd.tensor_scalar(ra[:, :], src, scale, eps, ALU.mult, ALU.add))
                step(nc.gpsimd.tensor_tensor(rs[:, which, :], ra[:, :], half_neg[:, :], ALU.pow))
                step(nc.gpsimd.tensor_tensor(rt[:, :], rs[:, which, :], rs[:, which, :], ALU.mult))
                step(nc.gpsimd.tensor_tensor(rt[:, :], rt[:, :], ra[:, :], ALU.mult))
                step(nc.gpsimd.tensor_scalar(rt[:, :], rt[:, :], -0.5, 1.5, ALU.mult, ALU.add))
                nc.gpsimd.tensor_tensor(rs[:, which, :], rs[:, which, :], rt[:, :],
                                        ALU.mult).then_inc(rstd_done, 1)
                pool.wait_ge(rstd_done, rstd_at(which))

            rstds = [0]

            def rstd_at(_):
                rstds[0] += 1
                return rstds[0]

            def norm_x(n):
                pool.wait_ge(stats_done, rstds[0] + 1)
                rsqrt(0, mv[:, 0, :, 1], 1.0, LN_EPS)

            def norm_mlp(n):
                pool.wait_ge(stats_done, rstds[0] + 1)
                rsqrt(1, mv[:, 1, :, 1], 1.0, LN_EPS)
                pool.wait_ge(stats_done, rstds[0] + 1)
                rsqrt(2, ssq[:, :], 1.0 / D, RMS_EPS)

            def stage_low(n, i):
                s = n * STAGES + i
                pool.wait_ge(act_read, count_of(n, PREP.index((Q, 0)) + i, BY_ACT))
                if s >= 2:
                    pool.wait_ge(fill_done, norm_fill(s - 2))
                step(nc.gpsimd.tensor_tensor(stage_s[s % 2][:, :], stage_f[s % 2][:, :], stage_f[s % 2][:, :], ALU.mult))
                nc.gpsimd.tensor_tensor(stage_p[s % 2][1][:, :], stage_f[s % 2][:, :],
                                        stage_p[s % 2][0][:, :].bitcast(F32), ALU.subtract).then_inc(low_done, 1)

            norm_x(0)
            for n in range(B):
                for i in range(STAGES):
                    stage_low(n, i)
                    if i == 1 and n + 1 < B:
                        norm_x(n + 1)
                if n + 2 < B:
                    pool.wait_ge(fill_done, n * FILLS + 6)
                    pool.dma_start(ctx_raw[n % 2][:, :, :], ctx_t[n + 2]).then_inc(loaded_ctx[n % 2], 16)

            pool.wait_ge(flag_done, 1)
            held = pool.value_load(flag[0:1, 0:1], min_val=0, max_val=CHECKS)
            with pool.If(held < CHECKS):
                for pair in range(B * GROUPS * 2):
                    pool.wait_ge(slow_high, pair + 1)
                    both = high[pair % 2][:, :, :].rearrange("p a n -> p (a n)")
                    nc.gpsimd.partition_all_reduce(both, both, P, bass.bass_isa.ReduceOp.max).then_inc(slow_max, 1)
                pool.wait_ge(slow_num, 1)
                nc.gpsimd.partition_all_reduce(keep[:, 1:2], keep[:, 0:1], P,
                                               bass.bass_isa.ReduceOp.max).then_inc(slow_keep, 1)
            with pool.Else():
                pass
            for n in range(B):
                norm_mlp(n)

            def w2_low(s):
                pool.wait_ge(w2_hi, s + 1)
                if s >= 2:
                    pool.wait_ge(y_done, SHARED + s - 2)
                nc.gpsimd.tensor_tensor(w2_p[s % 2][1][:, :, :], w2_raw[s % 2][:, :, :],
                                        w2_p[s % 2][0][:, :, :].bitcast(F32), ALU.subtract).then_inc(w2_lo, 1)

            w2_low(0)
            pool.wait_ge(dest_done, 1)
            pool.wait_ge(zeros_out, 16 * SLOTS)
            for t in range(T):
                for c in range(2):
                    pool.indirect_dma_start(out=slot_x, out_offset=bass.IndirectOffsetOnAxis(ap=dest[:, c, t:t + 1], axis=0),
                                            in_=normed[:, t, :], in_offset=None).then_inc(scattered, 16)
            for s in range(1, SLOTS + 1):
                w2_low(s)
            pool.wait_ge(y_out[0], 16 * ((SLOTS + 1) // 2))
            pool.wait_ge(y_out[1], 16 * (SLOTS // 2))
            for t in range(T):
                if t >= 4:
                    pool.wait_ge(combined, t - 3)
                for c in range(2):
                    pool.indirect_dma_start(out=y_in[t % 4][c][:, :], out_offset=None, in_=slot_y,
                                            in_offset=bass.IndirectOffsetOnAxis(ap=dest[:, c, t:t + 1], axis=0)
                                            ).then_inc(gathered[t % 4], 16)

        @block.scalar
        def _(act):
            act.wait_ge(loaded_small, 16 * 10)
            nc.scalar.activation(tanh_g[:, :], g_bc[:, :], ACT.Tanh).then_inc(tanh_done, 1)
            act.wait_ge(b1_read, 2)
            act.dma_start(b1_cols.rearrange("s p m -> p s m"), b1_all[:, :, :]).then_inc(b1_out, 16)
            act.wait_ge(consts_set, 1)
            for n in range(B):
                for i, (kind, j) in enumerate(PREP):
                    if kind == N:
                        continue
                    act.wait_ge(fill_done, n * FILLS + i + 1)
                    bank = prep_bank(n, i)
                    if kind == TX:
                        last = nc.scalar.activation(xn_p[0][:, j, :], bank, ACT.Copy)
                    elif kind == TC:
                        k, half = j // 2, j % 2
                        last = nc.scalar.activation(ctx_p[0][:, k, half * 512:half * 512 + 512],
                                                    bank[0:CH, :], ACT.Copy)
                    elif kind == V:
                        act.wait_ge(act_read, count_of(n, i, BY_ACT) - 1)
                        last = nc.scalar.activation(junk[:, :], bank, ACT.Square, accum_out=v_ss[:, n, j:j + 1])
                    else:
                        s = n * STAGES + (j if kind == Q else KD + j)
                        if s >= 2:
                            act.wait_ge(stage_out[s % 2], 32 * (s // 2))
                        bias = bq_col[:, j:j + 1] if kind == Q else bk_col[:, j // 2:j // 2 + 1]
                        nc.scalar.activation(stage_f[s % 2][:, :], bank, ACT.Identity, bias=bias)
                        last = nc.scalar.activation(stage_p[s % 2][0][:, :], bank, ACT.Identity, bias=bias)
                    last.then_inc(act_read, 1)

            def exponentials(ready):
                for u in range(2 * B * WS):
                    w = u // 2
                    act.wait_ge(ready, u + 1)
                    if w >= 2:
                        act.wait_ge(pv_done, w - 1)
                    if ready is scores_done:
                        nc.scalar.activation(prob[w % 2][u % 2][:, :, :], sc[u % 2][:, :, :], ACT.Exp,
                                             scale=SCALE).then_inc(exp_done, 1)
                    else:
                        nc.scalar.activation(prob[w % 2][u % 2][:, :, :], clip[u % 2][:, :, :],
                                             ACT.Exp).then_inc(exp_done, 1)

            act.wait_ge(flag_done, 1)
            held = act.value_load(flag[0:1, 0:1], min_val=0, max_val=CHECKS)
            with act.If(held < CHECKS):
                exponentials(slow_logits)
            with act.Else():
                exponentials(scores_done)

            def w1_high(s):
                act.wait_ge(raw1_in[s % 2], 16 * (s // 2 + 1))
                if s >= 2:
                    act.wait_ge(h_done, HM // 2 * (SHARED + s - 2))
                nc.scalar.activation(w1_p[s % 2][0][:, :, :], w1_raw[s % 2][:, :, :], ACT.Copy).then_inc(w1_hi, 1)

            def w2_high(s):
                act.wait_ge(raw2_in[s % 2], 16 * (s // 2 + 1))
                if s >= 2:
                    act.wait_ge(y_done, SHARED + s - 2)
                nc.scalar.activation(w2_p[s % 2][0][:, :, :], w2_raw[s % 2][:, :, :], ACT.Copy).then_inc(w2_hi, 1)

            def store_slot(j):
                act.wait_ge(y_read, SHARED + j + 1)
                act.dma_start(slot_y[j * CHUNK:(j + 1) * CHUNK, :].rearrange("(t p) d -> p t d", p=P),
                              y_sb[j % 2][:, :, :]).then_inc(y_out[j % 2], 16)

            w1_high(0)
            w2_high(0)
            for c in range(CHUNKS):
                s = max(0, c - SHARED + 1)
                act.wait_ge(biases_in[s % 3], 32 * (s // 3 + 1))
                for q in range(HM // 2):
                    f = c * (HM // 2) + q
                    act.wait_ge(h_done, f + 1)
                    if f >= 2:
                        act.wait_ge(h_split, f - 1)
                    for r in range(2):
                        m = 2 * q + r
                        last = nc.scalar.activation(h_f[f % 2][:, r, :], hps(f)[:, r, :], ACT.Relu,
                                                    bias=b1_sb[s % 3][:, m:m + 1])
                    last.then_inc(relu_done, 1)
                    if q == 0 and c - 2 >= SHARED:
                        store_slot(c - 2 - SHARED)
                    if c == 0 and q == 0:
                        act.wait_ge(ztop_done, 1)
                        nc.scalar.activation(s_top[:, :, :], z_top[:, :, 0:2], ACT.Exp,
                                             scale=-1.0).then_inc(exp_z, 1)
                    if q == 1 and c >= SHARED - 1 and s + 1 <= SLOTS:
                        w1_high(s + 1)
                    if q == 2 and c >= SHARED:
                        w2_high(s)
            store_slot(SLOTS - 2)
            store_slot(SLOTS - 1)

        @block.vector
        def _(dve):
            v = nc.vector
            count = [0]

            def step(ins):
                count[0] += 1
                ins.then_inc(dve_step, 1)
                return count[0]

            def settle():
                dve.wait_ge(dve_step, count[0])

            def split(hi, lo, src):
                step(v.tensor_copy(hi, src))
                settle()
                return v.tensor_tensor(lo, src, hi.bitcast(F32), ALU.subtract)

            fill = [0]

            def filled():
                if fill[0]:
                    dve.wait_ge(post_read, fill[0])
                fill[0] += 1
                dve.wait_ge(post_done, fill[0])
                return mb[(fill[0] - 1) % 2]

            def stats(which, tile, t):
                step(v.bn_stats(stat6[:, t, :], x_sb[:, tile, :]))
                settle()
                return v.bn_aggr(mv[:, which, t, :], stat6[:, t, :])

            stat_rounds = [0]

            def ln_x_stats(n):
                dve.wait_ge(loaded_x[n], 16)
                for t in range(QT):
                    last = stats(0, n * QT + t, t)
                    if t < QT - 1:
                        step(last)
                last.then_inc(stats_done, 1)
                stat_rounds[0] += 1

            def ln_x(n):
                dve.wait_ge(rstd_done, stat_rounds[0])
                if n == B - 1:
                    dve.wait_ge(zeros_out, 16 * SLOTS)
                for t in range(QT):
                    last = v.tensor_scalar(normed[:, n * QT + t, :], x_sb[:, n * QT + t, :], mv[:, 0, t, 0:1],
                                           rs[:, 0, t:t + 1], ALU.subtract, ALU.mult)
                    if t < QT - 1:
                        step(last)
                last.then_inc(xn_done, 1)

            def prep(n, i):
                kind, j = PREP[i]
                bank = prep_bank(n, i)
                if kind == TX:
                    dve.wait_ge(act_read, count_of(n, i, BY_ACT))
                    v.tensor_tensor(xn_p[1][:, j, :], bank, xn_p[0][:, j, :].bitcast(F32),
                                    ALU.subtract).then_inc(dve_read, 1)
                elif kind == TC:
                    dve.wait_ge(act_read, count_of(n, i, BY_ACT))
                    k, at = j // 2, slice(j % 2 * 512, j % 2 * 512 + 512)
                    v.tensor_tensor(ctx_p[1][:, k, at], bank[0:CH, :], ctx_p[0][:, k, at].bitcast(F32),
                                    ALU.subtract).then_inc(dve_read, 1)
                elif kind == N:
                    dve.wait_ge(fill_done, n * FILLS + i + 1)
                    v.tensor_reduce(norm2[:, n, j:j + 1], bank[0:8, :].bitcast(I32), AX.X, ALU.max
                                    ).then_inc(dve_read, 1)
                elif kind == V:
                    dve.wait_ge(act_read, count_of(n, i, BY_ACT))
                    for u in range(2):
                        last = v.tensor_tensor(
                            v_sb[n][:, 2 * j + u, :, 0:DH],
                            bank[:, u * D:(u + 1) * D].rearrange("p (h d) -> p h d", h=HEADS),
                            bv_bc[:, :].rearrange("p (h d) -> p h d", h=HEADS), ALU.add)
                        if u == 0:
                            step(last)
                    last.then_inc(dve_read, 1)

            def check():
                dve.wait_ge(dve_read, count_of(B - 1, FILLS - 1, BY_DVE))
                m2 = norm2[:, :, :].bitcast(F32)
                k4 = m2[:, :, KD:].rearrange("p n (m h) -> p n m h", h=2)
                step(v.tensor_tensor(k_max[:, :, :].bitcast(I32), norm2[:, :, KD:].rearrange("p n (m h) -> p n m h", h=2)[:, :, :, 0],
                                     norm2[:, :, KD:].rearrange("p n (m h) -> p n m h", h=2)[:, :, :, 1], ALU.max))
                step(v.memset(checks[:, :], 0.0))
                settle()
                step(v.tensor_tensor(qk_max[:, :, :], k_max[:, :, :], m2[:, :, 0:KD], ALU.mult))
                settle()
                step(v.tensor_scalar(qk_max[:, :, :], qk_max[:, :, :], (LOGIT_SAFE / SCALE) ** 2, None, ALU.is_le))
                settle()
                step(v.tensor_reduce(checks[0:8, 0:1], qk_max[:, :, :], AX.XY, ALU.add))
                step(v.tensor_scalar(v_ok[:, :, :], v_ss[:, :, :], V_SAFE, None, ALU.is_le))
                settle()
                v.tensor_reduce(checks[:, 1:2], v_ok[:, :, :], AX.XY, ALU.add).then_inc(checks_done, 1)
                dve.wait_ge(checks_sum, 1)
                v.tensor_reduce(checks[0:1, 0:1], mb[0][0:1, 0:2], AX.X, ALU.add).then_inc(checks_done, 1)
                dve.wait_ge(checks_done, 2)
                for bank in pv:
                    step(v.memset(bank[:, :], 0.0))
                dve.wait_ge(stage_out[0], 16 * STAGES * B)
                dve.wait_ge(stage_out[1], 16 * STAGES * B)
                v.tensor_copy(flag[:, :], checks[0:1, 0:1]).then_inc(flag_done, 1)

            def post(n, i):
                kind, t = POST[i]
                bank = filled()
                tile = n * QT + t
                if kind == T1:
                    o4 = bank[:, :].rearrange("p (h c) -> p h c", h=HEADS)
                    step(v.reciprocal(r_sum[:, :], o4[:, :, DH]))
                    settle()
                    v.tensor_tensor(on[t % 2][:, :, :], o4[:, :, 0:DH],
                                    r_sum[:, :].unsqueeze(2).to_broadcast([P, HEADS, DH]),
                                    ALU.mult).then_inc(post_read, 1)
                elif kind == T2:
                    src = bank[:, 0:KD * P].rearrange("p (k n) -> p k n", k=KD)
                    split(on_p[t % 2][0][:, :, :], on_p[t % 2][1][:, :, :], src).then_inc(post_read, 1)
                elif kind == T3:
                    step(v.tensor_tensor(stage_t[:, :], bank[:, 0:D], bo_bc[:, :], ALU.add))
                    settle()
                    v.scalar_tensor_tensor(x_sb[:, tile, :], stage_t[:, :], tanh_g[:, 0:1],
                                           x_sb[:, tile, :], ALU.mult, ALU.add).then_inc(post_read, 1)
                    dve.wait_ge(post_read, fill[0])
                    last = stats(1, tile, t)
                    if t < QT - 1:
                        step(last)
                    else:
                        last.then_inc(stats_done, 1)
                        stat_rounds[0] += 1
                elif kind == T4:
                    v.tensor_copy(n_t[:, :, :, :], bank[:, :].rearrange("p (t k n) -> p t k n", t=2, k=KD)
                                  ).then_inc(post_read, 1)
                else:
                    v.tensor_copy(logits[:, n * QT + 2 * t:n * QT + 2 * t + 2, :],
                                  bank[:, 0:2 * E].rearrange("p (t e) -> p t e", t=2)).then_inc(post_read, 1)

            def ln_mlp(n):
                dve.wait_ge(rstd_done, stat_rounds[0])
                for t in range(QT):
                    step(v.tensor_scalar(normed[:, n * QT + t, :], x_sb[:, n * QT + t, :], mv[:, 1, t, 0:1],
                                         rs[:, 1, t:t + 1], ALU.subtract, ALU.mult))
                for t in range(QT):
                    settle()
                    last = v.tensor_tensor_reduce(stage_t[:, :], normed[:, n * QT + t, :], normed[:, n * QT + t, :],
                                                  1.0, 0.0, ALU.mult, ALU.add, ssq[:, t:t + 1])
                    if t < QT - 1:
                        step(last)
                last.then_inc(stats_done, 1)
                stat_rounds[0] += 1

            def rms_mlp(n):
                dve.wait_ge(rstd_done, stat_rounds[0])
                for t in range(QT):
                    last = v.scalar_tensor_tensor(normed[:, n * QT + t, :], normed[:, n * QT + t, :],
                                                  rs[:, 2, t:t + 1], nw_bc[:, :], ALU.mult, ALU.mult)
                    if t < QT - 1:
                        step(last)
                last.then_inc(normed_done, 1)

            dve.wait_ge(loaded_w, 64)
            for i, (w, rows) in enumerate(((wq_p, P), (wk_p, CH), (wv_p, CH), (wo_p, P))):
                raw = w_raw[0:rows, i, :].rearrange("p (k n) -> p k n", k=2)
                split(w[0][:, :, :], w[1][:, :, :], raw).then_inc(w_split, 1)
            ln_x_stats(0)
            ln_x(0)
            dve.wait_ge(loaded_small, 160)
            dve.wait_ge(consts_set, 1)

            dve.wait_ge(b1_read, 1)
            step(v.tensor_copy(b1_all[:, :, :], pv[0][:, 0:HM * (E + 1)].rearrange("p (s m) -> p s m", s=E + 1)))
            step(v.tensor_copy(qk_col[:, :], pv[0][:, HM * (E + 1):HM * (E + 1) + 2 * KD]))
            v.tensor_copy(rw_t[:, :, :], pv[1][:, 0:KD * E].rearrange("p (k e) -> p k e", k=KD)
                          ).then_inc(b1_read, 1)

            for n in range(B):
                for i, (kind, j) in enumerate(PREP):
                    if n + 1 < B and (kind, j) == (Q, 0):
                        ln_x_stats(n + 1)
                    if n + 1 < B and (kind, j) == (V, 0):
                        ln_x(n + 1)
                    if kind in BY_DVE:
                        prep(n, i)
            check()
            dve.wait_ge(tanh_done, 1)

            def heads_out(b, g):
                at = b * GROUPS + g
                dve.wait_ge(pv_done, (at + 1) * KT)
                v.tensor_copy(o_t[:, g, :], pv[at % 2][:, :]).then_inc(pv_read, 1)

            def fast_attention():
                for b in range(B):
                    for s in range(WS):
                        if (i := post_slot(b, s)) is not None:
                            post(b - 1, i)
                        if b >= 1 and s == 14:
                            ln_mlp(b - 1)
                        if b >= 1 and s == 18:
                            rms_mlp(b - 1)
                        if s % KT == KT - 1:
                            heads_out(b, s // KT)

            def general_attention():
                slow = [0]

                def slowly(ins):
                    slow[0] += 1
                    ins.then_inc(slow_step, 1)
                    dve.wait_ge(slow_step, slow[0])

                slowly(v.memset(is_num[:, :, :], 1.0))
                u = 0
                for pair in range(B * GROUPS * 2):
                    i = pair % 2
                    if pair >= 2:
                        dve.wait_ge(slow_max_out, 16 * (pair - 1))
                    slowly(v.memset(high[i][:, :, :], -CLAMP))
                    for kt in range(KT):
                        u += 1
                        dve.wait_ge(slow_scores, u)
                        slowly(v.tensor_copy(clip[0][:, :, :], sc[i][:, :, :]))
                        slowly(v.tensor_tensor(clip[1][:, :, :], clip[0][:, :, :], clip[0][:, :, :], ALU.is_equal))
                        slowly(v.tensor_tensor(is_num[:, :, :], is_num[:, :, :], clip[1][:, :, :], ALU.min))
                        slowly(v.tensor_scalar(clip[0][:, :, :], clip[0][:, :, :], SCALE, CLAMP, ALU.mult, ALU.min))
                        ins = v.tensor_tensor(high[i][:, :, :], high[i][:, :, :], clip[0][:, :, :], ALU.max)
                        if kt < KT - 1:
                            slowly(ins)
                        else:
                            ins.then_inc(slow_high, 1)
                            dve.wait_ge(slow_high, pair + 1)
                slowly(v.tensor_reduce(keep[:, 1:2], is_num[:, :, :], AX.XY, ALU.min))
                v.tensor_scalar(keep[:, 0:1], keep[:, 1:2], -1.0, 1.0, ALU.mult, ALU.add).then_inc(slow_num, 1)
                dve.wait_ge(slow_keep, 1)
                slowly(v.tensor_scalar(keep[:, 0:1], keep[:, 1:2], -1.0, 1.0, ALU.mult, ALU.add))
                for b in range(B):
                    for s in range(WS):
                        w = b * WS + s
                        for i in range(2):
                            u = 2 * w + i
                            if s % KT == 0:
                                dve.wait_ge(slow_max_in[i], 16 * (b * GROUPS + s // KT + 1))
                                slowly(v.tensor_scalar(high[i][:, :, :], high[i][:, :, :], keep[:, 0:1], None, ALU.mult))
                            dve.wait_ge(scores_done, u + 1)
                            if u >= 2:
                                dve.wait_ge(exp_done, u - 1)
                            slowly(v.tensor_scalar(clip[i][:, :, :], sc[i][:, :, :], SCALE, CLAMP, ALU.mult, ALU.min))
                            slowly(v.tensor_scalar(clip[i][:, :, :], clip[i][:, :, :], -CLAMP, keep[:, 0:1],
                                                   ALU.max, ALU.mult))
                            v.tensor_tensor(clip[i][:, :, :], clip[i][:, :, :], high[i][:, :, :],
                                            ALU.subtract).then_inc(slow_logits, 1)
                        if s % KT == KT - 1:
                            heads_out(b, s // KT)
                    if b < B - 1:
                        for i in range(len(POST)):
                            if i == EARLY:
                                ln_mlp(b)
                                rms_mlp(b)
                            post(b, i)

            dve.wait_ge(flag_done, 1)
            held = dve.value_load(flag[0:1, 0:1], min_val=0, max_val=CHECKS)
            counts = count[0], fill[0], stat_rounds[0]
            with dve.If(held < CHECKS):
                general_attention()
                general = count[0], fill[0], stat_rounds[0]
            with dve.Else():
                count[0], fill[0], stat_rounds[0] = counts
                fast_attention()
                assert general == (count[0], fill[0], stat_rounds[0])
            for i in range(len(POST)):
                if i == EARLY:
                    ln_mlp(B - 1)
                    rms_mlp(B - 1)
                post(B - 1, i)

            dve.wait_ge(post_read, fill[0])

            def top_two():
                step(v.tensor_scalar(z_c[:, :, :], logits[:, :, :], Z_LOW, Z_HIGH, ALU.max, ALU.min))
                settle()
                for t in range(T):
                    last = v.max(z_top[:, t, :], z_c[:, t, :])
                    if t < T - 1:
                        step(last)
                last.then_inc(ztop_done, 1)
                dve.wait_ge(ztop_done, 1)
                for t in range(T):
                    step(v.max_index(e_top[:, t, :], z_top[:, t, :], z_c[:, t, :]))
                settle()
                step(v.tensor_copy(e_f[:, :, :], e_top[:, :, 0:2]))
                settle()
                for c in range(2):
                    step(v.tensor_tensor(mask[c][:, :, :], iota_e[:, :].unsqueeze(1).to_broadcast([P, T, E]),
                                         e_f[:, :, c:c + 1].to_broadcast([P, T, E]), ALU.is_equal))
                settle()
                v.tensor_tensor(mask_s[:, :, :], mask[0][:, :, :], mask[1][:, :, :], ALU.add
                                ).then_inc(masks_done, 1)

            def weights_of_two():
                dve.wait_ge(exp_z, 1)
                step(v.tensor_scalar(s_top[:, :, :], s_top[:, :, :], 1.0, None, ALU.add))
                settle()
                step(v.reciprocal(w_top[:, :, :], s_top[:, :, :]))
                settle()
                step(v.tensor_tensor(s_sum[:, :], w_top[:, :, 0], w_top[:, :, 1], ALU.add))
                settle()
                step(v.tensor_scalar(s_sum[:, :], s_sum[:, :], TOP_EPS, None, ALU.add))
                settle()
                step(v.reciprocal(s_sum[:, :], s_sum[:, :]))
                settle()
                step(v.scalar_tensor_tensor(w_top[:, :, :], w_top[:, :, :], tanh_g[:, 1:2],
                                            s_sum[:, :].unsqueeze(2).to_broadcast([P, T, 2]), ALU.mult, ALU.mult))

            def places():
                dve.wait_ge(rank_done, 1)
                step(v.memset(upto[:, 0, :], 0.0))
                settle()
                for t in range(T):
                    step(v.tensor_tensor(upto[:, t + 1, :], upto[:, t, :], pv[1][:, t * E:(t + 1) * E], ALU.add))
                    settle()
                step(v.tensor_scalar(n_i[:, :], upto[:, T, :], float(CHUNK - 1), None, ALU.add))
                settle()
                step(v.tensor_scalar(n_s[:, :], n_i[:, :], CHUNK.bit_length() - 1, None, ALU.logical_shift_right))
                settle()
                step(v.tensor_copy(n_slots[:, :], n_s[:, :]))
                step(v.memset(first[:, 0:1], 0.0))
                settle()
                for e in range(E):
                    step(v.tensor_tensor(first[:, e + 1:e + 2], first[:, e:e + 1], n_slots[:, e:e + 1], ALU.add))
                    settle()
                step(v.tensor_scalar(first_row[:, :], first[:, 0:E], float(CHUNK), None, ALU.mult))
                step(v.tensor_tensor(pos[:, :, :], pv[0][:, 0:T * E].rearrange("p (t e) -> p t e", t=T),
                                     upto[:, 0:T, :], ALU.add))
                settle()
                step(v.tensor_tensor(pos[:, :, :], pos[:, :, :],
                                     first_row[:, :].unsqueeze(1).to_broadcast([P, T, E]), ALU.add))
                settle()
                for c in range(2):
                    step(v.tensor_tensor(pick[:, :, :], pos[:, :, :], mask[c][:, :, :], ALU.mult))
                    settle()
                    step(v.tensor_reduce(dest_f[:, c, :], pick[:, :, :], AX.X, ALU.add))
                    settle()
                v.tensor_copy(dest[:, :, :], dest_f[:, :, :]).then_inc(dest_done, 1)
                step(v.memset(slot_ef[:, :], 0.0))
                for e in range(1, E):
                    settle()
                    step(v.scalar_tensor_tensor(slot_ef[:, :], iota_s[:, :], first[:, e:e + 1], slot_ef[:, :],
                                                ALU.is_ge, ALU.add))
                settle()
                v.tensor_copy(slot_e[:, :], slot_ef[:, :]).then_inc(dest_done, 1)

            def split_x(c):
                dve.wait_ge(xt_done, c + 1)
                if c >= 2:
                    dve.wait_ge(h_done, (c - 1) * HM // 2)
                src = mb[c % 2][:, :].rearrange("p (k n) -> p k n", k=KD)
                split(xt_p[c % 2][0][:, :, :], xt_p[c % 2][1][:, :, :], src).then_inc(xt_read, 1)

            def split_h(c, q):
                f = c * (HM // 2) + q
                dve.wait_ge(relu_done, f + 1)
                at = slice(2 * q, 2 * q + 2)
                split(h_p[c % 2][0][:, at, :], h_p[c % 2][1][:, at, :], h_f[f % 2][:, :, :]).then_inc(h_split, 1)

            def w1_low(s):
                dve.wait_ge(w1_hi, s + 1)
                v.tensor_tensor(w1_p[s % 2][1][:, :, :], w1_raw[s % 2][:, :, :],
                                w1_p[s % 2][0][:, :, :].bitcast(F32), ALU.subtract).then_inc(w1_lo, 1)

            def read_y(c):
                dve.wait_ge(y_done, c + 1)
                y = pv[c % 2][:, :].rearrange("p (t n) -> p t n", t=2)
                s = max(0, c - SHARED + 1)
                dve.wait_ge(biases_in[s % 3], 32 * (s // 3 + 1))
                if c >= SHARED:
                    j = c - SHARED
                    if j >= 2:
                        dve.wait_ge(y_out[j % 2], 16 * (j // 2))
                    v.tensor_tensor(y_sb[j % 2][:, :, :], y, b2_sb[s % 3][:, :].unsqueeze(1).to_broadcast([P, 2, D]),
                                    ALU.add).then_inc(y_read, 1)
                else:
                    step(v.tensor_tensor(y_sb[c % 2][:, :, :], y, b2_sb[0][:, :].unsqueeze(1).to_broadcast([P, 2, D]),
                                         ALU.add))
                    settle()
                    v.scalar_tensor_tensor(x_sb[:, 2 * c:2 * c + 2, :], y_sb[c % 2][:, :, :], tanh_g[:, 1:2],
                                           x_sb[:, 2 * c:2 * c + 2, :], ALU.mult, ALU.add).then_inc(y_read, 1)
                dve.wait_ge(y_read, c + 1)

            w1_low(0)
            split_x(0)
            top_two()
            for c in range(CHUNKS + 1):
                if c < CHUNKS:
                    s = max(0, c - SHARED + 1)
                    for q in range(HM // 2):
                        split_h(c, q)
                        if q == 0 and c + 1 < CHUNKS:
                            split_x(c + 1)
                        if q == 1 and c >= SHARED - 1 and s + 1 <= SLOTS:
                            w1_low(s + 1)
                        if c == 0 and q == 3:
                            weights_of_two()
                        if c == 1 and q == 0:
                            places()
                if c >= 1:
                    read_y(c - 1)
            for t in range(T):
                dve.wait_ge(gathered[t % 4], 32 * (t // 4 + 1))
                for i in range(2):
                    last = v.scalar_tensor_tensor(x_sb[:, t, :], y_in[t % 4][i][:, :], w_top[:, t, i:i + 1],
                                                  x_sb[:, t, :], ALU.mult, ALU.add)
                    if i == 0:
                        step(last)
                        settle()
                last.then_inc(combined, 1)

        @block.tensor
        def _(pe):
            mm = nc.tensor.matmul

            def product(dst, lhs, rhs, parts=KD):
                todo = [(k, a, b) for k in range(parts) for a, b in PASSES]
                for i, (k, a, b) in enumerate(todo):
                    last = mm(dst, lhs(a, k), rhs(b, k), start=(i == 0), stop=(i == len(todo) - 1))
                return last

            fill = [0]

            def bank():
                fill[0] += 1
                if fill[0] > 2:
                    pe.wait_ge(post_read, fill[0] - 2)
                return mb[(fill[0] - 1) % 2]

            def prep(n, i):
                kind, j = PREP[i]
                dst = prep_bank(n, i)
                f = n * FILLS + i
                if f >= 8:
                    bn, bi = (f - 8) // FILLS, (f - 8) % FILLS
                    if PREP[bi][0] in BY_DVE:
                        pe.wait_ge(dve_read, count_of(bn, bi, BY_DVE))
                    else:
                        pe.wait_ge(act_read, count_of(bn, bi, BY_ACT))
                if kind == TX:
                    pe.wait_ge(xn_done, n + 1)
                    for t in range(QT):
                        last = nc.tensor.transpose(dst[:, t * P:(t + 1) * P],
                                                   normed[:, n * QT + t, j * P:(j + 1) * P], ident[:, :])
                elif kind == TC:
                    k, half = j // 2, j % 2
                    pe.wait_ge(loaded_ctx[n % 2], 16 * (n // 2 + 1))
                    for t in range(4):
                        last = nc.tensor.transpose(dst[0:CH, t * P:(t + 1) * P],
                                                   ctx_raw[n % 2][:, 4 * half + t, k * CH:(k + 1) * CH], ident[:, :])
                elif kind == Q:
                    pe.wait_ge(dve_read, count_of(n, 1, BY_DVE))
                    last = product(dst, lambda a, k: wq_p[a][:, k, j * P:(j + 1) * P], lambda a, k: xn_p[a][:, k, :])
                elif kind == K:
                    m, half = j // 2, j % 2
                    pe.wait_ge(dve_read, count_of(n, 5, BY_DVE))
                    last = product(dst, lambda a, k: wk_p[a][:, k, m * P:(m + 1) * P],
                                   lambda a, k: ctx_p[a][:, k, half * 512:half * 512 + 512])
                elif kind == V:
                    for u in range(2):
                        kt = 2 * j + u
                        last = product(dst[:, u * D:(u + 1) * D],
                                       lambda a, k: ctx_p[a][:, k, kt * P:(kt + 1) * P],
                                       lambda a, k: wv_p[a][:, k, :])
                else:
                    s = n * STAGES + j
                    pe.wait_ge(low_done, s + 1)
                    last = mm(dst, head_of[:, :], stage_s[s % 2][:, :], start=True, stop=True)
                last.then_inc(fill_done, 1)

            def post(n, i):
                kind, t = POST[i]
                dst = bank()
                if kind == T1:
                    pe.wait_ge(pv_read, GROUPS * (n + 1))
                    for g in range(GROUPS):
                        last = nc.tensor.transpose(dst[:, g * P:(g + 1) * P], o_t[:, g, t * P:(t + 1) * P], ident[:, :])
                elif kind == T2:
                    pe.wait_ge(post_read, after(n, T1, t))
                    o = on[t % 2][:, :, :].rearrange("p h d -> p (h d)")
                    for k in range(KD):
                        last = nc.tensor.transpose(dst[:, k * P:(k + 1) * P], o[:, k * P:(k + 1) * P], ident[:, :])
                elif kind == T3:
                    pe.wait_ge(post_read, after(n, T2, t))
                    last = product(dst[:, 0:D], lambda a, k: on_p[t % 2][a][:, k, :], lambda a, k: wo_p[a][:, k, :])
                elif kind == T4:
                    pe.wait_ge(normed_done, n + 1)
                    for u in range(2):
                        for k in range(KD):
                            at = (u * KD + k) * P
                            last = nc.tensor.transpose(dst[:, at:at + P],
                                                       normed[:, n * QT + 2 * t + u, k * P:(k + 1) * P], ident[:, :])
                else:
                    pe.wait_ge(post_read, after(n, T4, t))
                    for u in range(2):
                        for k in range(KD):
                            last = mm(dst[:, u * E:(u + 1) * E], n_t[:, u, k, :], rw_t[:, k, :],
                                      start=(k == 0), stop=(k == KD - 1))
                last.then_inc(post_done, 1)

            def score(i, a, g, kt):
                rows = slice(64 * a, 64 * a + 64)
                return mm(sc[i][:, a, :], k_stack[rows, 2 * g + i, kt * P:(kt + 1) * P],
                          q_stack[rows, 2 * g + i, :], start=True, stop=True)

            def slow_at(b, g, i, kt):
                pair = (b * GROUPS + g) * 2 + i
                return 1 + pair * (1 + 5 * KT - 1) + 1 + 5 * (kt - 1) + 1

            def scores(w):
                b, g, kt = w // WS, w % WS // KT, w % KT
                if kt == 0:
                    pe.wait_ge(stack_in[g], 256 * (b + 1))
                for i in range(2):
                    u = 2 * w + i
                    if u >= 2:
                        pe.wait_ge(exp_done, u - 1)
                    for a in range(2):
                        last = score(i, a, g, kt)
                    last.then_inc(scores_done, 1)

            def values(w):
                b, g, kt = w // WS, w % WS // KT, w % KT
                gg = b * GROUPS + g
                if kt == 0 and gg >= 2:
                    pe.wait_ge(pv_read, gg - 1)
                pe.wait_ge(exp_done, 2 * w + 2)
                for j in range(4):
                    last = mm(pv[gg % 2][32 * j:32 * j + DH + 1, :], v_sb[b][:, kt, 4 * g + j, :],
                              prob[w % 2][j // 2][:, j % 2, :], start=(kt == 0), stop=(kt == KT - 1))
                last.then_inc(pv_done, 1)

            pe.wait_ge(consts_set, 1)
            pe.wait_ge(loaded_small, 160)
            nrows = HM * (E + 1) + 2 * KD
            nc.tensor.transpose(pv[0][:, 0:nrows], bias_rows[0:nrows, :], ident[0:nrows, 0:nrows])
            for k in range(KD):
                last = nc.tensor.transpose(pv[1][:, k * E:(k + 1) * E], rw_rows[:, k * P:(k + 1) * P], ident[0:E, 0:E])
            last.then_inc(b1_read, 1)

            pe.wait_ge(w_split, 4)
            pe.wait_ge(b1_read, 2)
            for n in range(B):
                for i in range(FILLS):
                    prep(n, i)
            pe.wait_ge(checks_done, 1)
            mm(mb[0][0:1, 0:2], ones[:, 0:1], checks[:, :], start=True, stop=True).then_inc(checks_sum, 1)

            def fast_attention():
                scores(0)
                for b in range(B):
                    for s in range(WS):
                        w = b * WS + s
                        if w + 1 < B * WS:
                            scores(w + 1)
                        values(w)
                        if (i := post_slot(b, s)) is not None:
                            post(b - 1, i)

            def general_attention():
                u = 0
                for b in range(B):
                    for g in range(GROUPS):
                        if b:
                            pe.wait_ge(slow_stack, 256 * ((b - 1) * GROUPS + g + 1))
                        else:
                            pe.wait_ge(stack_in[g], 256)
                        for i in range(2):
                            for kt in range(KT):
                                if kt:
                                    pe.wait_ge(slow_step, slow_at(b, g, i, kt))
                                elif i or g or b:
                                    pe.wait_ge(slow_high, (b * GROUPS + g) * 2 + i)
                                for a in range(2):
                                    last = score(i, a, g, kt)
                                last.then_inc(slow_scores, 1)
                pe.wait_ge(slow_stack, 256 * B * GROUPS)
                pe.wait_ge(slow_keep, 1)
                for b in range(B):
                    for s in range(WS):
                        scores(b * WS + s)
                        values(b * WS + s)
                    if b < B - 1:
                        for i in range(len(POST)):
                            post(b, i)

            pe.wait_ge(flag_done, 1)
            held = pe.value_load(flag[0:1, 0:1], min_val=0, max_val=CHECKS)
            fills = fill[0]
            with pe.If(held < CHECKS):
                general_attention()
            with pe.Else():
                fill[0] = fills
                fast_attention()
            for i in range(len(POST)):
                post(B - 1, i)

            pe.wait_ge(post_read, fill[0])

            def turn_x(c):
                if c >= 2:
                    pe.wait_ge(xt_read, c - 1)
                if c >= SHARED:
                    j = c - SHARED
                    pe.wait_ge(x_in_done[j % 2], 16 * (j // 2 + 1))
                for k in range(KD):
                    for t in range(2):
                        src = (normed[:, 2 * c + t, k * P:(k + 1) * P] if c < SHARED
                               else x_in[j % 2][:, t, k * P:(k + 1) * P])
                        at = (2 * k + t) * P
                        last = nc.tensor.transpose(mb[c % 2][:, at:at + P], src, ident[:, :])
                last.then_inc(xt_done, 1)

            def hidden(c):
                s = max(0, c - SHARED + 1)
                pe.wait_ge(xt_read, c + 1)
                pe.wait_ge(w1_lo, s + 1)
                for q in range(HM // 2):
                    f = c * (HM // 2) + q
                    if f >= 4:
                        pe.wait_ge(relu_done, f - 3)
                    for r in range(2):
                        m = 2 * q + r
                        last = product(hps(f)[:, r, :], lambda a, k: w1_p[s % 2][a][:, k, m * P:(m + 1) * P],
                                       lambda a, k: xt_p[c % 2][a][:, k, :])
                    last.then_inc(h_done, 1)

            def results(c):
                s = max(0, c - SHARED + 1)
                pe.wait_ge(w2_lo, s + 1)
                pe.wait_ge(h_split, (c + 1) * HM // 2)
                if c >= 2:
                    pe.wait_ge(y_read, c - 1)
                for t in range(2):
                    last = product(pv[c % 2][:, t * D:(t + 1) * D],
                                   lambda a, k: h_p[c % 2][a][:, k, t * P:(t + 1) * P],
                                   lambda a, k: w2_p[s % 2][a][:, k, :], HM)
                last.then_inc(y_done, 1)

            def ranks():
                pe.wait_ge(masks_done, 1)
                m = mask_s[:, :, :].rearrange("p t e -> p (t e)")
                mm(pv[0][:, 0:T * E], before[:, :], m, start=True, stop=True)
                mm(pv[1][:, 0:T * E], ones[:, :], m, start=True, stop=True).then_inc(rank_done, 1)

            turn_x(0)
            for c in range(CHUNKS + 1):
                if c < CHUNKS:
                    if c + 1 < CHUNKS:
                        turn_x(c + 1)
                    hidden(c)
                    if c == 0:
                        ranks()
                if c == 1:
                    pe.wait_ge(dest_done, 1)
                if c >= 1:
                    results(c - 1)


_INS = ['x', 'ctx_768', 'g_xattn', 'g_ffn', 'L0_xattn_Wq', 'L0_xattn_bq', 'L0_xattn_Wk', 'L0_xattn_bk',
        'L0_xattn_Wv', 'L0_xattn_bv', 'L0_xattn_Wo', 'L0_xattn_bo', 'L0_ffn_norm_weight', 'L0_ffn_router_w',
        'L0_ffn_sw1', 'L0_ffn_sb1', 'L0_ffn_sw2', 'L0_ffn_sb2', 'L0_ffn_ew1', 'L0_ffn_eb1', 'L0_ffn_ew2',
        'L0_ffn_eb2']


def kernel(**inputs):
    import numpy as np
    import concourse.bacc as bacc
    from concourse.bass_utils import run_bass_kernel_spmd

    nc = bacc.Bacc("TRN2", target_bir_lowering=False, num_devices=1)
    arrays, args = {}, []
    for name in _INS:
        a = np.ascontiguousarray(inputs[name])
        arrays[f"in_{name}"] = a
        args.append(nc.dram_tensor(f"in_{name}", a.shape, mybir.dt.from_np(a.dtype), kind="ExternalInput").ap())
    out = nc.dram_tensor("out", inputs["x"].shape, F32, kind="ExternalOutput").ap()
    flamingo_block(nc, *args, out)
    r = run_bass_kernel_spmd(nc, [arrays], core_ids=[0])
    return r.results[0]["out"]
```

```python
from contextlib import ExitStack

import concourse.bass as bass
from concourse import mybir

ALU = mybir.AluOpType
ACT = mybir.ActivationFunctionType
AX = mybir.AxisListType
F32 = mybir.dt.float32
F32R = mybir.dt.float32r
BF16 = mybir.dt.bfloat16
I32 = mybir.dt.int32
U32 = mybir.dt.uint32

P = 128
LN_EPS, RMS_EPS, TOP_EPS = 1e-5, 1e-8, 1e-6
Z_LOW, Z_HIGH = -88.7, 16.635533
CLAMP = 10000.0
LOGIT_SAFE, V_SAFE = 40.0, 1e24
AHEAD = 5


def flamingo_block(nc, x, ctx_kv, g_xattn, g_ffn, wq, bq, wk, bk, wv, bv, wo, bo,
                   norm_w, router_w, sw1, sb1, sw2, sb2, ew1, eb1, ew2, eb2, out):
    B, NQ, D = x.shape
    _, NK, CK = ctx_kv.shape
    E, _, H = ew1.shape
    HEADS, DH = 16, 16
    PH = P // DH
    SCALE = float(DH) ** -0.5
    QT = NQ // P
    T = B * QT
    KT = NK // P
    KD = D // P
    CH = CK // 2
    HM = H // P
    GROUPS = HEADS // 4
    CHUNK = 2 * P
    SHARED = B * NQ // CHUNK
    SLOTS = (2 * B * NQ - E) // CHUNK + E
    CAP = B * NQ + CHUNK
    S, R = "shared", "routed"
    CHUNKS = [(S, c) for c in range(AHEAD)] + [(R, j) for j in range(SLOTS)] + [(S, c) for c in range(AHEAD, SHARED)]
    SETS = SLOTS + 2

    def set_of(i):
        kind, c = CHUNKS[i]
        return c + 1 if kind == R else 0 if c < AHEAD else SETS - 1

    def last_of(s):
        return max(i for i in range(len(CHUNKS)) if set_of(i) == s)

    PASSES = ((0, 0), (0, 1), (1, 0))
    ROWS = 64 + len(PASSES) * DH
    DEEP = 4

    x_t = x.rearrange("b (t p) d -> b p t d", p=P)
    ctx_t = ctx_kv.rearrange("b (t p) c -> b p t c", p=P)
    out_t = out.rearrange("b (t p) d -> (b t) p d", p=P)

    k_rows = nc.dram_tensor("k_rows", (B, 2, D, NK), F32).ap()
    q_rows = nc.dram_tensor("q_rows", (B, 2, D, NQ), F32).ap()
    slot_x = nc.dram_tensor("slot_x", (E * CAP, D), F32).ap()
    slot_y = nc.dram_tensor("slot_y", (SLOTS * CHUNK, D), F32).ap()
    maxima = nc.dram_tensor("maxima", (B, HEADS // 2, P, 2 * NQ), F32).ap()
    b1_cols = nc.dram_tensor("b1_cols", (E + 1, P, HM), F32).ap()

    with ExitStack() as top:
        def sem(name):
            return top.enter_context(nc.semaphore(name))

        def sb(name, shape, dt=F32, scope=top):
            return scope.enter_context(nc.sbuf_tensor(name, shape, dt))

        x_sb = sb("x_sb", [P, T, D])
        normed = sb("normed", [P, T, D])
        wo_p = [sb(f"wo_p{i}", [P, KD, D], F32R) for i in range(2)]
        ident = sb("ident", [P, P])
        before = sb("before", [P, P])
        ones = sb("ones", [P, P])
        bo_bc = sb("bo_bc", [P, D])
        bv_bc = sb("bv_bc", [P, D])
        nw_bc = sb("nw_bc", [P, D])
        tanh_g = sb("tanh_g", [P, 2])
        g_bc = sb("g_bc", [P, 2])
        logits = sb("logits", [P, QT, E])
        rw_t = sb("rw_t", [P, KD, E])
        iota_e = sb("iota_e", [P, E])
        iota_s = sb("iota_s", [P, SLOTS])
        stat6 = sb("stat6", [P, QT, 6])
        mv = sb("mv", [P, 2, QT, 2])
        rs = sb("rs", [P, 3, QT])
        ra = sb("ra", [P, QT])
        rt = sb("rt", [P, QT])
        ssq = sb("ssq", [P, QT])
        half_neg = sb("half_neg", [P, QT])
        z_all = sb("z_all", [P, T, 2])
        e_all = sb("e_all", [P, 2, T])
        r_all = sb("r_all", [P, 2, T])
        dest = sb("dest", [P, 2, T], U32)
        flag = sb("flag", [1, 1], I32)

        one = ExitStack()
        k_stack = sb("k_stack", [P, HEADS // 2, NK], F32R, one)
        q_stack = sb("q_stack", [P, HEADS // 2, 2, NQ], F32R, one)
        v_sb = [sb(f"v{n}", [P, KT, HEADS, DH + 1], F32, one) for n in range(B)]

        qkv = ExitStack()
        ctx_raw = sb("ctx_raw", [P, KT, CK], F32, qkv)
        ctx_p = [sb(f"ctx_p{i}", [CH, 2, NK], F32R, qkv) for i in range(2)]
        xn_p = [sb(f"xn_p{i}", [P, KD, NQ], F32R, qkv) for i in range(2)]
        wq_p = [sb(f"wq_p{i}", [P, KD, D], F32R, qkv) for i in range(2)]
        wk_p = [sb(f"wk_p{i}", [CH, 2, D], F32R, qkv) for i in range(2)]
        wv_p = [sb(f"wv_p{i}", [CH, 2, D], F32R, qkv) for i in range(2)]
        qk_col = sb("qk_col", [P, 2 * KD], F32, qkv)
        bq_col, bk_col = qk_col[:, 0:KD], qk_col[:, KD:2 * KD]
        head_of = sb("head_of", [P, HEADS + PH], F32R, qkv)
        junk = sb("junk", [P, 512], BF16, qkv)
        v_ss = sb("v_ss", [P, B, KT // 2], F32, qkv)
        norm2 = sb("norm2", [HEADS, B, 3], I32, qkv)
        k_max = sb("k_max", [HEADS, B], F32, qkv)
        qk_max = sb("qk_max", [HEADS, B], F32, qkv)
        checks = sb("checks", [P, 2], F32, qkv)
        v_ok = sb("v_ok", [P, B, KT // 2], F32, qkv)

        raw = ExitStack()
        w_raw = sb("w_raw", [P, 4, 512], F32, raw)
        bias_rows = sb("bias_rows", [P, P], F32, raw)
        b1_all = sb("b1_all", [P, E + 1, HM], F32, raw)
        rw_rows = sb("rw_rows", [E, D], F32, raw)
        head_f = sb("head_f", [P, HEADS + PH], F32, raw)
        raw.close()
        stage_s = [sb(f"stage_s{i}", [P, 512], F32R, qkv) for i in range(DEEP)]
        stage_p = [[sb(f"stage_p{i}{j}", [P, 512], F32R, qkv) for j in range(2)] for i in range(DEEP)]
        qkv.close()

        prob = [[sb(f"prob{k}{i}", [P, 2, NQ], F32, one) for i in range(2)] for k in range(2)]
        clip = [sb(f"clip{i}", [P, 2, NQ], F32, one) for i in range(2)]
        high = [sb(f"high{i}", [P, 2, NQ], F32, one) for i in range(2)]
        is_num = sb("is_num", [P, 2, NQ], F32, one)
        keep = sb("keep", [P, 2], F32, one)
        after_at = ExitStack()
        o_t = sb("o_t", [P, GROUPS, NQ], F32, after_at)
        on = [sb(f"on{i}", [P, HEADS, DH], F32, after_at) for i in range(2)]
        on_p = [[sb(f"on_p{i}{j}", [P, KD, P], F32R, after_at) for j in range(2)] for i in range(2)]
        r_sum = sb("r_sum", [P, HEADS], F32, after_at)
        n_t = sb("n_t", [P, 2, KD, P], F32, after_at)
        stage_t = sb("stage_t", [P, D], F32, after_at)
        z_c = sb("z_c", [P, QT, E], F32, after_at)
        z_top = sb("z_top", [P, QT, 8], F32, after_at)
        e_top = sb("e_top", [P, QT, 8], U32, after_at)
        mask = [sb(f"mask{i}", [P, QT, E], F32, after_at) for i in range(2)]
        mask_s = sb("mask_s", [P, QT, E], F32, after_at)
        upto = sb("upto", [P, QT + 1, E], F32, after_at)
        pos = sb("pos", [P, QT, E], F32, after_at)
        pick = sb("pick", [P, QT, E], F32, after_at)
        dest_f = sb("dest_f", [P, 2, QT], F32, after_at)
        n_i = sb("n_i", [P, E], I32, after_at)
        n_s = sb("n_s", [P, E], I32, after_at)
        n_slots = sb("n_slots", [P, E], F32, after_at)
        pad_f = sb("pad_f", [P, E], F32, after_at)
        last_slot = sb("last_slot", [P, 1], F32, after_at)
        slot_n = sb("slot_n", [P, SLOTS], F32, after_at)
        slot_ef = sb("slot_ef", [P, SLOTS], F32, after_at)
        slot_1st = sb("slot_1st", [P, SLOTS], F32, after_at)
        slot_tmp = sb("slot_tmp", [P, SLOTS], F32, after_at)
        after_at.close()
        one.close()

        two = ExitStack()
        set_0 = dict(raw=[sb(f"w{i}_raw0", [P, 2048], F32, two) for i in (1, 2)],
                     w1=[sb(f"w1_p0{j}", [P, KD, H], F32R, two) for j in range(2)],
                     w2=[sb(f"w2_p0{j}", [P, HM, D], F32R, two) for j in range(2)])
        xt_p = [[sb(f"xt_p{i}{j}", [P, KD, CHUNK], F32R, two) for j in range(2)] for i in range(2)]
        h_f = [sb(f"h_f{i}", [P, 2, CHUNK], F32, two) for i in range(2)]
        y_sb = [sb(f"y_sb{i}", [P, 2, D], F32, two) for i in range(2)]
        h_p = [[sb(f"h_p{i}{j}", [P, HM, CHUNK], F32R, two) for j in range(2)] for i in range(2)]
        b1_sb = [sb(f"b1_sb{i}", [P, HM], F32, two) for i in range(3)]
        b2_sb = [sb(f"b2_sb{i}", [P, D], F32, two) for i in range(3)]
        zero_rows = sb("zero_rows", [P, D], F32, two)
        first = sb("first", [P, E + 1], F32, two)
        first_row = sb("first_row", [P, E], F32, two)
        pad_row = sb("pad_row", [P, E], I32, two)
        slot_e = sb("slot_e", [P, SLOTS], I32, two)
        slot_row = sb("slot_row", [P, SLOTS], I32, two)
        s_top = sb("s_top", [P, T, 2], F32, two)
        s_sum = sb("s_sum", [P, T], F32, two)
        w_top = sb("w_top", [P, T, 2], F32, two)
        one_hot = sb("one_hot", [P, 2 * T, E], F32, two)
        dest_y = sb("dest_y", [P, 2 * T], F32, two)
        x_in = [sb(f"x_in{i}", [P, 2, D], F32, two) for i in range(2)]
        set_1 = dict(raw=[sb(f"w{i}_raw1", [P, 2048], F32, two) for i in (1, 2)],
                     w1=[sb(f"w1_p1{j}", [P, KD, H], F32R, two) for j in range(2)],
                     w2=[sb(f"w2_p1{j}", [P, HM, D], F32R, two) for j in range(2)])
        w1_raw = [w["raw"][0][:, :].rearrange("p (k h) -> p k h", k=KD) for w in (set_0, set_1)]
        w2_raw = [w["raw"][1][:, :].rearrange("p (k d) -> p k d", k=HM) for w in (set_0, set_1)]
        w1_p, w2_p = [[w[name] for w in (set_0, set_1)] for name in ("w1", "w2")]
        y_in = [[sb(f"y_in{i}{j}", [P, D], F32, two) for j in range(2)] for i in range(4)]
        two.close()

        sc = [top.enter_context(nc.psum_tensor(f"sc{i}", [P, 2, 512], F32)) for i in range(2)]
        pv = [top.enter_context(nc.psum_tensor(f"pv{i}", [P, 512], F32)) for i in range(2)]
        mb = [top.enter_context(nc.psum_tensor(f"mb{i}", [P, 512], F32)) for i in range(2)]

        loaded_x = [sem(f"loaded_x{n}") for n in range(B)]
        loaded_w = sem("loaded_w")
        loaded_bias = sem("loaded_bias")
        loaded_small = sem("loaded_small")
        loaded_ctx = sem("loaded_ctx")
        ident_set = sem("ident_set")
        consts_set = sem("consts_set")
        zeros_set = sem("zeros_set")
        w_split = sem("w_split")
        tanh_done = sem("tanh_done")
        dve_step = sem("dve_step")
        pool_step = sem("pool_step")
        stats_done = sem("stats_done")
        rstd_done = sem("rstd_done")
        xn_done = sem("xn_done")
        normed_done = sem("normed_done")
        fill_done = sem("fill_done")
        act_read = sem("act_read")
        dve_read = sem("dve_read")
        checks_done = sem("checks_done")
        checks_sum = sem("checks_sum")
        flag_done = sem("flag_done")
        post_done = sem("post_done")
        post_read = sem("post_read")
        slow_stack = sem("slow_stack")
        slow_scores = sem("slow_scores")
        slow_step = sem("slow_step")
        slow_high = sem("slow_high")
        slow_max = sem("slow_max")
        slow_max_out = sem("slow_max_out")
        slow_max_in = [sem(f"slow_max_in{i}") for i in range(2)]
        slow_num = sem("slow_num")
        slow_keep = sem("slow_keep")
        slow_logits = sem("slow_logits")
        stage_out = [sem(f"stage_out{i}") for i in range(DEEP)]
        stack_in = [sem(f"stack_in{h}") for h in range(2)]
        scores_done = sem("scores_done")
        exp_done = sem("exp_done")
        pv_done = sem("pv_done")
        pv_read = sem("pv_read")
        b1_read = sem("b1_read")
        b1_out = sem("b1_out")
        masks_done = sem("masks_done")
        exp_z = sem("exp_z")
        dest_done = sem("dest_done")
        slots_done = sem("slots_done")
        padded = sem("padded")
        dest_y_done = sem("dest_y_done")
        scattered = sem("scattered")
        raw1_in = [sem(f"raw1_in{i}") for i in range(2)]
        raw2_in = [sem(f"raw2_in{i}") for i in range(2)]
        biases_in = [sem(f"biases_in{i}") for i in range(3)]
        w1_hi = sem("w1_hi")
        w1_lo = sem("w1_lo")
        w2_hi = sem("w2_hi")
        w2_lo = sem("w2_lo")
        x_in_done = [sem(f"x_in_done{i}") for i in range(2)]
        h_done = sem("h_done")
        relu_done = sem("relu_done")
        h_split = sem("h_split")
        y_done = sem("y_done")
        y_read = sem("y_read")
        y_out = [sem(f"y_out{i}") for i in range(2)]
        gathered = [sem(f"gathered{i}") for i in range(4)]
        combined = sem("combined")
        stored = sem("stored")

        TX, TC, Q, K, V, N = range(6)
        PREP = []
        for n in range(B + 1):
            if n < B:
                PREP += [(n, TC, i) for i in range(4)]
            if n:
                PREP += [(n - 1, Q, m) for m in range(KD)]
            if n < B:
                PREP += [(n, K, i) for i in range(KD)]
            if n:
                PREP += [(n - 1, N, 2)]
            if n < B:
                PREP += [(n, K, 2), (n, K, 3), (n, N, 0), (n, V, 0), (n, V, 1), (n, N, 1),
                         (n, V, 2), (n, V, 3)] + [(n, TX, i) for i in range(KD)]
        FILLS = len(PREP)
        STAGED = [(n, kind, j) for n, kind, j in PREP if kind in (Q, K)]
        STAGES = len(STAGED)
        BY_ACT = (TX, TC, Q, K, V)

        def acts(f):
            return sum(kind in BY_ACT for _, kind, _ in PREP[:f + 1])

        def at(n, kind, j):
            return PREP.index((n, kind, j))

        def outs(i, s):
            return 32 * ((s - i + DEEP - 1) // DEEP)

        def stores(i, before_chunk):
            return sum(kind == R for k, (kind, _) in enumerate(CHUNKS) if k % 2 == i and k < before_chunk)

        def prep_bank(f):
            f %= 8
            return sc[f // 2][:, f % 2, :] if f < 4 else pv[f - 4][:, :] if f < 6 else mb[f - 6][:, :]

        def norm_staged(n, which):
            return [STAGED.index((n, Q, m) if which == 2 else (n, K, 2 * which + m)) for m in range(KD)]

        def norm_of(s):
            n, kind, j = STAGED[s]
            return at(n, N, 2 if kind == Q else j // 2)

        T1, T2, T3, T4, T5, T6 = range(6)
        POST = ((T1, 0), (T1, 1), (T2, 0), (T1, 2), (T2, 1), (T3, 0), (T1, 3), (T2, 2),
                (T3, 1), (T2, 3), (T3, 2), (T3, 3), (T4, 0), (T5, 0), (T4, 1), (T5, 1), (T6, 0))
        EARLY = 12
        WS = GROUPS * KT
        POST_AT = list(range(EARLY)) + [20, 21, 22, 23, 28]
        LN_AT, RMS_AT = 14, 18

        X = "x"
        LAST_AT = [0, 0, 1, 1, 2, 2, 3, 3, 4, 4, 5, 5, 8, 9, 9, 10, 13]
        LAST_LN, LAST_RMS, SLOTS_AT = 6, 7, 13
        COMBINE_AT = [4 * len(CHUNKS) - k for k in range(5, 0, -1)]
        TURN_AT = 3
        MB = [(X, 0)]
        for at_q in range(len(CHUNKS) * 4):
            MB += [(B - 1, i) for i, when in enumerate(LAST_AT) if when == at_q]
            if at_q % 4 == TURN_AT and at_q // 4 + 1 < len(CHUNKS):
                MB += [(X, at_q // 4 + 1)]

        def mb_count(what):
            return (B - 1) * len(POST) + MB.index(what) + 1

        STACK = 4 * len(PASSES) * 16

        def post_slot(b, s):
            return POST_AT.index(s) if b > 0 and s in POST_AT else None

        def after(n, kind, t):
            i = POST.index((kind, t))
            return n * len(POST) + i + 1 if n < B - 1 else mb_count((n, i))

        CHECKS = HEADS * B + P * B * KT // 2

        def hps(f):
            return sc[f % 4 // 2][:, f % 2, :].rearrange("p (r n) -> p r n", r=2)

        block = top.enter_context(nc.Block())

        @block.sync
        def _(sp):
            def load(dst, src, done):
                sp.dma_start(dst, src).then_inc(done, 16)

            load(ctx_raw[:, :, :], ctx_t[0], loaded_ctx)
            load(w_raw[0:CH, 1, :].rearrange("p (k n) -> p k n", k=2), wk.rearrange("(k p) n -> p k n", p=CH), loaded_w)
            load(w_raw[0:CH, 2, :].rearrange("p (k n) -> p k n", k=2), wv.rearrange("(k p) n -> p k n", p=CH), loaded_w)
            load(x_sb[:, 0:QT, :], x_t[0], loaded_x[0])
            load(w_raw[:, 0, :].rearrange("p (k n) -> p k n", k=KD), wq.rearrange("(k p) n -> p k n", p=P), loaded_w)
            load(w_raw[:, 3, :].rearrange("p (k n) -> p k n", k=KD), wo.rearrange("(k p) n -> p k n", p=P), loaded_w)
            for n in range(1, B):
                load(x_sb[:, n * QT:(n + 1) * QT, :], x_t[n], loaded_x[n])

            def write_rows(s):
                n, kind, j = STAGED[s]
                m, half = (j, 0) if kind == Q else (j % 2, j // 2)
                rows = (q_rows if kind == Q else k_rows)[n]
                for part in range(2):
                    if part == 0:
                        sp.wait_ge(act_read, acts(at(*STAGED[s])))
                    else:
                        sp.wait_ge(dve_read, at(*STAGED[s]) + 1)
                    sp.dma_start(rows[part, m * P:(m + 1) * P, half * 512:half * 512 + 512],
                                 stage_p[s % DEEP][part][:, :].bitcast(F32)).then_inc(stage_out[s % DEEP], 16)

            def stack_loads(n, h, done):
                pairs = slice(4 * h, 4 * h + 4)
                return [(stack[64 * a + DH * blk:64 * a + DH * blk + DH, pairs, :].bitcast(F32),
                         rows[n, part].rearrange("(pair a d) n -> a d pair n", a=2, d=DH)[a, :, pairs, :], done)
                        for blk, parts in enumerate(((0, 0), (0, 1), (1, 0))) for a in range(2)
                        for rows, stack, part in ((k_rows, k_stack, parts[0]), (q_rows, q_stack[:, :, a], parts[1]))]

            def load_stacks(n, h, done):
                for dst, src, done in stack_loads(n, h, done):
                    load(dst, src, done)

            def next_stacks(n, h):
                sp.wait_ge(scores_done, 2 * KT * ((n - 1) * GROUPS + 2 * h + 2))
                load_stacks(n, h, stack_in[h])

            written = max(norm_staged(0, 2)) + 1
            first = stack_loads(0, 0, stack_in[0]) + stack_loads(0, 1, stack_in[1])
            for s in range(STAGES):
                write_rows(s)
                if s == written + 1:
                    for i in range(DEEP):
                        sp.wait_ge(stage_out[i], outs(i, written))
                    sp.wait_ge(zeros_set, 1)
                if s > written:
                    for _ in range(min(2, len(first))):
                        load(*first.pop(0))
            for one_load in first:
                load(*one_load)
            for i in range(DEEP):
                sp.wait_ge(stage_out[i], outs(i, STAGES))
            sp.wait_ge(flag_done, 1)
            held = sp.value_load(flag[0:1, 0:1], min_val=0, max_val=CHECKS)
            with sp.If(held < CHECKS):
                pair = 0
                for n in range(B):
                    for g in range(GROUPS):
                        if n >= 1 and g % 2 == 0:
                            sp.wait_ge(slow_scores, 2 * KT * ((n - 1) * GROUPS + g + 2))
                            load_stacks(n, g // 2, slow_stack)
                        for i in range(2):
                            pair += 1
                            sp.wait_ge(slow_max, pair)
                            sp.dma_start(maxima[n, 2 * g + i], high[i][:, :, :].rearrange("p a n -> p (a n)")
                                         ).then_inc(slow_max_out, 16)
                            sp.wait_ge(slow_max_out, 16 * pair)
                for h in range(2):
                    load_stacks(0, h, slow_stack)
                for n in range(B):
                    for g in range(GROUPS):
                        for i in range(2):
                            if n or g:
                                sp.wait_ge(slow_logits, 2 * KT * (n * GROUPS + g))
                            sp.dma_start(high[i][:, :, :].rearrange("p a n -> p (a n)"),
                                         maxima[n, 2 * g + i]).then_inc(slow_max_in[i], 16)
                        if n + 1 < B and g % 2:
                            next_stacks(n + 1, g // 2)
            with sp.Else():
                for n in range(1, B):
                    for h in range(2):
                        next_stacks(n, h)

            def load_w1(s):
                m1 = sw1
                if 0 < s < SETS - 1:
                    e = sp.value_load(slot_e[0:1, s - 1:s], min_val=0, max_val=E - 1)
                    m1 = ew1[bass.ds(e, 1)].rearrange("e d h -> (e d) h")
                if s >= 2:
                    sp.wait_ge(w1_hi, s - 1)
                    sp.wait_ge(w1_lo, s - 1)
                sp.dma_start(w1_raw[s % 2], m1.rearrange("(k p) h -> p k h", p=P)).then_inc(raw1_in[s % 2], 16)

            def load_w2(s):
                m2 = sw2
                if 0 < s < SETS - 1:
                    e = sp.value_load(slot_e[0:1, s - 1:s], min_val=0, max_val=E - 1)
                    m2 = ew2[bass.ds(e, 1)].rearrange("e h d -> (e h) d")
                if s >= 2:
                    sp.wait_ge(w2_hi, s - 1)
                    sp.wait_ge(w2_lo, s - 1)
                sp.dma_start(w2_raw[s % 2], m2.rearrange("(k p) d -> p k d", p=P)).then_inc(raw2_in[s % 2], 16)

            def load_biases(s):
                c1, c2 = b1_cols[0], sb2.rearrange("(a n) -> a n", a=1)
                if 0 < s < SETS - 1:
                    e = sp.value_load(slot_e[0:1, s - 1:s], min_val=0, max_val=E - 1)
                    c1 = b1_cols[1:E + 1][bass.ds(e, 1)].rearrange("e p m -> (e p) m")
                    c2 = eb2[bass.ds(e, 1), :]
                if s >= 3:
                    sp.wait_ge(relu_done, HM // 2 * (last_of(s - 3) + 1))
                    sp.wait_ge(y_read, last_of(s - 3) + 1)
                sp.dma_start(b1_sb[s % 3][:, :], c1).then_inc(biases_in[s % 3], 16)
                sp.dma_start(b2_sb[s % 3][:, :], c2.to_broadcast([P, D])).then_inc(biases_in[s % 3], 16)

            def load_slot(j):
                row = sp.value_load(slot_row[0:1, j:j + 1], min_val=0, max_val=E * CAP - CHUNK)
                if j >= 2:
                    sp.wait_ge(post_done, mb_count((X, CHUNKS.index((R, j - 2)))))
                sp.dma_start(x_in[j % 2][:, :, :],
                             slot_x[bass.ds(row, CHUNK), :].rearrange("(t p) d -> p t d", p=P)
                             ).then_inc(x_in_done[j % 2], 16)

            sp.wait_ge(scores_done, 2 * KT * (B * GROUPS - 2))
            load_w1(0)
            load_w2(0)
            sp.wait_ge(pv_done, B * WS)
            sp.wait_ge(b1_out, 16)
            load_biases(0)
            sp.wait_ge(slots_done, 1)
            load_w1(1)
            for e in range(E):
                row = sp.value_load(pad_row[0:1, e:e + 1], min_val=0, max_val=E * CAP - CHUNK)
                sp.dma_start(slot_x[bass.ds(row, CHUNK), :].rearrange("(t p) d -> p t d", p=P),
                             zero_rows[:, :].unsqueeze(1).to_broadcast([P, 2, D])).then_inc(padded, 16)
            load_w2(1)
            load_biases(1)
            sp.wait_ge(scattered, 16 * 2 * T)
            sp.wait_ge(padded, 16 * E)
            load_slot(0)
            load_slot(1)
            for j in range(SLOTS):
                load_w1(j + 2)
                load_biases(j + 2)
                load_w2(j + 2)
                if j + 2 < SLOTS:
                    load_slot(j + 2)
            for t in range(T):
                sp.wait_ge(combined, t + 1)
                sp.dma_start(out_t[t], x_sb[:, t, :]).then_inc(stored, 16)
            sp.wait_ge(stored, 16 * T)

        @block.gpsimd
        def _(pool):
            count = [0]

            def step(ins):
                count[0] += 1
                ins.then_inc(pool_step, 1)
                pool.wait_ge(pool_step, count[0])

            step(nc.gpsimd.memset(ident[:, :], 0.0))
            step(nc.gpsimd.affine_select(out=ident[:, :], in_=ident[:, :], compare_op=ALU.not_equal,
                                         fill=1.0, base=0, pattern=[[-1, P]], channel_multiplier=1))
            step(nc.gpsimd.memset(head_f[:, :], 1.0))
            step(nc.gpsimd.affine_select(out=head_f[:, :], in_=head_f[:, :], compare_op=ALU.is_ge,
                                         fill=0.0, base=PH * DH, pattern=[[-DH, HEADS + PH]], channel_multiplier=1))
            step(nc.gpsimd.affine_select(out=head_f[:, :], in_=head_f[:, :], compare_op=ALU.is_ge,
                                         fill=0.0, base=DH - 1 - PH * DH, pattern=[[DH, HEADS + PH]],
                                         channel_multiplier=-1))
            step(nc.gpsimd.memset(half_neg[:, :], -0.5))
            nc.gpsimd.tensor_copy(head_of[:, :], head_f[:, :]).then_inc(ident_set, 1)
            pool.wait_ge(ident_set, 1)
            def rsqrt(which, src, scale, eps):
                step(nc.gpsimd.tensor_scalar(ra[:, :], src, scale, eps, ALU.mult, ALU.add))
                step(nc.gpsimd.tensor_tensor(rs[:, which, :], ra[:, :], half_neg[:, :], ALU.pow))
                step(nc.gpsimd.tensor_tensor(rt[:, :], rs[:, which, :], rs[:, which, :], ALU.mult))
                step(nc.gpsimd.tensor_tensor(rt[:, :], rt[:, :], ra[:, :], ALU.mult))
                step(nc.gpsimd.tensor_scalar(rt[:, :], rt[:, :], -0.5, 1.5, ALU.mult, ALU.add))
                nc.gpsimd.tensor_tensor(rs[:, which, :], rs[:, which, :], rt[:, :],
                                        ALU.mult).then_inc(rstd_done, 1)
                pool.wait_ge(rstd_done, rstd_at(which))

            rstds = [0]

            def rstd_at(_):
                rstds[0] += 1
                return rstds[0]

            def norm_x(n):
                pool.wait_ge(stats_done, rstds[0] + 1)
                rsqrt(0, mv[:, 0, :, 1], 1.0, LN_EPS)

            def norm_mlp(n):
                pool.wait_ge(stats_done, rstds[0] + 1)
                rsqrt(1, mv[:, 1, :, 1], 1.0, LN_EPS)
                pool.wait_ge(stats_done, rstds[0] + 1)
                rsqrt(2, ssq[:, :], 1.0 / D, RMS_EPS)

            norm_x(0)
            step(nc.gpsimd.memset(q_stack[0:64, :, 1, :].bitcast(F32), 0.0))
            step(nc.gpsimd.memset(q_stack[32:64, :, 0, :].bitcast(F32), 0.0))
            step(nc.gpsimd.memset(k_stack[32:64, :, :].bitcast(F32), 0.0))
            nc.gpsimd.memset(q_stack[64:P, :, 0, :].bitcast(F32), 0.0).then_inc(zeros_set, 1)
            pool.wait_ge(zeros_set, 1)
            step(nc.gpsimd.memset(before[:, :], 1.0))
            step(nc.gpsimd.affine_select(out=before[:, :], in_=before[:, :], compare_op=ALU.is_gt,
                                         fill=0.0, base=0, pattern=[[1, P]], channel_multiplier=-1))
            step(nc.gpsimd.memset(ones[:, :], 1.0))
            step(nc.gpsimd.iota(iota_e[:, :], pattern=[[1, E]], base=0, channel_multiplier=0,
                                allow_small_or_imprecise_dtypes=True))
            step(nc.gpsimd.iota(iota_s[:, :], pattern=[[1, SLOTS]], base=0, channel_multiplier=0,
                                allow_small_or_imprecise_dtypes=True))
            for v in v_sb:
                step(nc.gpsimd.memset(v[:, :, :, DH:DH + 1], 1.0))
            pool.nop().then_inc(consts_set, 1)
            for n in range(1, B):
                norm_x(n)

            pool.wait_ge(flag_done, 1)
            held = pool.value_load(flag[0:1, 0:1], min_val=0, max_val=CHECKS)
            with pool.If(held < CHECKS):
                for pair in range(B * GROUPS * 2):
                    pool.wait_ge(slow_high, pair + 1)
                    both = high[pair % 2][:, :, :].rearrange("p a n -> p (a n)")
                    nc.gpsimd.partition_all_reduce(both, both, P, bass.bass_isa.ReduceOp.max).then_inc(slow_max, 1)
                pool.wait_ge(slow_num, 1)
                nc.gpsimd.partition_all_reduce(keep[:, 1:2], keep[:, 0:1], P,
                                               bass.bass_isa.ReduceOp.max).then_inc(slow_keep, 1)
            with pool.Else():
                pass

            def w2_low(s):
                pool.wait_ge(w2_hi, s + 1)
                if s >= 2:
                    pool.wait_ge(y_done, last_of(s - 2) + 1)
                nc.gpsimd.tensor_tensor(w2_p[s % 2][1][:, :, :], w2_raw[s % 2],
                                        w2_p[s % 2][0][:, :, :].bitcast(F32), ALU.subtract).then_inc(w2_lo, 1)

            for n in range(B):
                if n == B - 1:
                    w2_low(0)
                norm_mlp(n)
                pool.wait_ge(dest_done, n + 1)
                for t in range(n * QT, (n + 1) * QT):
                    for c in range(2):
                        pool.indirect_dma_start(out=slot_x, out_offset=bass.IndirectOffsetOnAxis(ap=dest[:, c, t:t + 1], axis=0),
                                                in_=normed[:, t, :], in_offset=None).then_inc(scattered, 16)
            for s in range(1, SETS):
                w2_low(s)
            pool.wait_ge(dest_y_done, 1)
            pool.wait_ge(y_out[0], 16 * stores(0, len(CHUNKS)))
            pool.wait_ge(y_out[1], 16 * stores(1, len(CHUNKS)))
            for t in range(T):
                if t >= 4:
                    pool.wait_ge(combined, t - 3)
                for c in range(2):
                    pool.indirect_dma_start(out=y_in[t % 4][c][:, :], out_offset=None, in_=slot_y,
                                            in_offset=bass.IndirectOffsetOnAxis(ap=dest[:, c, t:t + 1], axis=0)
                                            ).then_inc(gathered[t % 4], 16)

        @block.scalar
        def _(act):
            def row(v):
                return v.rearrange("(a n) -> a n", a=1).to_broadcast([P, v.shape[0]])

            nb = HM * (E + 1)
            for dst, src in ((bias_rows[nb:nb + KD, :], bq.rearrange("(k p) -> k p", p=P)),
                             (bias_rows[nb + KD:nb + 2 * KD, :], bk.rearrange("(k p) -> k p", p=P)),
                             (bias_rows[0:HM, :], sb1.rearrange("(m p) -> m p", p=P)),
                             (bias_rows[HM:nb, :], eb1.rearrange("e (m p) -> (e m) p", p=P)),
                             (rw_rows[:, :], router_w)):
                act.dma_start(dst, src).then_inc(loaded_bias, 16)
            for dst, src in ((bv_bc[:, :], row(bv)), (bo_bc[:, :], row(bo)), (nw_bc[:, :], row(norm_w)),
                             (g_bc[:, 0:1], row(g_xattn)), (g_bc[:, 1:2], row(g_ffn))):
                act.dma_start(dst, src).then_inc(loaded_small, 16)
            act.wait_ge(b1_read, 2)
            act.dma_start(b1_cols.rearrange("s p m -> p s m"), b1_all[:, :, :]).then_inc(b1_out, 16)
            s = 0
            for f, (n, kind, j) in enumerate(PREP):
                if kind == N:
                    continue
                act.wait_ge(fill_done, f + 1)
                bank = prep_bank(f)
                if kind == TX:
                    last = nc.scalar.activation(xn_p[0][:, j, :], bank, ACT.Copy)
                elif kind == TC:
                    k, half = j % 2, j // 2
                    last = nc.scalar.activation(ctx_p[0][:, k, half * 512:half * 512 + 512],
                                                bank[0:CH, :], ACT.Copy)
                elif kind == V:
                    act.wait_ge(act_read, acts(f) - 1)
                    last = nc.scalar.activation(junk[:, :], bank, ACT.Square, accum_out=v_ss[:, n, j:j + 1])
                else:
                    bias = bq_col[:, j:j + 1] if kind == Q else bk_col[:, j % 2:j % 2 + 1]
                    if s == 0:
                        act.wait_ge(b1_out, 16)
                        act.wait_ge(w_split, 4)
                    if s >= DEEP:
                        act.wait_ge(fill_done, norm_of(s - DEEP) + 1)
                        act.wait_ge(stage_out[s % DEEP], outs(s % DEEP, s))
                    nc.scalar.activation(stage_s[s % DEEP][:, :], bank, ACT.Square, bias=bias)
                    last = nc.scalar.activation(stage_p[s % DEEP][0][:, :], bank, ACT.Identity, bias=bias)
                    s += 1
                last.then_inc(act_read, 1)
                if (kind, j) == (TC, 3) and n + 1 < B:
                    act.dma_start(ctx_raw[:, :, :], ctx_t[n + 1]).then_inc(loaded_ctx, 16)
            act.wait_ge(loaded_small, 16 * 5)
            nc.scalar.activation(tanh_g[:, :], g_bc[:, :], ACT.Tanh).then_inc(tanh_done, 1)

            def exponentials(ready):
                for u in range(2 * B * WS):
                    w = u // 2
                    act.wait_ge(ready, u + 1)
                    if w >= 2:
                        act.wait_ge(pv_done, w - 1)
                    if ready is scores_done:
                        nc.scalar.activation(prob[w % 2][u % 2][:, :, :], sc[u % 2][:, :, :], ACT.Exp,
                                             scale=SCALE).then_inc(exp_done, 1)
                    else:
                        nc.scalar.activation(prob[w % 2][u % 2][:, :, :], clip[u % 2][:, :, :],
                                             ACT.Exp).then_inc(exp_done, 1)

            act.wait_ge(flag_done, 1)
            held = act.value_load(flag[0:1, 0:1], min_val=0, max_val=CHECKS)
            with act.If(held < CHECKS):
                exponentials(slow_logits)
            with act.Else():
                exponentials(scores_done)

            def w1_high(s):
                act.wait_ge(raw1_in[s % 2], 16 * (s // 2 + 1))
                if s >= 2:
                    act.wait_ge(h_done, HM // 2 * (last_of(s - 2) + 1))
                nc.scalar.activation(w1_p[s % 2][0][:, :, :], w1_raw[s % 2], ACT.Copy).then_inc(w1_hi, 1)

            def w2_high(s):
                act.wait_ge(raw2_in[s % 2], 16 * (s // 2 + 1))
                if s >= 2:
                    act.wait_ge(y_done, last_of(s - 2) + 1)
                nc.scalar.activation(w2_p[s % 2][0][:, :, :], w2_raw[s % 2], ACT.Copy).then_inc(w2_hi, 1)

            w1_high(0)
            w2_high(0)
            for i, (chunk, c) in enumerate(CHUNKS):
                s = set_of(i)
                act.wait_ge(biases_in[s % 3], 32 * (s // 3 + 1))
                for q in range(HM // 2):
                    f = i * (HM // 2) + q
                    act.wait_ge(h_done, f + 1)
                    if f >= 2:
                        act.wait_ge(h_split, f - 1)
                    for m in (2 * q, 2 * q + 1):
                        last = nc.scalar.activation(h_f[f % 2][:, m % 2, :], hps(f)[:, m % 2, :], ACT.Relu,
                                                    bias=b1_sb[s % 3][:, m:m + 1])
                    if chunk == S:
                        for m in (2 * q, 2 * q + 1):
                            last = nc.scalar.activation(h_p[i % 2][0][:, m, :], hps(f)[:, m % 2, :], ACT.Relu,
                                                        bias=b1_sb[s % 3][:, m:m + 1])
                    last.then_inc(relu_done, 1)
                    if q == 0 and i >= 2 and CHUNKS[i - 2][0] == R:
                        act.wait_ge(y_read, i - 1)
                        j = CHUNKS[i - 2][1]
                        act.dma_start(slot_y[j * CHUNK:(j + 1) * CHUNK, :].rearrange("(t p) d -> p t d", p=P),
                                      y_sb[i % 2][:, :, :]).then_inc(y_out[i % 2], 16)
                    if q == 1 and i == last_of(s) and s + 1 < SETS:
                        w1_high(s + 1)
                    if q == 2 and s > 0 and set_of(i - 1) != s:
                        w2_high(s)
                    if q == 3 and i == AHEAD:
                        act.wait_ge(dest_done, B)
                        nc.scalar.activation(s_top[:, :, :], z_all[:, :, :], ACT.Exp, scale=-1.0).then_inc(exp_z, 1)

        @block.vector
        def _(dve):
            v = nc.vector
            count = [0]

            def step(ins):
                count[0] += 1
                ins.then_inc(dve_step, 1)
                return count[0]

            def settle():
                dve.wait_ge(dve_step, count[0])

            def split(hi, lo, src):
                step(v.tensor_copy(hi, src))
                settle()
                return v.tensor_tensor(lo, src, hi.bitcast(F32), ALU.subtract)

            fill = [0]

            def filled():
                if fill[0]:
                    dve.wait_ge(post_read, fill[0])
                fill[0] += 1
                dve.wait_ge(post_done, fill[0])
                return mb[(fill[0] - 1) % 2]

            def stats(which, tile, t):
                step(v.bn_stats(stat6[:, t, :], x_sb[:, tile, :]))
                settle()
                return v.bn_aggr(mv[:, which, t, :], stat6[:, t, :])

            stat_rounds = [0]

            def ln_x_stats(n):
                dve.wait_ge(loaded_x[n], 16)
                for t in range(QT):
                    last = stats(0, n * QT + t, t)
                    if t < QT - 1:
                        step(last)
                last.then_inc(stats_done, 1)
                stat_rounds[0] += 1

            def ln_x(n):
                dve.wait_ge(rstd_done, stat_rounds[0])
                for t in range(QT):
                    last = v.tensor_scalar(normed[:, n * QT + t, :], x_sb[:, n * QT + t, :], mv[:, 0, t, 0:1],
                                           rs[:, 0, t:t + 1], ALU.subtract, ALU.mult)
                    if t < QT - 1:
                        step(last)
                last.then_inc(xn_done, 1)

            def prep(f):
                n, kind, j = PREP[f]
                bank = prep_bank(f)
                if kind == N:
                    dve.wait_ge(fill_done, f + 1)
                else:
                    dve.wait_ge(act_read, acts(f))
                if kind == TX:
                    last = v.tensor_tensor(xn_p[1][:, j, :], bank, xn_p[0][:, j, :].bitcast(F32), ALU.subtract)
                elif kind == TC:
                    k, cols = j % 2, slice(j // 2 * 512, j // 2 * 512 + 512)
                    last = v.tensor_tensor(ctx_p[1][:, k, cols], bank[0:CH, :], ctx_p[0][:, k, cols].bitcast(F32),
                                           ALU.subtract)
                elif kind == N:
                    last = v.tensor_reduce(norm2[:, n, j:j + 1], bank[0:HEADS, :].bitcast(I32), AX.X,
                                           ALU.max)
                elif kind == V:
                    last = v.tensor_copy(v_sb[n][:, 2 * j:2 * j + 2, :, 0:DH].rearrange("p t h d -> p (t h) d"),
                                         bank.rearrange("p (h d) -> p h d", d=DH))
                else:
                    s = STAGED.index((n, kind, j))
                    if s >= DEEP:
                        dve.wait_ge(stage_out[s % DEEP], outs(s % DEEP, s))
                    bias = bq_col[:, j:j + 1] if kind == Q else bk_col[:, j % 2:j % 2 + 1]
                    last = v.scalar_tensor_tensor(stage_p[s % DEEP][1][:, :], bank, bias,
                                                  stage_p[s % DEEP][0][:, :].bitcast(F32), ALU.add, ALU.subtract)
                last.then_inc(dve_read, 1)

            def check():
                dve.wait_ge(dve_read, FILLS)
                step(v.tensor_tensor(k_max[:, :].bitcast(I32), norm2[:, :, 0], norm2[:, :, 1], ALU.max))
                step(v.memset(checks[:, :], 0.0))
                settle()
                step(v.tensor_tensor(qk_max[:, :], k_max[:, :], norm2[:, :, 2].bitcast(F32), ALU.mult))
                settle()
                step(v.tensor_scalar(qk_max[:, :], qk_max[:, :], (LOGIT_SAFE / SCALE) ** 2, None, ALU.is_le))
                settle()
                step(v.tensor_reduce(checks[0:HEADS, 0:1], qk_max[:, :], AX.X, ALU.add))
                step(v.tensor_scalar(v_ok[:, :, :], v_ss[:, :, :], V_SAFE, None, ALU.is_le))
                settle()
                v.tensor_reduce(checks[:, 1:2], v_ok[:, :, :], AX.XY, ALU.add).then_inc(checks_done, 1)
                dve.wait_ge(checks_sum, 1)
                v.tensor_reduce(checks[0:1, 0:1], mb[0][0:1, 0:2], AX.X, ALU.add).then_inc(checks_done, 1)
                dve.wait_ge(checks_done, 2)
                for bank in pv:
                    step(v.memset(bank[:, :], 0.0))
                for i in range(DEEP):
                    dve.wait_ge(stage_out[i], outs(i, STAGES))
                v.tensor_copy(flag[:, :], checks[0:1, 0:1]).then_inc(flag_done, 1)

            def post(n, i):
                kind, t = POST[i]
                bank = filled()
                tile = n * QT + t
                if kind == T1:
                    o4 = bank[:, :].rearrange("p (h c) -> p h c", h=HEADS)
                    step(v.reciprocal(r_sum[:, :], o4[:, :, DH]))
                    settle()
                    step(v.tensor_tensor(on[t % 2][:, :, :], o4[:, :, 0:DH],
                                         r_sum[:, :].unsqueeze(2).to_broadcast([P, HEADS, DH]), ALU.mult))
                    settle()
                    v.tensor_tensor(on[t % 2][:, :, :].rearrange("p h d -> p (h d)"),
                                    on[t % 2][:, :, :].rearrange("p h d -> p (h d)"), bv_bc[:, :],
                                    ALU.add).then_inc(post_read, 1)
                elif kind == T2:
                    src = bank[:, 0:KD * P].rearrange("p (k n) -> p k n", k=KD)
                    split(on_p[t % 2][0][:, :, :], on_p[t % 2][1][:, :, :], src).then_inc(post_read, 1)
                elif kind == T3:
                    step(v.tensor_tensor(stage_t[:, :], bank[:, 0:D], bo_bc[:, :], ALU.add))
                    settle()
                    v.scalar_tensor_tensor(x_sb[:, tile, :], stage_t[:, :], tanh_g[:, 0:1],
                                           x_sb[:, tile, :], ALU.mult, ALU.add).then_inc(post_read, 1)
                    dve.wait_ge(post_read, fill[0])
                    last = stats(1, tile, t)
                    if t < QT - 1:
                        step(last)
                    else:
                        last.then_inc(stats_done, 1)
                        stat_rounds[0] += 1
                elif kind == T4:
                    v.tensor_copy(n_t[:, :, :, :], bank[:, :].rearrange("p (t k n) -> p t k n", t=2, k=KD)
                                  ).then_inc(post_read, 1)
                elif kind == T5:
                    v.tensor_copy(logits[:, 2 * t:2 * t + 2, :],
                                  bank[:, 0:2 * E].rearrange("p (t e) -> p t e", t=2)).then_inc(post_read, 1)
                    if t == 1:
                        dve.wait_ge(post_read, fill[0])
                        top_two(n)
                else:
                    places(n, bank)

            def top_two(n):
                rows = slice(n * QT, (n + 1) * QT)
                step(v.tensor_scalar(z_c[:, :, :], logits[:, :, :], Z_LOW, Z_HIGH, ALU.max, ALU.min))
                settle()
                for t in range(QT):
                    step(v.max(z_top[:, t, :], z_c[:, t, :]))
                settle()
                for t in range(QT):
                    step(v.max_index(e_top[:, t, :], z_top[:, t, :], z_c[:, t, :]))
                step(v.tensor_copy(z_all[:, rows, :], z_top[:, :, 0:2]))
                settle()
                step(v.tensor_copy(e_all[:, :, rows].rearrange("p c t -> p t c"), e_top[:, :, 0:2]))
                settle()
                for c in range(2):
                    step(v.tensor_tensor(mask[c][:, :, :], iota_e[:, :].unsqueeze(1).to_broadcast([P, QT, E]),
                                         e_all[:, c, rows].unsqueeze(2).to_broadcast([P, QT, E]), ALU.is_equal))
                settle()
                v.tensor_tensor(mask_s[:, :, :], mask[0][:, :, :], mask[1][:, :, :], ALU.add
                                ).then_inc(masks_done, 1)

            def places(n, bank):
                rows = slice(n * QT, (n + 1) * QT)
                if n == 0:
                    step(v.memset(upto[:, 0, :], 0.0))
                else:
                    step(v.tensor_copy(upto[:, 0, :], upto[:, QT, :]))
                settle()
                for t in range(QT):
                    step(v.tensor_tensor(upto[:, t + 1, :], upto[:, t, :],
                                         bank[:, (QT + t) * E:(QT + t + 1) * E], ALU.add))
                    settle()
                v.tensor_tensor(pos[:, :, :], bank[:, 0:QT * E].rearrange("p (t e) -> p t e", t=QT),
                                upto[:, 0:QT, :], ALU.add).then_inc(post_read, 1)
                dve.wait_ge(post_read, fill[0])
                for c in range(2):
                    step(v.tensor_tensor(pick[:, :, :], pos[:, :, :], mask[c][:, :, :], ALU.mult))
                    settle()
                    step(v.tensor_reduce(r_all[:, c, rows], pick[:, :, :], AX.X, ALU.add))
                    settle()
                step(v.scalar_tensor_tensor(dest_f[:, :, :], e_all[:, :, rows], float(CAP), r_all[:, :, rows],
                                            ALU.mult, ALU.add))
                settle()
                v.tensor_copy(dest[:, :, rows], dest_f[:, :, :]).then_inc(dest_done, 1)

            def slots():
                step(v.scalar_tensor_tensor(pad_f[:, :], iota_e[:, :], float(CAP), upto[:, QT, :], ALU.mult, ALU.add))
                step(v.tensor_scalar(n_i[:, :], upto[:, QT, :], float(CHUNK - 1), None, ALU.add))
                settle()
                step(v.tensor_copy(pad_row[:, :], pad_f[:, :]))
                step(v.tensor_scalar(n_s[:, :], n_i[:, :], CHUNK.bit_length() - 1, None, ALU.logical_shift_right))
                settle()
                step(v.tensor_copy(n_slots[:, :], n_s[:, :]))
                step(v.memset(first[:, 0:1], 0.0))
                settle()
                for e in range(E):
                    step(v.tensor_tensor(first[:, e + 1:e + 2], first[:, e:e + 1], n_slots[:, e:e + 1], ALU.add))
                    settle()
                step(v.tensor_scalar(last_slot[:, :], first[:, E:E + 1], -1.0, None, ALU.add))
                step(v.memset(slot_ef[:, :], 0.0))
                step(v.memset(slot_1st[:, :], 0.0))
                settle()
                step(v.tensor_scalar(slot_n[:, :], iota_s[:, :], last_slot[:, 0:1], None, ALU.min))
                for e in range(1, E):
                    settle()
                    step(v.scalar_tensor_tensor(slot_ef[:, :], slot_n[:, :], first[:, e:e + 1], slot_ef[:, :],
                                                ALU.is_ge, ALU.add))
                    step(v.tensor_scalar(slot_tmp[:, :], slot_n[:, :], first[:, e:e + 1], n_slots[:, e - 1:e],
                                         ALU.is_ge, ALU.mult))
                    settle()
                    step(v.tensor_tensor(slot_1st[:, :], slot_1st[:, :], slot_tmp[:, :], ALU.add))
                settle()
                step(v.tensor_copy(slot_e[:, :], slot_ef[:, :]))
                step(v.tensor_tensor(slot_n[:, :], slot_n[:, :], slot_1st[:, :], ALU.subtract))
                step(v.tensor_scalar(slot_ef[:, :], slot_ef[:, :], float(CAP), None, ALU.mult))
                settle()
                step(v.scalar_tensor_tensor(slot_n[:, :], slot_n[:, :], float(CHUNK), slot_ef[:, :], ALU.mult, ALU.add))
                settle()
                v.tensor_copy(slot_row[:, :], slot_n[:, :]).then_inc(slots_done, 1)

            def ln_mlp(n):
                dve.wait_ge(rstd_done, stat_rounds[0])
                for t in range(QT):
                    step(v.tensor_scalar(normed[:, n * QT + t, :], x_sb[:, n * QT + t, :], mv[:, 1, t, 0:1],
                                         rs[:, 1, t:t + 1], ALU.subtract, ALU.mult))
                for t in range(QT):
                    settle()
                    last = v.tensor_tensor_reduce(stage_t[:, :], normed[:, n * QT + t, :], normed[:, n * QT + t, :],
                                                  1.0, 0.0, ALU.mult, ALU.add, ssq[:, t:t + 1])
                    if t < QT - 1:
                        step(last)
                last.then_inc(stats_done, 1)
                stat_rounds[0] += 1

            def rms_mlp(n):
                dve.wait_ge(rstd_done, stat_rounds[0])
                for t in range(QT):
                    last = v.scalar_tensor_tensor(normed[:, n * QT + t, :], normed[:, n * QT + t, :],
                                                  rs[:, 2, t:t + 1], nw_bc[:, :], ALU.mult, ALU.mult)
                    if t < QT - 1:
                        step(last)
                last.then_inc(normed_done, 1)


            dve.wait_ge(loaded_w, 64)
            for i, (w, rows) in enumerate(((wq_p, P), (wk_p, CH), (wv_p, CH), (wo_p, P))):
                raw = w_raw[0:rows, i, :].rearrange("p (k n) -> p k n", k=2)
                split(w[0][:, :, :], w[1][:, :, :], raw).then_inc(w_split, 1)
            ln_x_stats(0)

            dve.wait_ge(b1_read, 1)
            step(v.tensor_copy(b1_all[:, :, :], pv[0][:, 0:HM * (E + 1)].rearrange("p (s m) -> p s m", s=E + 1)))
            step(v.tensor_copy(qk_col[:, :], pv[0][:, HM * (E + 1):HM * (E + 1) + 2 * KD]))
            v.tensor_copy(rw_t[:, :, :], pv[1][:, 0:KD * E].rearrange("p (k e) -> p k e", k=KD)
                          ).then_inc(b1_read, 1)

            for f, (n, kind, j) in enumerate(PREP):
                if (kind, j) == (TC, 2):
                    ln_x(n)
                if n + 1 < B and (kind, j) == (V, 3):
                    ln_x_stats(n + 1)
                prep(f)
            dve.wait_ge(loaded_small, 80)
            dve.wait_ge(consts_set, 1)
            check()
            dve.wait_ge(tanh_done, 1)

            def heads_out(b, g):
                at = b * GROUPS + g
                dve.wait_ge(pv_done, (at + 1) * KT)
                v.tensor_copy(o_t[:, g, :], pv[at % 2][:, :]).then_inc(pv_read, 1)

            def fast_attention():
                for b in range(B):
                    for s in range(WS):
                        if (i := post_slot(b, s)) is not None:
                            post(b - 1, i)
                        if b >= 1 and s == LN_AT:
                            ln_mlp(b - 1)
                        if b >= 1 and s == RMS_AT:
                            rms_mlp(b - 1)
                        if s % KT == KT - 1:
                            heads_out(b, s // KT)

            def general_attention():
                slow = [0]

                def slowly(ins):
                    slow[0] += 1
                    ins.then_inc(slow_step, 1)
                    dve.wait_ge(slow_step, slow[0])

                slowly(v.memset(is_num[:, :, :], 1.0))
                u = 0
                for pair in range(B * GROUPS * 2):
                    i = pair % 2
                    if pair >= 2:
                        dve.wait_ge(slow_max_out, 16 * (pair - 1))
                    slowly(v.memset(high[i][:, :, :], -CLAMP))
                    for kt in range(KT):
                        u += 1
                        dve.wait_ge(slow_scores, u)
                        slowly(v.tensor_copy(clip[0][:, :, :], sc[i][:, :, :]))
                        slowly(v.tensor_tensor(clip[1][:, :, :], clip[0][:, :, :], clip[0][:, :, :], ALU.is_equal))
                        slowly(v.tensor_tensor(is_num[:, :, :], is_num[:, :, :], clip[1][:, :, :], ALU.min))
                        slowly(v.tensor_scalar(clip[0][:, :, :], clip[0][:, :, :], SCALE, CLAMP, ALU.mult, ALU.min))
                        ins = v.tensor_tensor(high[i][:, :, :], high[i][:, :, :], clip[0][:, :, :], ALU.max)
                        if kt < KT - 1:
                            slowly(ins)
                        else:
                            ins.then_inc(slow_high, 1)
                            dve.wait_ge(slow_high, pair + 1)
                slowly(v.tensor_reduce(keep[:, 1:2], is_num[:, :, :], AX.XY, ALU.min))
                v.tensor_scalar(keep[:, 0:1], keep[:, 1:2], -1.0, 1.0, ALU.mult, ALU.add).then_inc(slow_num, 1)
                dve.wait_ge(slow_keep, 1)
                slowly(v.tensor_scalar(keep[:, 0:1], keep[:, 1:2], -1.0, 1.0, ALU.mult, ALU.add))
                for b in range(B):
                    for s in range(WS):
                        w = b * WS + s
                        for i in range(2):
                            u = 2 * w + i
                            if s % KT == 0:
                                dve.wait_ge(slow_max_in[i], 16 * (b * GROUPS + s // KT + 1))
                                slowly(v.tensor_scalar(high[i][:, :, :], high[i][:, :, :], keep[:, 0:1], None, ALU.mult))
                            dve.wait_ge(scores_done, u + 1)
                            if u >= 2:
                                dve.wait_ge(exp_done, u - 1)
                            slowly(v.tensor_scalar(clip[i][:, :, :], sc[i][:, :, :], SCALE, CLAMP, ALU.mult, ALU.min))
                            slowly(v.tensor_scalar(clip[i][:, :, :], clip[i][:, :, :], -CLAMP, keep[:, 0:1],
                                                   ALU.max, ALU.mult))
                            v.tensor_tensor(clip[i][:, :, :], clip[i][:, :, :], high[i][:, :, :],
                                            ALU.subtract).then_inc(slow_logits, 1)
                        if s % KT == KT - 1:
                            heads_out(b, s // KT)
                    if b < B - 1:
                        for i in range(len(POST)):
                            if i == EARLY:
                                ln_mlp(b)
                                rms_mlp(b)
                            post(b, i)

            dve.wait_ge(flag_done, 1)
            held = dve.value_load(flag[0:1, 0:1], min_val=0, max_val=CHECKS)
            counts = count[0], fill[0], stat_rounds[0]
            with dve.If(held < CHECKS):
                general_attention()
                general = count[0], fill[0], stat_rounds[0]
            with dve.Else():
                count[0], fill[0], stat_rounds[0] = counts
                fast_attention()
                assert general == (count[0], fill[0], stat_rounds[0])
            def places_y():
                dve.wait_ge(scattered, 16 * 2 * T)
                step(v.tensor_scalar(first_row[:, :], first[:, 0:E], float(CHUNK), None, ALU.mult))
                step(v.tensor_tensor(one_hot[:, :, :], iota_e[:, :].unsqueeze(1).to_broadcast([P, 2 * T, E]),
                                     e_all[:, :, :].rearrange("p c t -> p (c t)").unsqueeze(2).to_broadcast([P, 2 * T, E]),
                                     ALU.is_equal))
                settle()
                step(v.tensor_tensor(one_hot[:, :, :], one_hot[:, :, :],
                                     first_row[:, :].unsqueeze(1).to_broadcast([P, 2 * T, E]), ALU.mult))
                settle()
                step(v.tensor_reduce(dest_y[:, :], one_hot[:, :, :], AX.X, ALU.add))
                settle()
                step(v.tensor_tensor(dest_y[:, :], dest_y[:, :], r_all[:, :, :].rearrange("p c t -> p (c t)"), ALU.add))
                settle()
                v.tensor_copy(dest[:, :, :].rearrange("p c t -> p (c t)"), dest_y[:, :]).then_inc(dest_y_done, 1)


            def weights_of_two():
                dve.wait_ge(exp_z, 1)
                step(v.tensor_scalar(s_top[:, :, :], s_top[:, :, :], 1.0, None, ALU.add))
                settle()
                step(v.reciprocal(w_top[:, :, :], s_top[:, :, :]))
                settle()
                step(v.tensor_tensor(s_sum[:, :], w_top[:, :, 0], w_top[:, :, 1], ALU.add))
                settle()
                step(v.tensor_scalar(s_sum[:, :], s_sum[:, :], TOP_EPS, None, ALU.add))
                settle()
                step(v.reciprocal(s_sum[:, :], s_sum[:, :]))
                settle()
                step(v.scalar_tensor_tensor(w_top[:, :, :], w_top[:, :, :], tanh_g[:, 1:2],
                                            s_sum[:, :].unsqueeze(2).to_broadcast([P, T, 2]), ALU.mult, ALU.mult))

            def split_x(i):
                bank = filled()
                if i >= 2:
                    dve.wait_ge(h_done, (i - 1) * HM // 2)
                src = bank[:, :].rearrange("p (k n) -> p k n", k=KD)
                split(xt_p[i % 2][0][:, :, :], xt_p[i % 2][1][:, :, :], src).then_inc(post_read, 1)

            def split_h(i, q):
                f = i * (HM // 2) + q
                dve.wait_ge(relu_done, f + 1)
                hi, lo = (h_p[i % 2][k][:, 2 * q:2 * q + 2, :] for k in range(2))
                if CHUNKS[i][0] == R:
                    last = split(hi, lo, h_f[f % 2][:, :, :])
                else:
                    last = v.tensor_tensor(lo, h_f[f % 2][:, :, :], hi.bitcast(F32), ALU.subtract)
                last.then_inc(h_split, 1)

            def w1_low(s):
                dve.wait_ge(w1_hi, s + 1)
                v.tensor_tensor(w1_p[s % 2][1][:, :, :], w1_raw[s % 2],
                                w1_p[s % 2][0][:, :, :].bitcast(F32), ALU.subtract).then_inc(w1_lo, 1)

            def read_y(i):
                dve.wait_ge(y_done, i + 1)
                y = pv[i % 2][:, :].rearrange("p (t n) -> p t n", t=2)
                chunk, c = CHUNKS[i]
                s = set_of(i)
                dve.wait_ge(biases_in[s % 3], 32 * (s // 3 + 1))
                dve.wait_ge(y_out[i % 2], 16 * stores(i % 2, i))
                b2 = b2_sb[s % 3][:, :].unsqueeze(1).to_broadcast([P, 2, D])
                if chunk == R:
                    v.tensor_tensor(y_sb[i % 2][:, :, :], y, b2, ALU.add).then_inc(y_read, 1)
                else:
                    step(v.tensor_tensor(y_sb[i % 2][:, :, :], y, b2, ALU.add))
                    settle()
                    v.scalar_tensor_tensor(x_sb[:, 2 * c:2 * c + 2, :], y_sb[i % 2][:, :, :], tanh_g[:, 1:2],
                                           x_sb[:, 2 * c:2 * c + 2, :], ALU.mult, ALU.add).then_inc(y_read, 1)
                dve.wait_ge(y_read, i + 1)

            def combine(t):
                dve.wait_ge(gathered[t % 4], 32 * (t // 4 + 1))
                for i in range(2):
                    last = v.scalar_tensor_tensor(x_sb[:, t, :], y_in[t % 4][i][:, :], w_top[:, t, i:i + 1],
                                                  x_sb[:, t, :], ALU.mult, ALU.add)
                    if i == 0:
                        step(last)
                        settle()
                last.then_inc(combined, 1)

            step(v.memset(zero_rows[:, :], 0.0))
            settle()
            split_x(0)
            w1_low(0)
            tiles = 0
            for i in range(len(CHUNKS)):
                s = set_of(i)
                for q in range(HM // 2):
                    at_q = 4 * i + q
                    if at_q == LAST_LN:
                        ln_mlp(B - 1)
                    if at_q == LAST_RMS:
                        rms_mlp(B - 1)
                    for k, when in enumerate(LAST_AT):
                        if when == at_q:
                            post(B - 1, k)
                    if at_q == SLOTS_AT:
                        dve.wait_ge(dest_done, B)
                        slots()
                    if q == TURN_AT and i + 1 < len(CHUNKS):
                        split_x(i + 1)
                    split_h(i, q)
                    if q == 1 and i == last_of(s) and s + 1 < SETS:
                        w1_low(s + 1)
                    if i == AHEAD + 1 and q == 0:
                        weights_of_two()
                    if i == AHEAD + 2 and q == 0:
                        places_y()
                    if at_q in COMBINE_AT:
                        combine(tiles)
                        tiles += 1
                if i >= 1:
                    read_y(i - 1)
            read_y(len(CHUNKS) - 1)
            for t in range(tiles, T):
                combine(t)

        @block.tensor
        def _(pe):
            mm = nc.tensor.matmul

            def product(dst, lhs, rhs, parts=KD):
                todo = [(k, a, b) for k in range(parts) for a, b in PASSES]
                for i, (k, a, b) in enumerate(todo):
                    last = mm(dst, lhs(a, k), rhs(b, k), start=(i == 0), stop=(i == len(todo) - 1))
                return last

            fill = [0]

            def bank():
                fill[0] += 1
                if fill[0] > 2:
                    pe.wait_ge(post_read, fill[0] - 2)
                return mb[(fill[0] - 1) % 2]

            def prep(f):
                n, kind, j = PREP[f]
                dst = prep_bank(f)
                if f >= 8:
                    pe.wait_ge(dve_read, f - 7)
                if kind == TX:
                    pe.wait_ge(xn_done, n + 1)
                    for t in range(QT):
                        last = nc.tensor.transpose(dst[:, t * P:(t + 1) * P],
                                                   normed[:, n * QT + t, j * P:(j + 1) * P], ident[:, :])
                elif kind == TC:
                    k, half = j % 2, j // 2
                    pe.wait_ge(loaded_ctx, 16 * (n + 1))
                    for t in range(4):
                        last = nc.tensor.transpose(dst[0:CH, t * P:(t + 1) * P],
                                                   ctx_raw[:, 4 * half + t, k * CH:(k + 1) * CH], ident[:, :])
                elif kind == Q:
                    pe.wait_ge(dve_read, at(n, TX, KD - 1) + 1)
                    last = product(dst, lambda a, k: wq_p[a][:, k, j * P:(j + 1) * P], lambda a, k: xn_p[a][:, k, :])
                elif kind == K:
                    m, half = j % 2, j // 2
                    pe.wait_ge(dve_read, at(n, TC, 2 * half + 1) + 1)
                    last = product(dst, lambda a, k: wk_p[a][:, k, m * P:(m + 1) * P],
                                   lambda a, k: ctx_p[a][:, k, half * 512:half * 512 + 512])
                elif kind == V:
                    for u in range(2):
                        kt = 2 * j + u
                        last = product(dst[:, u * D:(u + 1) * D],
                                       lambda a, k: ctx_p[a][:, k, kt * P:(kt + 1) * P],
                                       lambda a, k: wv_p[a][:, k, :])
                else:
                    for m, s in enumerate(norm_staged(n, j)):
                        pe.wait_ge(act_read, acts(at(*STAGED[s])))
                        first_col = PH * (KD - 1 - m)
                        last = mm(dst[0:HEADS, :], head_of[:, first_col:first_col + HEADS], stage_s[s % DEEP][:, :],
                                  start=(m == 0), stop=(m == KD - 1))
                last.then_inc(fill_done, 1)

            def post(n, i):
                kind, t = POST[i]
                dst = bank()
                if kind == T1:
                    pe.wait_ge(pv_read, GROUPS * (n + 1))
                    for g in range(GROUPS):
                        last = nc.tensor.transpose(dst[:, g * P:(g + 1) * P], o_t[:, g, t * P:(t + 1) * P], ident[:, :])
                elif kind == T2:
                    pe.wait_ge(post_read, after(n, T1, t))
                    o = on[t % 2][:, :, :].rearrange("p h d -> p (h d)")
                    for k in range(KD):
                        last = nc.tensor.transpose(dst[:, k * P:(k + 1) * P], o[:, k * P:(k + 1) * P], ident[:, :])
                elif kind == T3:
                    pe.wait_ge(post_read, after(n, T2, t))
                    last = product(dst[:, 0:D], lambda a, k: on_p[t % 2][a][:, k, :], lambda a, k: wo_p[a][:, k, :])
                elif kind == T4:
                    pe.wait_ge(normed_done, n + 1)
                    for u in range(2):
                        for k in range(KD):
                            at = (u * KD + k) * P
                            last = nc.tensor.transpose(dst[:, at:at + P],
                                                       normed[:, n * QT + 2 * t + u, k * P:(k + 1) * P], ident[:, :])
                elif kind == T6:
                    pe.wait_ge(masks_done, n + 1)
                    m = mask_s[:, :, :].rearrange("p t e -> p (t e)")
                    mm(dst[:, 0:QT * E], before[:, :], m, start=True, stop=True)
                    last = mm(dst[:, QT * E:2 * QT * E], ones[:, :], m, start=True, stop=True)
                else:
                    pe.wait_ge(post_read, after(n, T4, t))
                    for u in range(2):
                        for k in range(KD):
                            last = mm(dst[:, u * E:(u + 1) * E], n_t[:, u, k, :], rw_t[:, k, :],
                                      start=(k == 0), stop=(k == KD - 1))
                last.then_inc(post_done, 1)

            def score(i, a, g, kt):
                return mm(sc[i][:, a, :], k_stack[0:ROWS, 2 * g + i, kt * P:(kt + 1) * P],
                          q_stack[0:ROWS, 2 * g + i, a, :], start=True, stop=True)

            def slow_at(b, g, i, kt):
                pair = (b * GROUPS + g) * 2 + i
                return 1 + pair * (1 + 5 * KT - 1) + 1 + 5 * (kt - 1) + 1

            def scores(w):
                b, g, kt = w // WS, w % WS // KT, w % KT
                if kt == 0:
                    pe.wait_ge(stack_in[g // 2], STACK * (b + 1))
                for i in range(2):
                    u = 2 * w + i
                    if u >= 2:
                        pe.wait_ge(exp_done, u - 1)
                    for a in range(2):
                        last = score(i, a, g, kt)
                    last.then_inc(scores_done, 1)

            def values(w):
                b, g, kt = w // WS, w % WS // KT, w % KT
                gg = b * GROUPS + g
                if kt == 0 and gg >= 2:
                    pe.wait_ge(pv_read, gg - 1)
                pe.wait_ge(exp_done, 2 * w + 2)
                for j in range(4):
                    last = mm(pv[gg % 2][32 * j:32 * j + DH + 1, :], v_sb[b][:, kt, 4 * g + j, :],
                              prob[w % 2][j // 2][:, j % 2, :], start=(kt == 0), stop=(kt == KT - 1))
                last.then_inc(pv_done, 1)

            pe.wait_ge(ident_set, 1)
            pe.wait_ge(loaded_bias, 80)
            nrows = HM * (E + 1) + 2 * KD
            nc.tensor.transpose(pv[0][:, 0:nrows], bias_rows[0:nrows, :], ident[0:nrows, 0:nrows])
            for k in range(KD):
                last = nc.tensor.transpose(pv[1][:, k * E:(k + 1) * E], rw_rows[:, k * P:(k + 1) * P], ident[0:E, 0:E])
            last.then_inc(b1_read, 1)

            pe.wait_ge(w_split, 4)
            pe.wait_ge(b1_read, 2)
            for f in range(FILLS):
                prep(f)
            pe.wait_ge(consts_set, 1)
            pe.wait_ge(checks_done, 1)
            mm(mb[0][0:1, 0:2], ones[:, 0:1], checks[:, :], start=True, stop=True).then_inc(checks_sum, 1)

            def fast_attention():
                scores(0)
                for b in range(B):
                    for s in range(WS):
                        w = b * WS + s
                        if w + 1 < B * WS:
                            scores(w + 1)
                        values(w)
                        if (i := post_slot(b, s)) is not None:
                            post(b - 1, i)

            def general_attention():
                u = 0
                for b in range(B):
                    for g in range(GROUPS):
                        if b:
                            pe.wait_ge(slow_stack, STACK * ((b - 1) * 2 + g // 2 + 1))
                        else:
                            pe.wait_ge(stack_in[g // 2], STACK)
                        for i in range(2):
                            for kt in range(KT):
                                if kt:
                                    pe.wait_ge(slow_step, slow_at(b, g, i, kt))
                                elif i or g or b:
                                    pe.wait_ge(slow_high, (b * GROUPS + g) * 2 + i)
                                for a in range(2):
                                    last = score(i, a, g, kt)
                                last.then_inc(slow_scores, 1)
                pe.wait_ge(slow_stack, STACK * B * 2)
                pe.wait_ge(slow_keep, 1)
                for b in range(B):
                    for s in range(WS):
                        scores(b * WS + s)
                        values(b * WS + s)
                    if b < B - 1:
                        for i in range(len(POST)):
                            post(b, i)

            pe.wait_ge(flag_done, 1)
            held = pe.value_load(flag[0:1, 0:1], min_val=0, max_val=CHECKS)
            fills = fill[0]
            with pe.If(held < CHECKS):
                general_attention()
            with pe.Else():
                fill[0] = fills
                fast_attention()
            def turn_x(i):
                dst = bank()
                chunk, c = CHUNKS[i]
                if chunk == R:
                    pe.wait_ge(x_in_done[c % 2], 16 * (c // 2 + 1))
                else:
                    pe.wait_ge(normed_done, (2 * c + 1) // QT + 1)
                for k in range(KD):
                    for t in range(2):
                        src = (normed[:, 2 * c + t, k * P:(k + 1) * P] if chunk == S
                               else x_in[c % 2][:, t, k * P:(k + 1) * P])
                        at = (2 * k + t) * P
                        last = nc.tensor.transpose(dst[:, at:at + P], src, ident[:, :])
                last.then_inc(post_done, 1)

            def hidden(i, q):
                s = set_of(i)
                f = i * (HM // 2) + q
                if q == 0:
                    pe.wait_ge(post_read, mb_count((X, i)))
                    pe.wait_ge(w1_lo, s + 1)
                if f >= 4:
                    pe.wait_ge(relu_done, f - 3)
                for r in range(2):
                    m = 2 * q + r
                    last = product(hps(f)[:, r, :], lambda a, k: w1_p[s % 2][a][:, k, m * P:(m + 1) * P],
                                   lambda a, k: xt_p[i % 2][a][:, k, :])
                last.then_inc(h_done, 1)

            def results(i):
                s = set_of(i)
                pe.wait_ge(w2_lo, s + 1)
                pe.wait_ge(h_split, (i + 1) * HM // 2)
                if i >= 2:
                    pe.wait_ge(y_read, i - 1)
                for t in range(2):
                    last = product(pv[i % 2][:, t * D:(t + 1) * D],
                                   lambda a, k: h_p[i % 2][a][:, k, t * P:(t + 1) * P],
                                   lambda a, k: w2_p[s % 2][a][:, k, :], HM)
                last.then_inc(y_done, 1)

            pe.wait_ge(pv_read, B * GROUPS)
            turn_x(0)
            for i in range(len(CHUNKS)):
                for q in range(HM // 2):
                    for k, when in enumerate(LAST_AT):
                        if when == 4 * i + q:
                            post(B - 1, k)
                    if q == TURN_AT and i + 1 < len(CHUNKS):
                        turn_x(i + 1)
                    hidden(i, q)
                if i >= 1:
                    results(i - 1)
            results(len(CHUNKS) - 1)


_INS = ['x', 'ctx_768', 'g_xattn', 'g_ffn', 'L0_xattn_Wq', 'L0_xattn_bq', 'L0_xattn_Wk', 'L0_xattn_bk',
        'L0_xattn_Wv', 'L0_xattn_bv', 'L0_xattn_Wo', 'L0_xattn_bo', 'L0_ffn_norm_weight', 'L0_ffn_router_w',
        'L0_ffn_sw1', 'L0_ffn_sb1', 'L0_ffn_sw2', 'L0_ffn_sb2', 'L0_ffn_ew1', 'L0_ffn_eb1', 'L0_ffn_ew2',
        'L0_ffn_eb2']


def kernel(**inputs):
    import numpy as np
    import concourse.bacc as bacc
    from concourse.bass_utils import run_bass_kernel_spmd

    nc = bacc.Bacc("TRN2", target_bir_lowering=False, num_devices=1)
    arrays, args = {}, []
    for name in _INS:
        a = np.ascontiguousarray(inputs[name])
        arrays[f"in_{name}"] = a
        args.append(nc.dram_tensor(f"in_{name}", a.shape, mybir.dt.from_np(a.dtype), kind="ExternalInput").ap())
    out = nc.dram_tensor("out", inputs["x"].shape, F32, kind="ExternalOutput").ap()
    flamingo_block(nc, *args, out)
    r = run_bass_kernel_spmd(nc, [arrays], core_ids=[0])
    return r.results[0]["out"]
```

```python
from contextlib import ExitStack

import concourse.bass as bass
from concourse import mybir

ALU = mybir.AluOpType
ACT = mybir.ActivationFunctionType
AX = mybir.AxisListType
F32 = mybir.dt.float32
F32R = mybir.dt.float32r
BF16 = mybir.dt.bfloat16
I32 = mybir.dt.int32
U32 = mybir.dt.uint32

P = 128
LN_EPS, RMS_EPS, TOP_EPS = 1e-5, 1e-8, 1e-6
Z_LOW, Z_HIGH = -88.7, 16.635533
CLAMP = 10000.0
LOGIT_SAFE, V_SAFE = 40.0, 1e24
MAIN = 21
AHEAD = 5
COMBINE_E = [14, 15, 16, 17, 18, 19, 20, 21]


def flamingo_block(nc, x, ctx_kv, g_xattn, g_ffn, wq, bq, wk, bk, wv, bv, wo, bo,
                   norm_w, router_w, sw1, sb1, sw2, sb2, ew1, eb1, ew2, eb2, out):
    B, NQ, D = x.shape
    _, NK, CK = ctx_kv.shape
    E, _, H = ew1.shape
    HEADS, DH = 16, 16
    PH = P // DH
    SCALE = float(DH) ** -0.5
    QT = NQ // P
    T = B * QT
    KT = NK // P
    KD = D // P
    CH = CK // 2
    HM = H // P
    GROUPS = HEADS // 4
    CHUNK = 2 * P
    SHARED = B * NQ // CHUNK
    SLOTS = (2 * B * NQ - E) // CHUNK + E
    CAP = B * NQ + CHUNK
    S, R = "shared", "routed"
    CHUNKS = ([(S, c) for c in range(AHEAD)] + [(R, j) for j in range(MAIN)]
              + [(S, c) for c in range(AHEAD, SHARED)])
    LATE = SLOTS - MAIN
    SETS = MAIN + 2

    def set_of(i):
        kind, c = CHUNKS[i]
        return c + 1 if kind == R else 0 if c < AHEAD else SETS - 1

    def last_of(s):
        return max(i for i in range(len(CHUNKS)) if set_of(i) == s)

    PASSES = ((0, 0), (0, 1), (1, 0))
    ROWS = 64 + len(PASSES) * DH
    DEEP = 4

    x_t = x.rearrange("b (t p) d -> b p t d", p=P)
    ctx_t = ctx_kv.rearrange("b (t p) c -> b p t c", p=P)
    out_t = out.rearrange("b (t p) d -> (b t) p d", p=P)

    k_rows = nc.dram_tensor("k_rows", (B, 2, D, NK), F32).ap()
    q_rows = nc.dram_tensor("q_rows", (B, 2, D, NQ), F32).ap()
    slot_x = nc.dram_tensor("slot_x", (E * CAP, D + 1), F32).ap()
    y_tok = nc.dram_tensor("y_tok", (2 * B * NQ + CHUNK, D), F32).ap()
    y_late = nc.dram_tensor("y_late", (2 * B * NQ + CHUNK, D), F32).ap()
    maxima = nc.dram_tensor("maxima", (B, HEADS // 2, P, 2 * NQ), F32).ap()
    b1_cols = nc.dram_tensor("b1_cols", (E + 1, P, HM), F32).ap()

    with ExitStack() as top:
        def sem(name):
            return top.enter_context(nc.semaphore(name))

        def sb(name, shape, dt=F32, scope=top):
            return scope.enter_context(nc.sbuf_tensor(name, shape, dt))

        x_sb = sb("x_sb", [P, T, D])
        normed = sb("normed", [P, T, D + 1])
        wo_p = [sb(f"wo_p{i}", [P, KD, D], F32R) for i in range(2)]
        ident = sb("ident", [P, P])
        before = sb("before", [P, P])
        ones = sb("ones", [P, P])
        bo_bc = sb("bo_bc", [P, D])
        tanh_g = sb("tanh_g", [P, 2])
        g_bc = sb("g_bc", [P, 2])
        rw_t = sb("rw_t", [P, KD, E])
        iota_e = sb("iota_e", [P, E])
        iota_s = sb("iota_s", [P, SLOTS])
        stat6 = sb("stat6", [P, QT, 6])
        mv = sb("mv", [P, 2, QT, 2])
        rs = sb("rs", [P, 2, QT])
        ra = sb("ra", [P, QT])
        rt = sb("rt", [P, QT])
        ms = sb("ms", [P, QT])
        half_neg = sb("half_neg", [P, QT])
        z_all = sb("z_all", [P, T, 2])
        e_all = sb("e_all", [P, 2, T])
        r_all = sb("r_all", [P, 2, T])
        dest = sb("dest", [P, 2, T], U32)
        flag = sb("flag", [1, 1], I32)

        one = ExitStack()
        k_stack = sb("k_stack", [P, HEADS // 2, NK], F32R, one)
        q_stack = sb("q_stack", [P, HEADS // 2, 2, NQ], F32R, one)
        v_sb = [sb(f"v{n}", [P, KT, HEADS, DH + 1], F32, one) for n in range(B)]

        qkv = ExitStack()
        ctx_raw = sb("ctx_raw", [P, KT, CK], F32, qkv)
        ctx_p = [sb(f"ctx_p{i}", [CH, 2, NK], F32R, qkv) for i in range(2)]
        xn_p = [sb(f"xn_p{i}", [P, KD, NQ], F32R, qkv) for i in range(2)]
        wq_p = [sb(f"wq_p{i}", [P, KD, D], F32R, qkv) for i in range(2)]
        wk_p = [sb(f"wk_p{i}", [CH, 2, D], F32R, qkv) for i in range(2)]
        wv_p = [sb(f"wv_p{i}", [CH, 2, D], F32R, qkv) for i in range(2)]
        bv_bc = sb("bv_bc", [P, 2, D], F32, qkv)
        qk_col = sb("qk_col", [P, 2 * KD], F32, qkv)
        bq_col, bk_col = qk_col[:, 0:KD], qk_col[:, KD:2 * KD]
        head_of = sb("head_of", [P, HEADS + PH], F32R, qkv)
        junk = sb("junk", [P, 512], BF16, qkv)
        v_ss = sb("v_ss", [P, B, KT // 2], F32, qkv)
        norm2 = sb("norm2", [HEADS, B, 3], I32, qkv)
        k_max = sb("k_max", [HEADS, B], F32, qkv)
        qk_max = sb("qk_max", [HEADS, B], F32, qkv)
        checks = sb("checks", [P, 2], F32, qkv)
        v_ok = sb("v_ok", [P, B, KT // 2], F32, qkv)

        raw = ExitStack()
        w_raw = sb("w_raw", [P, 4, 512], F32, raw)
        bias_rows = sb("bias_rows", [P, P], F32, raw)
        b1_all = sb("b1_all", [P, E + 1, HM], F32, raw)
        rw_rows = sb("rw_rows", [E, D], F32, raw)
        head_f = sb("head_f", [P, HEADS + PH], F32, raw)
        raw.close()
        stage_s = [sb(f"stage_s{i}", [P, 512], F32R, qkv) for i in range(DEEP)]
        stage_p = [[sb(f"stage_p{i}{j}", [P, 512], F32R, qkv) for j in range(2)] for i in range(DEEP)]
        qkv.close()

        prob = [[sb(f"prob{k}{i}", [P, 2, NQ], F32, one) for i in range(2)] for k in range(2)]
        clip = [sb(f"clip{i}", [P, 2, NQ], F32, one) for i in range(2)]
        high = [sb(f"high{i}", [P, 2, NQ], F32, one) for i in range(2)]
        is_num = sb("is_num", [P, 2, NQ], F32, one)
        keep = sb("keep", [P, 2], F32, one)
        after_at = ExitStack()
        o_t = sb("o_t", [P, GROUPS, NQ], F32, after_at)
        on = [sb(f"on{i}", [P, HEADS, DH], F32, after_at) for i in range(2)]
        on_p = [[sb(f"on_p{i}{j}", [P, KD, P], F32R, after_at) for j in range(2)] for i in range(2)]
        r_sum = sb("r_sum", [P, HEADS], F32, after_at)
        n_t = sb("n_t", [P, QT, KD, P], F32, after_at)
        nw_bc = sb("nw_bc", [P, D], F32, after_at)
        second = sb("second", [P, QT, D + 1], F32, after_at)
        logits = sb("logits", [P, QT, E], F32, after_at)
        z_c = sb("z_c", [P, QT, E], F32, after_at)
        z_top = sb("z_top", [P, QT, 8], F32, after_at)
        e_top = sb("e_top", [P, QT, 8], U32, after_at)
        mask = [sb(f"mask{i}", [P, QT, E], F32, after_at) for i in range(2)]
        mask_s = sb("mask_s", [P, QT, E], F32, after_at)
        upto = sb("upto", [P, QT + 1, E], F32, after_at)
        pos = sb("pos", [P, QT, E], F32, after_at)
        pick = sb("pick", [P, QT, E], F32, after_at)
        dest_f = sb("dest_f", [P, 2, QT], F32, after_at)
        n_i = sb("n_i", [P, E], I32, after_at)
        n_s = sb("n_s", [P, E], I32, after_at)
        n_slots = sb("n_slots", [P, E], F32, after_at)
        scan = sb("scan", [P, E], F32, after_at)
        scan_2 = sb("scan_2", [P, E], F32, after_at)
        reached = sb("reached", [P, SLOTS, E - 1], F32, after_at)
        pad_f = sb("pad_f", [P, E], F32, after_at)
        last_slot = sb("last_slot", [P, 1], F32, after_at)
        slot_n = sb("slot_n", [P, SLOTS], F32, after_at)
        slot_ef = sb("slot_ef", [P, SLOTS], F32, after_at)
        slot_1st = sb("slot_1st", [P, SLOTS], F32, after_at)
        after_at.close()
        one.close()

        two = ExitStack()
        raw_0 = [sb(f"w{i}_raw0", [P, 2048], F32, two) for i in (1, 2)]
        h_p0 = [sb(f"h_p0{j}", [P, HM, CHUNK], F32R, two) for j in range(2)]
        w1_p0 = [sb(f"w1_p0{j}", [P, KD, H], F32R, two) for j in range(2)]
        h_p1 = [sb(f"h_p1{j}", [P, HM, CHUNK], F32R, two) for j in range(2)]
        w2_p0 = [sb(f"w2_p0{j}", [P, HM, D], F32R, two) for j in range(2)]
        xt_p = [[sb(f"xt_p{i}{j}", [P, KD, CHUNK], F32R, two) for j in range(2)] for i in range(2)]
        h_f = [sb(f"h_f{i}", [P, 2, CHUNK], F32, two) for i in range(2)]
        y_sb = [sb(f"y_sb{i}", [P, 2, D], F32, two) for i in range(2)]
        h_p = [h_p0, h_p1]
        set_0 = dict(raw=raw_0, w1=w1_p0, w2=w2_p0)
        b1_sb = [sb(f"b1_sb{i}", [P, HM], F32, two) for i in range(3)]
        b2_sb = [sb(f"b2_sb{i}", [P, D], F32, two) for i in range(3)]
        zero_rows = sb("zero_rows", [P, 2, D + 1], F32, two)
        y_row = [sb(f"y_row{i}", [P, 2], U32, two) for i in range(4)]
        first = sb("first", [P, E + 1], F32, two)
        pad_row = sb("pad_row", [P, E], I32, two)
        slot_e = sb("slot_e", [P, SLOTS], I32, two)
        n_used = sb("n_used", [P, 1], I32, two)
        slot_row = sb("slot_row", [P, SLOTS], I32, two)
        s_top = sb("s_top", [P, T, 2], F32, two)
        s_sum = sb("s_sum", [P, T], F32, two)
        w_top = sb("w_top", [P, T, 2], F32, two)
        x_in = [sb(f"x_in{i}", [P, 2, D + 1], F32, two) for i in range(2)]
        last_1 = ExitStack()
        y_all = [sb(f"y_all{i}", [P, T, D], F32, last_1) for i in range(2)]
        last_1.close()
        set_1 = dict(raw=[sb(f"w{i}_raw1", [P, 2048], F32, two) for i in (1, 2)],
                     w1=[sb(f"w1_p1{j}", [P, KD, H], F32R, two) for j in range(2)],
                     w2=[sb(f"w2_p1{j}", [P, HM, D], F32R, two) for j in range(2)])
        w1_raw = [w["raw"][0][:, :].rearrange("p (k h) -> p k h", k=KD) for w in (set_0, set_1)]
        w2_raw = [w["raw"][1][:, :].rearrange("p (k d) -> p k d", k=HM) for w in (set_0, set_1)]
        w1_p, w2_p = [[w[name] for w in (set_0, set_1)] for name in ("w1", "w2")]
        two.close()

        sc = [top.enter_context(nc.psum_tensor(f"sc{i}", [P, 2, 512], F32)) for i in range(3)]
        pv = top.enter_context(nc.psum_tensor("pv", [P, 512], F32))
        mb = top.enter_context(nc.psum_tensor("mb", [P, 512], F32))

        loaded_x = [sem(f"loaded_x{n}") for n in range(B)]
        loaded_w = sem("loaded_w")
        loaded_bias = sem("loaded_bias")
        loaded_small = sem("loaded_small")
        loaded_nw = sem("loaded_nw")
        loaded_ctx = sem("loaded_ctx")
        ident_set = sem("ident_set")
        heads_set = sem("heads_set")
        consts_set = sem("consts_set")
        zeros_set = sem("zeros_set")
        w_split = sem("w_split")
        tanh_done = sem("tanh_done")
        dve_step = sem("dve_step")
        pool_step = sem("pool_step")
        stats_done = sem("stats_done")
        bo_added = sem("bo_added")
        rstd_done = sem("rstd_done")
        xn_done = sem("xn_done")
        normed_done = sem("normed_done")
        fill_done = sem("fill_done")
        act_read = sem("act_read")
        dve_read = sem("dve_read")
        checks_done = sem("checks_done")
        checks_sum = sem("checks_sum")
        flag_done = sem("flag_done")
        post_done = sem("post_done")
        post_read = sem("post_read")
        slow_stack = sem("slow_stack")
        slow_scores = sem("slow_scores")
        slow_step = sem("slow_step")
        slow_high = sem("slow_high")
        slow_max = sem("slow_max")
        slow_max_out = sem("slow_max_out")
        slow_max_in = [sem(f"slow_max_in{i}") for i in range(2)]
        slow_num = sem("slow_num")
        slow_keep = sem("slow_keep")
        slow_logits = sem("slow_logits")
        stage_out = [sem(f"stage_out{i}") for i in range(DEEP)]
        stack_in = [sem(f"stack_in{h}") for h in range(2)]
        scores_done = sem("scores_done")
        exp_done = sem("exp_done")
        pv_done = sem("pv_done")
        pv_read = sem("pv_read")
        b1_read = sem("b1_read")
        b1_out = sem("b1_out")
        masks_done = sem("masks_done")
        exp_z = sem("exp_z")
        dest_done = sem("dest_done")
        slots_done = sem("slots_done")
        padded = sem("padded")
        scattered = sem("scattered")
        raw1_in = [sem(f"raw1_in{i}") for i in range(2)]
        raw2_in = [sem(f"raw2_in{i}") for i in range(2)]
        biases_in = [sem(f"biases_in{i}") for i in range(3)]
        w1_hi = sem("w1_hi")
        w1_lo = sem("w1_lo")
        w2_hi = sem("w2_hi")
        w2_lo = sem("w2_lo")
        x_in_done = [sem(f"x_in_done{i}") for i in range(2)]
        h_done = sem("h_done")
        relu_done = sem("relu_done")
        h_split = sem("h_split")
        y_done = sem("y_done")
        y_read = sem("y_read")
        y_out = [sem(f"y_out{i}") for i in range(2)]
        gathered = [sem(f"gathered{i}") for i in range(4)]
        combined = sem("combined")
        zeros_out = sem("zeros_out")
        late_zero = sem("late_zero")
        late_in = sem("late_in")
        late_hi = sem("late_hi")
        late_w1 = sem("late_w1")
        late_w2 = sem("late_w2")
        late_turned = sem("late_turned")
        late_x = sem("late_x")
        late_h = sem("late_h")
        late_relu = sem("late_relu")
        late_split = sem("late_split")
        late_y = sem("late_y")
        late_result = sem("late_result")
        late_out = sem("late_out")
        late_back = sem("late_back")
        late_combined = sem("late_combined")
        stored = sem("stored")

        TX, TC, Q, K, V, N = range(6)
        PREP = []
        for n in range(B + 1):
            if n < B:
                PREP += [(n, TC, i) for i in range(4)]
            if n:
                PREP += [(n - 1, Q, m) for m in range(KD)]
            if n < B:
                PREP += [(n, K, i) for i in range(KD)]
            if n:
                PREP += [(n - 1, N, 2)]
            if n < B:
                PREP += [(n, K, 2), (n, K, 3), (n, N, 0), (n, V, 0), (n, V, 1), (n, N, 1),
                         (n, TX, 0), (n, V, 2), (n, TX, 1), (n, V, 3)]
        FILLS = len(PREP)
        LN_AT, STATS_AT = (K, 2), (V, 3)
        STAGED = [(n, kind, j) for n, kind, j in PREP if kind in (Q, K)]
        STAGES = len(STAGED)
        BY_ACT = (TX, TC, Q, K, V)

        def acts(f):
            return sum(kind in BY_ACT for _, kind, _ in PREP[:f + 1])

        def at(n, kind, j):
            return PREP.index((n, kind, j))

        def outs(i, s):
            return 32 * ((s - i + DEEP - 1) // DEEP)

        def stores(i, before_chunk):
            return sum(kind == R for k, (kind, _) in enumerate(CHUNKS) if k % 2 == i and k < before_chunk)

        def prep_bank(f):
            f %= 8
            return sc[f // 2][:, f % 2, :] if f < 6 else pv[:, :] if f == 6 else mb[:, :]

        def norm_staged(n, which):
            return [STAGED.index((n, Q, m) if which == 2 else (n, K, 2 * which + m)) for m in range(KD)]

        def norm_of(s):
            n, kind, j = STAGED[s]
            return at(n, N, 2 if kind == Q else j // 2)

        T1, T2, T3, T4, T5, T6 = range(6)
        POST = ((T1, 0), (T1, 1), (T2, 0), (T1, 2), (T2, 1), (T3, 0), (T1, 3), (T2, 2),
                (T3, 1), (T2, 3), (T3, 2), (T3, 3), (T4, 0), (T4, 1), (T5, 0), (T5, 1), (T6, 0))
        EARLY = 12
        WS = GROUPS * KT
        POST_AT = list(range(EARLY)) + [18, 19, 20, 21, 26]
        NORM_AT = 16

        X, EIGHTHS = "x", 8
        LAST_AT = list(range(EARLY)) + [16,17,18,19,22]
        LAST_NORM, SLOTS_AT = 14, 23
        COMBINE_AT = [EIGHTHS * (AHEAD + MAIN) + k for k in COMBINE_E]
        W1_LOW_AT = 1

        def turn_at(i):
            return 5 if i == AHEAD - 1 else 3

        MB = [(X, 0)]
        for at_e in range(len(CHUNKS) * EIGHTHS):
            MB += [(B - 1, i) for i, when in enumerate(LAST_AT) if when == at_e]
            if at_e % EIGHTHS == turn_at(at_e // EIGHTHS) and at_e // EIGHTHS + 1 < len(CHUNKS):
                MB += [(X, at_e // EIGHTHS + 1)]

        SPLIT_1, SPLIT_2 = B * WS - 10, B * WS - 8
        FIRST_X = (B - 1) * len(POST) + 1

        def mb_bank(k):
            return mb[:, :] if k <= FIRST_X or (k - FIRST_X) % 2 == 0 else sc[2][:, 1, :]

        def result_bank(i):
            return pv[:, :] if i % 2 == 0 else sc[2][:, 0, :]

        def mb_count(what):
            return (B - 1) * len(POST) + MB.index(what) + 1

        STACK = 4 * len(PASSES) * 16

        def post_slot(b, s):
            return POST_AT.index(s) if b > 0 and s in POST_AT else None

        def after(n, kind, t):
            i = POST.index((kind, t))
            return n * len(POST) + i + 1 if n < B - 1 else mb_count((n, i))

        CHECKS = HEADS * B + P * B * KT // 2

        def hps(f):
            return sc[f % 4 // 2][:, f % 2, :].rearrange("p (r n) -> p r n", r=2)

        block = top.enter_context(nc.Block())

        @block.sync
        def _(sp):
            def load(dst, src, done):
                sp.dma_start(dst, src).then_inc(done, 16)

            load(ctx_raw[:, :, :], ctx_t[0], loaded_ctx)
            load(w_raw[0:CH, 1, :].rearrange("p (k n) -> p k n", k=2), wk.rearrange("(k p) n -> p k n", p=CH), loaded_w)
            load(w_raw[0:CH, 2, :].rearrange("p (k n) -> p k n", k=2), wv.rearrange("(k p) n -> p k n", p=CH), loaded_w)
            load(x_sb[:, 0:QT, :], x_t[0], loaded_x[0])
            load(w_raw[:, 0, :].rearrange("p (k n) -> p k n", k=KD), wq.rearrange("(k p) n -> p k n", p=P), loaded_w)
            load(w_raw[:, 3, :].rearrange("p (k n) -> p k n", k=KD), wo.rearrange("(k p) n -> p k n", p=P), loaded_w)
            for n in range(1, B):
                load(x_sb[:, n * QT:(n + 1) * QT, :], x_t[n], loaded_x[n])

            def write_rows(s):
                n, kind, j = STAGED[s]
                m, half = (j, 0) if kind == Q else (j % 2, j // 2)
                rows = (q_rows if kind == Q else k_rows)[n]
                for part in range(2):
                    if part == 0:
                        sp.wait_ge(act_read, acts(at(*STAGED[s])))
                    else:
                        sp.wait_ge(dve_read, at(*STAGED[s]) + 1)
                    sp.dma_start(rows[part, m * P:(m + 1) * P, half * 512:half * 512 + 512],
                                 stage_p[s % DEEP][part][:, :].bitcast(F32)).then_inc(stage_out[s % DEEP], 16)

            def stack_loads(n, h, done):
                pairs = slice(4 * h, 4 * h + 4)
                return [(stack[64 * a + DH * blk:64 * a + DH * blk + DH, pairs, :].bitcast(F32),
                         rows[n, part].rearrange("(pair a d) n -> a d pair n", a=2, d=DH)[a, :, pairs, :], done)
                        for blk, parts in enumerate(((0, 0), (0, 1), (1, 0))) for a in range(2)
                        for rows, stack, part in ((k_rows, k_stack, parts[0]), (q_rows, q_stack[:, :, a], parts[1]))]

            def load_stacks(n, h, done):
                for dst, src, done in stack_loads(n, h, done):
                    load(dst, src, done)

            def next_stacks(n, h):
                sp.wait_ge(scores_done, 2 * KT * ((n - 1) * GROUPS + 2 * h + 2))
                load_stacks(n, h, stack_in[h])

            written = max(norm_staged(0, 2)) + 1
            first = stack_loads(0, 0, stack_in[0]) + stack_loads(0, 1, stack_in[1])
            for s in range(STAGES):
                write_rows(s)
                if s == written + 1:
                    for i in range(DEEP):
                        sp.wait_ge(stage_out[i], outs(i, written))
                    sp.wait_ge(zeros_set, 1)
                if s > written:
                    for _ in range(min(2, len(first))):
                        load(*first.pop(0))
            for one_load in first:
                load(*one_load)
            for i in range(DEEP):
                sp.wait_ge(stage_out[i], outs(i, STAGES))
            sp.wait_ge(flag_done, 1)
            load(nw_bc[:, :], norm_w.rearrange("(a n) -> a n", a=1).to_broadcast([P, D]), loaded_nw)
            held = sp.value_load(flag[0:1, 0:1], min_val=0, max_val=CHECKS)
            with sp.If(held < CHECKS):
                pair = 0
                for n in range(B):
                    for g in range(GROUPS):
                        if n >= 1 and g % 2 == 0:
                            sp.wait_ge(slow_scores, 2 * KT * ((n - 1) * GROUPS + g + 2))
                            load_stacks(n, g // 2, slow_stack)
                        for i in range(2):
                            pair += 1
                            sp.wait_ge(slow_max, pair)
                            sp.dma_start(maxima[n, 2 * g + i], high[i][:, :, :].rearrange("p a n -> p (a n)")
                                         ).then_inc(slow_max_out, 16)
                            sp.wait_ge(slow_max_out, 16 * pair)
                for h in range(2):
                    load_stacks(0, h, slow_stack)
                for n in range(B):
                    for g in range(GROUPS):
                        for i in range(2):
                            if n or g:
                                sp.wait_ge(slow_logits, 2 * KT * (n * GROUPS + g))
                            sp.dma_start(high[i][:, :, :].rearrange("p a n -> p (a n)"),
                                         maxima[n, 2 * g + i]).then_inc(slow_max_in[i], 16)
                        if n + 1 < B and g % 2:
                            next_stacks(n + 1, g // 2)
            with sp.Else():
                for n in range(1, B):
                    for h in range(2):
                        next_stacks(n, h)

            def load_w1(s):
                m1 = sw1
                if 0 < s < SETS - 1:
                    e = sp.value_load(slot_e[0:1, s - 1:s], min_val=0, max_val=E - 1)
                    m1 = ew1[bass.ds(e, 1)].rearrange("e d h -> (e d) h")
                if s >= 2:
                    sp.wait_ge(w1_hi, s - 1)
                    sp.wait_ge(w1_lo, s - 1)
                sp.dma_start(w1_raw[s % 2], m1.rearrange("(k p) h -> p k h", p=P)).then_inc(raw1_in[s % 2], 16)

            def load_w2(s):
                m2 = sw2
                if 0 < s < SETS - 1:
                    e = sp.value_load(slot_e[0:1, s - 1:s], min_val=0, max_val=E - 1)
                    m2 = ew2[bass.ds(e, 1)].rearrange("e h d -> (e h) d")
                if s >= 2:
                    sp.wait_ge(w2_hi, s - 1)
                    sp.wait_ge(w2_lo, s - 1)
                sp.dma_start(w2_raw[s % 2], m2.rearrange("(k p) d -> p k d", p=P)).then_inc(raw2_in[s % 2], 16)

            def load_biases(s):
                c1, c2 = b1_cols[0], sb2.rearrange("(a n) -> a n", a=1)
                if 0 < s < SETS - 1:
                    e = sp.value_load(slot_e[0:1, s - 1:s], min_val=0, max_val=E - 1)
                    c1 = b1_cols[1:E + 1][bass.ds(e, 1)].rearrange("e p m -> (e p) m")
                    c2 = eb2[bass.ds(e, 1), :]
                if s >= 3:
                    sp.wait_ge(relu_done, HM // 2 * (last_of(s - 3) + 1))
                    sp.wait_ge(y_read, last_of(s - 3) + 1)
                sp.dma_start(b1_sb[s % 3][:, :], c1).then_inc(biases_in[s % 3], 16)
                sp.dma_start(b2_sb[s % 3][:, :], c2.to_broadcast([P, D])).then_inc(biases_in[s % 3], 16)

            def load_slot(j):
                row = sp.value_load(slot_row[0:1, j:j + 1], min_val=0, max_val=E * CAP - CHUNK)
                if j >= 2:
                    sp.wait_ge(post_read, mb_count((X, CHUNKS.index((R, j - 2)))))
                sp.dma_start(x_in[j % 2][:, :, :],
                             slot_x[bass.ds(row, CHUNK), :].rearrange("(t p) d -> p t d", p=P)
                             ).then_inc(x_in_done[j % 2], 16)

            sp.wait_ge(scores_done, 2 * KT * (B * GROUPS - 2))
            load_w1(0)
            load_w2(0)
            sp.wait_ge(pv_done, B * WS)
            sp.wait_ge(b1_out, 16)
            load_biases(0)
            sp.wait_ge(slots_done, 1)
            load_w1(1)
            for e in range(E):
                row = sp.value_load(pad_row[0:1, e:e + 1], min_val=0, max_val=E * CAP - CHUNK)
                sp.dma_start(slot_x[bass.ds(row, CHUNK), :].rearrange("(t p) d -> p t d", p=P),
                             zero_rows[:, :, :]).then_inc(padded, 16)
            load_biases(1)
            sp.wait_ge(scattered, 16 * 2 * T)
            sp.wait_ge(padded, 16 * E)
            load_slot(0)
            load_w2(1)
            load_slot(1)
            for j in range(MAIN):
                load_w1(j + 2)
                load_biases(j + 2)
                load_w2(j + 2)
                if j + 2 < MAIN:
                    load_slot(j + 2)
            for i in range(2):
                sp.wait_ge(y_out[i], 32 * stores(i, len(CHUNKS)))
            for k in range(4):
                for c in range(2):
                    sp.dma_start(y_all[c][:, 4 * k:4 * k + 4, :],
                                 y_tok[c * B * NQ:(c + 1) * B * NQ].rearrange("(t p) d -> p t d", p=P)[:, 4 * k:4 * k + 4, :]
                                 ).then_inc(gathered[k], 16)
            used = sp.value_load(n_used[0:1, 0:1], min_val=0, max_val=SLOTS)
            with sp.If(used > MAIN):
                sp.wait_ge(y_read, len(CHUNKS))
                for k in range(LATE):
                    j = MAIN + k
                    if k:
                        sp.wait_ge(late_out, 32 * k)
                    e = sp.value_load(slot_e[0:1, j:j + 1], min_val=0, max_val=E - 1)
                    row = sp.value_load(slot_row[0:1, j:j + 1], min_val=0, max_val=E * CAP - CHUNK)
                    load(w1_raw[0], ew1[bass.ds(e, 1)].rearrange("e d h -> (e d) h").rearrange("(k p) h -> p k h", p=P), late_in)
                    load(w2_raw[0], ew2[bass.ds(e, 1)].rearrange("e h d -> (e h) d").rearrange("(k p) d -> p k d", p=P), late_in)
                    load(b1_sb[0][:, :], b1_cols[1:E + 1][bass.ds(e, 1)].rearrange("e p m -> (e p) m"), late_in)
                    load(b2_sb[0][:, :], eb2[bass.ds(e, 1), :].to_broadcast([P, D]), late_in)
                    load(x_in[0][:, :, :], slot_x[bass.ds(row, CHUNK), :].rearrange("(t p) d -> p t d", p=P), late_in)
                sp.wait_ge(late_out, 32 * LATE)
                sp.wait_ge(combined, T)
                for c in range(2):
                    load(y_all[c][:, :, :], y_late[c * B * NQ:(c + 1) * B * NQ].rearrange("(t p) d -> p t d", p=P), late_back)
                for t in range(T):
                    sp.wait_ge(late_combined, t + 1)
                    load(out_t[t], x_sb[:, t, :], stored)
            with sp.Else():
                for t in range(T):
                    sp.wait_ge(combined, t + 1)
                    if t >= 2 * AHEAD:
                        sp.wait_ge(y_read, AHEAD + MAIN + (t // 2 - AHEAD) + 1)
                    sp.dma_start(out_t[t], x_sb[:, t, :]).then_inc(stored, 16)
            sp.wait_ge(stored, 16 * T)

        @block.gpsimd
        def _(pool):
            count = [0]

            def step(ins):
                count[0] += 1
                ins.then_inc(pool_step, 1)
                pool.wait_ge(pool_step, count[0])

            def rsqrt(which, src, eps):
                step(nc.gpsimd.tensor_scalar(ra[:, :], src, eps, None, ALU.add))
                step(nc.gpsimd.tensor_tensor(rs[:, which, :], ra[:, :], half_neg[:, :], ALU.pow))
                step(nc.gpsimd.tensor_tensor(rt[:, :], rs[:, which, :], rs[:, which, :], ALU.mult))
                step(nc.gpsimd.tensor_tensor(rt[:, :], rt[:, :], ra[:, :], ALU.mult))
                step(nc.gpsimd.tensor_scalar(rt[:, :], rt[:, :], -0.5, 1.5, ALU.mult, ALU.add))
                return nc.gpsimd.tensor_tensor(rs[:, which, :], rs[:, which, :], rt[:, :], ALU.mult)

            rounds = [0]

            def wait_stats():
                rounds[0] += 1
                pool.wait_ge(stats_done, rounds[0])

            def norm_x(n):
                wait_stats()
                rsqrt(0, mv[:, 0, :, 1], LN_EPS).then_inc(rstd_done, 1)
                pool.wait_ge(rstd_done, rounds[0])

            def norm_mlp(n):
                wait_stats()
                var = mv[:, 1, :, 1]
                step(nc.gpsimd.tensor_scalar(ms[:, :], var, LN_EPS, RMS_EPS, ALU.add, ALU.mult))
                step(nc.gpsimd.tensor_tensor(ms[:, :], ms[:, :], var, ALU.add))
                rsqrt(1, ms[:, :], 0.0).then_inc(rstd_done, 1)
                pool.wait_ge(rstd_done, rounds[0])

            step(nc.gpsimd.memset(ident[:, :], 0.0))
            nc.gpsimd.affine_select(out=ident[:, :], in_=ident[:, :], compare_op=ALU.not_equal,
                                    fill=1.0, base=0, pattern=[[-1, P]], channel_multiplier=1).then_inc(ident_set, 1)
            step(nc.gpsimd.memset(half_neg[:, :], -0.5))
            step(nc.gpsimd.memset(head_f[:, :], 1.0))
            step(nc.gpsimd.affine_select(out=head_f[:, :], in_=head_f[:, :], compare_op=ALU.is_ge,
                                         fill=0.0, base=PH * DH, pattern=[[-DH, HEADS + PH]], channel_multiplier=1))
            step(nc.gpsimd.affine_select(out=head_f[:, :], in_=head_f[:, :], compare_op=ALU.is_ge,
                                         fill=0.0, base=DH - 1 - PH * DH, pattern=[[DH, HEADS + PH]],
                                         channel_multiplier=-1))
            nc.gpsimd.tensor_copy(head_of[:, :], head_f[:, :]).then_inc(heads_set, 1)
            pool.wait_ge(heads_set, 1)
            step(nc.gpsimd.memset(k_stack[32:64, :, :].bitcast(F32), 0.0))
            step(nc.gpsimd.memset(q_stack[0:64, :, 1, :].bitcast(F32), 0.0))
            norm_x(0)
            step(nc.gpsimd.memset(q_stack[32:64, :, 0, :].bitcast(F32), 0.0))
            nc.gpsimd.memset(q_stack[64:P, :, 0, :].bitcast(F32), 0.0).then_inc(zeros_set, 1)
            pool.wait_ge(zeros_set, 1)
            step(nc.gpsimd.memset(before[:, :], 1.0))
            step(nc.gpsimd.affine_select(out=before[:, :], in_=before[:, :], compare_op=ALU.is_gt,
                                         fill=0.0, base=0, pattern=[[1, P]], channel_multiplier=-1))
            step(nc.gpsimd.memset(ones[:, :], 1.0))
            step(nc.gpsimd.iota(iota_e[:, :], pattern=[[1, E]], base=0, channel_multiplier=0,
                                allow_small_or_imprecise_dtypes=True))
            step(nc.gpsimd.iota(iota_s[:, :], pattern=[[1, SLOTS]], base=0, channel_multiplier=0,
                                allow_small_or_imprecise_dtypes=True))
            step(nc.gpsimd.iota(normed[:, :, D].bitcast(I32), pattern=[[P, T]], base=0, channel_multiplier=1))
            for v in v_sb:
                step(nc.gpsimd.memset(v[:, :, :, DH:DH + 1], 1.0))
            pool.nop().then_inc(consts_set, 1)
            for n in range(1, B):
                norm_x(n)

            pool.wait_ge(tanh_done, 1)
            step(nc.gpsimd.tensor_scalar(bo_bc[:, :], bo_bc[:, :], tanh_g[:, 0:1], None, ALU.mult))
            for n in range(B):
                pool.wait_ge(xn_done, n + 1)
                at_rows = x_sb[:, n * QT:(n + 1) * QT, :]
                nc.gpsimd.tensor_tensor(at_rows, at_rows, bo_bc[:, :].unsqueeze(1).to_broadcast([P, QT, D]),
                                        ALU.add).then_inc(bo_added, 1)
            pool.wait_ge(flag_done, 1)
            for k in range(2 * B * NQ // 1024):
                pool.dma_start(y_tok[1024 * k:1024 * (k + 1), :].rearrange("(p g r) d -> p g (r d)", p=64, g=HEADS // 2),
                               q_stack[64:P, :, 0, :].bitcast(F32)).then_inc(zeros_out, 16)
            held = pool.value_load(flag[0:1, 0:1], min_val=0, max_val=CHECKS)
            with pool.If(held < CHECKS):
                for pair in range(B * GROUPS * 2):
                    pool.wait_ge(slow_high, pair + 1)
                    both = high[pair % 2][:, :, :].rearrange("p a n -> p (a n)")
                    nc.gpsimd.partition_all_reduce(both, both, P, bass.bass_isa.ReduceOp.max).then_inc(slow_max, 1)
                pool.wait_ge(slow_num, 1)
                nc.gpsimd.partition_all_reduce(keep[:, 1:2], keep[:, 0:1], P,
                                               bass.bass_isa.ReduceOp.max).then_inc(slow_keep, 1)
            with pool.Else():
                pass

            def w2_low(s):
                pool.wait_ge(w2_hi, s + 1)
                if s >= 2:
                    pool.wait_ge(y_done, last_of(s - 2) + 1)
                nc.gpsimd.tensor_tensor(w2_p[s % 2][1][:, :, :], w2_raw[s % 2],
                                        w2_p[s % 2][0][:, :, :].bitcast(F32), ALU.subtract).then_inc(w2_lo, 1)

            def scatter_y(i):
                pool.wait_ge(y_read, i + 1)
                if i == AHEAD:
                    pool.wait_ge(zeros_out, 16 * (2 * B * NQ // 1024))
                if i > AHEAD:
                    pool.wait_ge(y_out[(i - 1) % 2], 32 * stores((i - 1) % 2, i))
                for t in range(2):
                    pool.indirect_dma_start(out=y_tok, out_offset=bass.IndirectOffsetOnAxis(ap=y_row[i % 4][:, t:t + 1], axis=0),
                                            in_=y_sb[i % 2][:, t, :], in_offset=None).then_inc(y_out[i % 2], 16)

            for n in range(B):
                norm_mlp(n)
                if n == B - 2:
                    w2_low(0)
                pool.wait_ge(dest_done, n + 1)
                for t in range(n * QT, (n + 1) * QT):
                    for c in range(2):
                        pool.indirect_dma_start(out=slot_x, out_offset=bass.IndirectOffsetOnAxis(ap=dest[:, c, t:t + 1], axis=0),
                                                in_=normed[:, t, :] if c == 0 else second[:, t - n * QT, :],
                                                in_offset=None).then_inc(scattered, 16)
            for s in range(1, SETS):
                i = AHEAD + s - 3
                if i >= AHEAD:
                    scatter_y(i)
                w2_low(s)
            scatter_y(AHEAD + MAIN - 1)

            used = pool.value_load(n_used[0:1, 0:1], min_val=0, max_val=SLOTS)
            with pool.If(used > MAIN):
                zeros = h_p[1][0][:, :, :].bitcast(F32)
                pool.wait_ge(y_read, len(CHUNKS))
                step(nc.gpsimd.memset(zeros, 0.0))
                for k in range(2 * B * NQ // 1024):
                    pool.dma_start(y_late[1024 * k:1024 * (k + 1), :].rearrange("(p r) d -> p r d", p=P),
                                   zeros).then_inc(late_zero, 16)
                pool.dma_start(y_late[2 * B * NQ:, :].rearrange("(p r) d -> p r d", p=P),
                               zeros[:, 0:2, :]).then_inc(late_zero, 16)
                pool.wait_ge(late_zero, 16 * (2 * B * NQ // 1024 + 1))
                for k in range(LATE):
                    pool.wait_ge(late_hi, 2 * (k + 1))
                    nc.gpsimd.tensor_tensor(w2_p[0][1][:, :, :], w2_raw[0], w2_p[0][0][:, :, :].bitcast(F32),
                                            ALU.subtract).then_inc(late_w2, 1)
                    pool.wait_ge(late_result, k + 1)
                    for t in range(2):
                        pool.indirect_dma_start(out=y_late, out_offset=bass.IndirectOffsetOnAxis(ap=y_row[0][:, t:t + 1], axis=0),
                                                in_=y_sb[0][:, t, :], in_offset=None).then_inc(late_out, 16)
                    pool.wait_ge(late_out, 32 * (k + 1))
            with pool.Else():
                pass

        @block.scalar
        def _(act):
            def row(v):
                return v.rearrange("(a n) -> a n", a=1).to_broadcast([P, v.shape[0]])

            nb = HM * (E + 1)
            for dst, src in ((bias_rows[nb:nb + KD, :], bq.rearrange("(k p) -> k p", p=P)),
                             (bias_rows[nb + KD:nb + 2 * KD, :], bk.rearrange("(k p) -> k p", p=P)),
                             (bias_rows[0:HM, :], sb1.rearrange("(m p) -> m p", p=P)),
                             (bias_rows[HM:nb, :], eb1.rearrange("e (m p) -> (e m) p", p=P)),
                             (rw_rows[:, :], router_w)):
                act.dma_start(dst, src).then_inc(loaded_bias, 16)
            for dst, src in ((bv_bc[:, 0, :], row(bv)), (bv_bc[:, 1, :], row(bv)), (bo_bc[:, :], row(bo)),
                             (g_bc[:, 0:1], row(g_xattn)), (g_bc[:, 1:2], row(g_ffn))):
                act.dma_start(dst, src).then_inc(loaded_small, 16)
            act.wait_ge(b1_read, 2)
            act.dma_start(b1_cols.rearrange("s p m -> p s m"), b1_all[:, :, :]).then_inc(b1_out, 16)
            s = 0
            for f, (n, kind, j) in enumerate(PREP):
                if kind == N:
                    continue
                act.wait_ge(fill_done, f + 1)
                bank = prep_bank(f)
                if kind == TX:
                    last = nc.scalar.activation(xn_p[0][:, j, :], bank, ACT.Copy)
                elif kind == TC:
                    k, half = j % 2, j // 2
                    last = nc.scalar.activation(ctx_p[0][:, k, half * 512:half * 512 + 512],
                                                bank[0:CH, :], ACT.Copy)
                elif kind == V:
                    act.wait_ge(act_read, acts(f) - 1)
                    last = nc.scalar.activation(junk[:, :], bank, ACT.Square, accum_out=v_ss[:, n, j:j + 1])
                else:
                    bias = bq_col[:, j:j + 1] if kind == Q else bk_col[:, j % 2:j % 2 + 1]
                    if s == 0:
                        act.wait_ge(b1_out, 16)
                        act.wait_ge(heads_set, 1)
                        act.wait_ge(w_split, 4)
                    if s >= DEEP:
                        act.wait_ge(fill_done, norm_of(s - DEEP) + 1)
                        act.wait_ge(stage_out[s % DEEP], outs(s % DEEP, s))
                    nc.scalar.activation(stage_s[s % DEEP][:, :], bank, ACT.Square, bias=bias)
                    last = nc.scalar.activation(stage_p[s % DEEP][0][:, :], bank, ACT.Identity, bias=bias)
                    s += 1
                last.then_inc(act_read, 1)
                if (kind, j) == (TC, 3) and n + 1 < B:
                    act.dma_start(ctx_raw[:, :, :], ctx_t[n + 1]).then_inc(loaded_ctx, 16)
            act.wait_ge(loaded_small, 16 * 5)
            nc.scalar.activation(tanh_g[:, :], g_bc[:, :], ACT.Tanh).then_inc(tanh_done, 1)

            def w1_high(s):
                act.wait_ge(raw1_in[s % 2], 16 * (s // 2 + 1))
                if s >= 2:
                    act.wait_ge(h_done, HM // 2 * (last_of(s - 2) + 1))
                nc.scalar.activation(w1_p[s % 2][0][:, :, :], w1_raw[s % 2], ACT.Copy).then_inc(w1_hi, 1)

            def w2_high(s):
                act.wait_ge(raw2_in[s % 2], 16 * (s // 2 + 1))
                if s >= 2:
                    act.wait_ge(y_done, last_of(s - 2) + 1)
                nc.scalar.activation(w2_p[s % 2][0][:, :, :], w2_raw[s % 2], ACT.Copy).then_inc(w2_hi, 1)

            def exponentials(ready):
                for u in range(2 * B * WS):
                    w = u // 2
                    if u == 2 * SPLIT_1:
                        act.wait_ge(zeros_out, 16 * (2 * B * NQ // 1024))
                    if ready is scores_done and u == 2 * SPLIT_1:
                        w1_high(0)
                    if ready is scores_done and u == 2 * SPLIT_2:
                        w2_high(0)
                    act.wait_ge(ready, u + 1)
                    if w >= 2:
                        act.wait_ge(pv_done, w - 1)
                    if ready is scores_done:
                        nc.scalar.activation(prob[w % 2][u % 2][:, :, :], sc[u % 3][:, :, :], ACT.Exp,
                                             scale=SCALE).then_inc(exp_done, 1)
                    else:
                        nc.scalar.activation(prob[w % 2][u % 2][:, :, :], clip[u % 2][:, :, :],
                                             ACT.Exp).then_inc(exp_done, 1)
                if ready is slow_logits:
                    w1_high(0)
                    w2_high(0)

            act.wait_ge(flag_done, 1)
            held = act.value_load(flag[0:1, 0:1], min_val=0, max_val=CHECKS)
            with act.If(held < CHECKS):
                exponentials(slow_logits)
            with act.Else():
                exponentials(scores_done)

            for i, (chunk, c) in enumerate(CHUNKS):
                s = set_of(i)
                act.wait_ge(biases_in[s % 3], 32 * (s // 3 + 1))
                for q in range(HM // 2):
                    f = i * (HM // 2) + q
                    act.wait_ge(h_done, f + 1)
                    if f >= 2:
                        act.wait_ge(h_split, f - 1)
                    for m in (2 * q, 2 * q + 1):
                        last = nc.scalar.activation(h_f[f % 2][:, m % 2, :], hps(f)[:, m % 2, :], ACT.Relu,
                                                    bias=b1_sb[s % 3][:, m:m + 1])
                    if chunk == S:
                        for m in (2 * q, 2 * q + 1):
                            last = nc.scalar.activation(h_p[i % 2][0][:, m, :], hps(f)[:, m % 2, :], ACT.Relu,
                                                        bias=b1_sb[s % 3][:, m:m + 1])
                    last.then_inc(relu_done, 1)
                    if q == (3 if s == 0 else 1) and i == last_of(s) and s + 1 < SETS:
                        w1_high(s + 1)
                    if q == 2 and s > 0 and set_of(i - 1) != s:
                        w2_high(s)
                    if q == 3 and i == AHEAD:
                        act.wait_ge(dest_done, B)
                        nc.scalar.activation(s_top[:, :, :], z_all[:, :, :], ACT.Exp, scale=-1.0).then_inc(exp_z, 1)

            used = act.value_load(n_used[0:1, 0:1], min_val=0, max_val=SLOTS)
            with act.If(used > MAIN):
                for k in range(LATE):
                    act.wait_ge(late_in, 80 * (k + 1))
                    for part, raw in ((w1_p[0][0], w1_raw[0]), (w2_p[0][0], w2_raw[0])):
                        nc.scalar.activation(part[:, :, :], raw, ACT.Copy).then_inc(late_hi, 1)
                    for q in range(HM // 2):
                        act.wait_ge(late_h, 4 * k + q + 1)
                        if q >= 2:
                            act.wait_ge(late_split, 4 * k + q - 1)
                        for m in (2 * q, 2 * q + 1):
                            last = nc.scalar.activation(h_f[q % 2][:, m % 2, :], hps(q)[:, m % 2, :], ACT.Relu,
                                                        bias=b1_sb[0][:, m:m + 1])
                        last.then_inc(late_relu, 1)
            with act.Else():
                pass

        @block.vector
        def _(dve):
            v = nc.vector
            count = [0]

            def step(ins):
                count[0] += 1
                ins.then_inc(dve_step, 1)
                return count[0]

            def settle():
                dve.wait_ge(dve_step, count[0])

            def split(hi, lo, src):
                step(v.tensor_copy(hi, src))
                settle()
                return v.tensor_tensor(lo, src, hi.bitcast(F32), ALU.subtract)

            fill = [0]

            def filled():
                if fill[0]:
                    dve.wait_ge(post_read, fill[0])
                fill[0] += 1
                dve.wait_ge(post_done, fill[0])
                return mb_bank(fill[0])

            def stats(which, tile, t):
                step(v.bn_stats(stat6[:, t, :], x_sb[:, tile, :]))
                settle()
                return v.bn_aggr(mv[:, which, t, :], stat6[:, t, :])

            stat_rounds = [0]

            def ln_x_stats(n):
                dve.wait_ge(loaded_x[n], 16)
                for t in range(QT):
                    last = stats(0, n * QT + t, t)
                    if t < QT - 1:
                        step(last)
                last.then_inc(stats_done, 1)
                stat_rounds[0] += 1

            def ln_x(n):
                dve.wait_ge(rstd_done, stat_rounds[0])
                for t in range(QT):
                    last = v.tensor_scalar(normed[:, n * QT + t, 0:D], x_sb[:, n * QT + t, :], mv[:, 0, t, 0:1],
                                           rs[:, 0, t:t + 1], ALU.subtract, ALU.mult)
                    if t < QT - 1:
                        step(last)
                last.then_inc(xn_done, 1)

            def prep(f):
                n, kind, j = PREP[f]
                bank = prep_bank(f)
                if kind == N:
                    dve.wait_ge(fill_done, f + 1)
                else:
                    dve.wait_ge(act_read, acts(f))
                if kind == TX:
                    last = v.tensor_tensor(xn_p[1][:, j, :], bank, xn_p[0][:, j, :].bitcast(F32), ALU.subtract)
                elif kind == TC:
                    k, cols = j % 2, slice(j // 2 * 512, j // 2 * 512 + 512)
                    last = v.tensor_tensor(ctx_p[1][:, k, cols], bank[0:CH, :], ctx_p[0][:, k, cols].bitcast(F32),
                                           ALU.subtract)
                elif kind == N:
                    last = v.tensor_reduce(norm2[:, n, j:j + 1], bank[0:HEADS, :].bitcast(I32), AX.X,
                                           ALU.max)
                elif kind == V:
                    last = v.tensor_tensor(v_sb[n][:, 2 * j:2 * j + 2, :, 0:DH].rearrange("p t h d -> p (t h) d"),
                                           bank.rearrange("p (h d) -> p h d", d=DH),
                                           bv_bc[:, :, :].rearrange("p t (h d) -> p (t h) d", d=DH), ALU.add)
                else:
                    s = STAGED.index((n, kind, j))
                    if s >= DEEP:
                        dve.wait_ge(stage_out[s % DEEP], outs(s % DEEP, s))
                    bias = bq_col[:, j:j + 1] if kind == Q else bk_col[:, j % 2:j % 2 + 1]
                    last = v.scalar_tensor_tensor(stage_p[s % DEEP][1][:, :], bank, bias,
                                                  stage_p[s % DEEP][0][:, :].bitcast(F32), ALU.add, ALU.subtract)
                last.then_inc(dve_read, 1)

            def check_v():
                step(v.memset(checks[:, :], 0.0))
                dve.wait_ge(act_read, acts(FILLS - 1))
                step(v.tensor_scalar(v_ok[:, :, :], v_ss[:, :, :], V_SAFE, None, ALU.is_le))
                settle()
                step(v.tensor_reduce(checks[:, 1:2], v_ok[:, :, :], AX.XY, ALU.add))

            def check_qk():
                dve.wait_ge(dve_read, FILLS)
                step(v.tensor_tensor(k_max[:, :].bitcast(I32), norm2[:, :, 0], norm2[:, :, 1], ALU.max))
                settle()
                step(v.tensor_tensor(qk_max[:, :], k_max[:, :], norm2[:, :, 2].bitcast(F32), ALU.mult))
                settle()
                step(v.tensor_scalar(qk_max[:, :], qk_max[:, :], (LOGIT_SAFE / SCALE) ** 2, None, ALU.is_le))
                settle()
                v.tensor_reduce(checks[0:HEADS, 0:1], qk_max[:, :], AX.X, ALU.add).then_inc(checks_done, 1)
                step(v.memset(pv[:, :], 0.0))
                dve.wait_ge(checks_sum, 1)
                v.tensor_reduce(checks[0:1, 0:1], mb[0:1, 0:2], AX.X, ALU.add).then_inc(checks_done, 1)
                dve.wait_ge(checks_done, 2)
                for i in range(DEEP):
                    dve.wait_ge(stage_out[i], outs(i, STAGES))
                v.tensor_copy(flag[:, :], checks[0:1, 0:1]).then_inc(flag_done, 1)

            def post(n, i):
                kind, t = POST[i]
                bank = filled()
                tile = n * QT + t
                if kind == T1:
                    o4 = bank[:, :].rearrange("p (h c) -> p h c", h=HEADS)
                    step(v.reciprocal(r_sum[:, :], o4[:, :, DH]))
                    settle()
                    v.tensor_tensor(on[t % 2][:, :, :], o4[:, :, 0:DH],
                                    r_sum[:, :].unsqueeze(2).to_broadcast([P, HEADS, DH]),
                                    ALU.mult).then_inc(post_read, 1)
                elif kind == T2:
                    src = bank[:, 0:KD * P].rearrange("p (k n) -> p k n", k=KD)
                    split(on_p[t % 2][0][:, :, :], on_p[t % 2][1][:, :, :], src).then_inc(post_read, 1)
                elif kind == T3:
                    dve.wait_ge(bo_added, n + 1)
                    v.scalar_tensor_tensor(x_sb[:, tile, :], bank[:, 0:D], tanh_g[:, 0:1],
                                           x_sb[:, tile, :], ALU.mult, ALU.add).then_inc(post_read, 1)
                    dve.wait_ge(post_read, fill[0])
                    last = stats(1, tile, t)
                    if t < QT - 1:
                        step(last)
                    else:
                        last.then_inc(stats_done, 1)
                        stat_rounds[0] += 1
                elif kind == T4:
                    v.tensor_copy(n_t[:, 2 * t:2 * t + 2, :, :], bank[:, :].rearrange("p (t k n) -> p t k n", t=2, k=KD)
                                  ).then_inc(post_read, 1)
                elif kind == T5:
                    v.tensor_copy(logits[:, 2 * t:2 * t + 2, :],
                                  bank[:, 0:2 * E].rearrange("p (t e) -> p t e", t=2)).then_inc(post_read, 1)
                    if t == 1:
                        dve.wait_ge(post_read, fill[0])
                        top_two(n)
                else:
                    places(n, bank)

            def top_two(n):
                rows = slice(n * QT, (n + 1) * QT)
                step(v.tensor_scalar(z_c[:, :, :], logits[:, :, :], Z_LOW, Z_HIGH, ALU.max, ALU.min))
                settle()
                for t in range(QT):
                    step(v.max(z_top[:, t, :], z_c[:, t, :]))
                settle()
                for t in range(QT):
                    step(v.max_index(e_top[:, t, :], z_top[:, t, :], z_c[:, t, :]))
                step(v.tensor_copy(z_all[:, rows, :], z_top[:, :, 0:2]))
                settle()
                step(v.tensor_copy(e_all[:, :, rows].rearrange("p c t -> p t c"), e_top[:, :, 0:2]))
                settle()
                for c in range(2):
                    step(v.tensor_tensor(mask[c][:, :, :], iota_e[:, :].unsqueeze(1).to_broadcast([P, QT, E]),
                                         e_all[:, c, rows].unsqueeze(2).to_broadcast([P, QT, E]), ALU.is_equal))
                settle()
                v.tensor_tensor(mask_s[:, :, :], mask[0][:, :, :], mask[1][:, :, :], ALU.add
                                ).then_inc(masks_done, 1)
                if n > 0:
                    dve.wait_ge(scattered, 16 * 2 * QT * n)
                step(v.tensor_copy(second[:, :, 0:D], normed[:, rows, 0:D]))
                step(v.tensor_scalar(second[:, :, D].bitcast(I32), normed[:, rows, D].bitcast(I32),
                                     B * NQ, None, ALU.add))

            def places(n, bank):
                rows = slice(n * QT, (n + 1) * QT)
                settle()
                if n == 0:
                    step(v.memset(upto[:, 0, :], 0.0))
                else:
                    step(v.tensor_copy(upto[:, 0, :], upto[:, QT, :]))
                settle()
                for t in range(QT):
                    step(v.tensor_tensor(upto[:, t + 1, :], upto[:, t, :],
                                         bank[:, (QT + t) * E:(QT + t + 1) * E], ALU.add))
                    settle()
                v.tensor_tensor(pos[:, :, :], bank[:, 0:QT * E].rearrange("p (t e) -> p t e", t=QT),
                                upto[:, 0:QT, :], ALU.add).then_inc(post_read, 1)
                dve.wait_ge(post_read, fill[0])
                for c in range(2):
                    step(v.tensor_tensor(pick[:, :, :], pos[:, :, :], mask[c][:, :, :], ALU.mult))
                    settle()
                    step(v.tensor_reduce(r_all[:, c, rows], pick[:, :, :], AX.X, ALU.add))
                    settle()
                step(v.scalar_tensor_tensor(dest_f[:, :, :], e_all[:, :, rows], float(CAP), r_all[:, :, rows],
                                            ALU.mult, ALU.add))
                settle()
                v.tensor_copy(dest[:, :, rows], dest_f[:, :, :]).then_inc(dest_done, 1)

            def slots():
                step(v.scalar_tensor_tensor(pad_f[:, :], iota_e[:, :], float(CAP), upto[:, QT, :], ALU.mult, ALU.add))
                step(v.tensor_scalar(n_i[:, :], upto[:, QT, :], float(CHUNK - 1), None, ALU.add))
                settle()
                step(v.tensor_copy(pad_row[:, :], pad_f[:, :]))
                step(v.tensor_scalar(n_s[:, :], n_i[:, :], CHUNK.bit_length() - 1, None, ALU.logical_shift_right))
                settle()
                step(v.tensor_copy(n_slots[:, :], n_s[:, :]))
                step(v.memset(first[:, 0:1], 0.0))
                settle()
                src, dst = n_slots, scan
                for back in (1, 2, 4):
                    out_ = first[:, 1:E + 1] if back == 4 else dst[:, :]
                    step(v.tensor_copy(out_[:, 0:back], src[:, 0:back]))
                    step(v.tensor_tensor(out_[:, back:E], src[:, back:E], src[:, 0:E - back], ALU.add))
                    settle()
                    src, dst = dst, scan_2
                step(v.tensor_copy(n_used[:, :], first[:, E:E + 1]))
                step(v.tensor_scalar(last_slot[:, :], first[:, E:E + 1], -1.0, None, ALU.add))
                settle()
                step(v.tensor_scalar(slot_n[:, :], iota_s[:, :], last_slot[:, 0:1], None, ALU.min))
                settle()
                shape = [P, SLOTS, E - 1]
                step(v.tensor_tensor(reached[:, :, :], slot_n[:, :].unsqueeze(2).to_broadcast(shape),
                                     first[:, 1:E].unsqueeze(1).to_broadcast(shape), ALU.is_ge))
                settle()
                step(v.tensor_reduce(slot_ef[:, :], reached[:, :, :], AX.X, ALU.add))
                settle()
                step(v.tensor_tensor(reached[:, :, :], reached[:, :, :],
                                     n_slots[:, 0:E - 1].unsqueeze(1).to_broadcast(shape), ALU.mult))
                settle()
                step(v.tensor_reduce(slot_1st[:, :], reached[:, :, :], AX.X, ALU.add))
                settle()
                step(v.tensor_copy(slot_e[:, :], slot_ef[:, :]))
                step(v.tensor_tensor(slot_n[:, :], slot_n[:, :], slot_1st[:, :], ALU.subtract))
                step(v.tensor_scalar(slot_ef[:, :], slot_ef[:, :], float(CAP), None, ALU.mult))
                settle()
                step(v.scalar_tensor_tensor(slot_n[:, :], slot_n[:, :], float(CHUNK), slot_ef[:, :], ALU.mult, ALU.add))
                settle()
                v.tensor_copy(slot_row[:, :], slot_n[:, :]).then_inc(slots_done, 1)

            def norm_mlp(n):
                dve.wait_ge(rstd_done, stat_rounds[0])
                dve.wait_ge(loaded_nw, 16)
                for t in range(QT):
                    step(v.tensor_scalar(normed[:, n * QT + t, 0:D], x_sb[:, n * QT + t, :], mv[:, 1, t, 0:1],
                                         rs[:, 1, t:t + 1], ALU.subtract, ALU.mult))
                settle()
                at_rows = normed[:, n * QT:(n + 1) * QT, 0:D]
                v.tensor_tensor(at_rows, at_rows, nw_bc[:, :].unsqueeze(1).to_broadcast([P, QT, D]),
                                ALU.mult).then_inc(normed_done, 1)


            dve.wait_ge(b1_read, 1)
            step(v.tensor_copy(b1_all[:, :, :], pv[:, 0:HM * (E + 1)].rearrange("p (s m) -> p s m", s=E + 1)))
            step(v.tensor_copy(qk_col[:, :], pv[:, HM * (E + 1):HM * (E + 1) + 2 * KD]))
            v.tensor_copy(rw_t[:, :, :], pv[:, P:P + KD * E].rearrange("p (k e) -> p k e", k=KD)
                          ).then_inc(b1_read, 1)

            SPLIT_AT = {(0, TC, 2): ((1, wk_p, CH),), (0, K, 0): ((2, wv_p, CH), (0, wq_p, P), (3, wo_p, P))}
            for f, (n, kind, j) in enumerate(PREP):
                if (n, kind, j) == (0, V, 0):
                    dve.wait_ge(loaded_small, 80)
                if (n, kind, j) in SPLIT_AT:
                    dve.wait_ge(loaded_w, 64)
                    for i, w, rows in SPLIT_AT[n, kind, j]:
                        raw = w_raw[0:rows, i, :].rearrange("p (k n) -> p k n", k=2)
                        split(w[0][:, :, :], w[1][:, :, :], raw).then_inc(w_split, 1)
                if (n, kind, j) == (0, K, 0):
                    ln_x_stats(0)
                if (kind, j) == LN_AT:
                    ln_x(n)
                if n + 1 < B and (kind, j) == STATS_AT:
                    ln_x_stats(n + 1)
                if f == FILLS - 1:
                    check_v()
                prep(f)
            dve.wait_ge(consts_set, 1)
            check_qk()
            dve.wait_ge(tanh_done, 1)

            def heads_out(b, g):
                at = b * GROUPS + g
                dve.wait_ge(pv_done, (at + 1) * KT)
                v.tensor_copy(o_t[:, g, :], pv[:, :]).then_inc(pv_read, 1)

            def split_x(i):
                bank = filled()
                if CHUNKS[i][0] == R:
                    dve.wait_ge(y_out[i % 2], 32 * stores(i % 2, i - 3))
                    step(v.tensor_copy(y_row[i % 4][:, :], x_in[CHUNKS[i][1] % 2][:, :, D].bitcast(U32)))
                if i >= 2:
                    dve.wait_ge(h_done, (i - 1) * HM // 2)
                src = bank[:, :].rearrange("p (k n) -> p k n", k=KD)
                split(xt_p[i % 2][0][:, :, :], xt_p[i % 2][1][:, :, :], src).then_inc(post_read, 1)

            def w1_low(s):
                dve.wait_ge(w1_hi, s + 1)
                v.tensor_tensor(w1_p[s % 2][1][:, :, :], w1_raw[s % 2],
                                w1_p[s % 2][0][:, :, :].bitcast(F32), ALU.subtract).then_inc(w1_lo, 1)

            def fast_attention():
                for b in range(B):
                    for s in range(WS):
                        if s % KT == KT - 1:
                            heads_out(b, s // KT)
                        if (i := post_slot(b, s)) is not None:
                            post(b - 1, i)
                        if b >= 1 and s == NORM_AT:
                            norm_mlp(b - 1)
                        if b * WS + s == SPLIT_1 + 2:
                            w1_low(0)
                        if b * WS + s == B * WS - 1:
                            split_x(0)

            def general_attention():
                slow = [0]

                def slowly(ins):
                    slow[0] += 1
                    ins.then_inc(slow_step, 1)
                    dve.wait_ge(slow_step, slow[0])

                slowly(v.memset(is_num[:, :, :], 1.0))
                u = 0
                for pair in range(B * GROUPS * 2):
                    i = pair % 2
                    if pair >= 2:
                        dve.wait_ge(slow_max_out, 16 * (pair - 1))
                    slowly(v.memset(high[i][:, :, :], -CLAMP))
                    for kt in range(KT):
                        u += 1
                        dve.wait_ge(slow_scores, u)
                        slowly(v.tensor_copy(clip[0][:, :, :], sc[i][:, :, :]))
                        slowly(v.tensor_tensor(clip[1][:, :, :], clip[0][:, :, :], clip[0][:, :, :], ALU.is_equal))
                        slowly(v.tensor_tensor(is_num[:, :, :], is_num[:, :, :], clip[1][:, :, :], ALU.min))
                        slowly(v.tensor_scalar(clip[0][:, :, :], clip[0][:, :, :], SCALE, CLAMP, ALU.mult, ALU.min))
                        ins = v.tensor_tensor(high[i][:, :, :], high[i][:, :, :], clip[0][:, :, :], ALU.max)
                        if kt < KT - 1:
                            slowly(ins)
                        else:
                            ins.then_inc(slow_high, 1)
                            dve.wait_ge(slow_high, pair + 1)
                slowly(v.tensor_reduce(keep[:, 1:2], is_num[:, :, :], AX.XY, ALU.min))
                v.tensor_scalar(keep[:, 0:1], keep[:, 1:2], -1.0, 1.0, ALU.mult, ALU.add).then_inc(slow_num, 1)
                dve.wait_ge(slow_keep, 1)
                slowly(v.tensor_scalar(keep[:, 0:1], keep[:, 1:2], -1.0, 1.0, ALU.mult, ALU.add))
                for b in range(B):
                    for s in range(WS):
                        w = b * WS + s
                        for i in range(2):
                            u = 2 * w + i
                            if s % KT == 0:
                                dve.wait_ge(slow_max_in[i], 16 * (b * GROUPS + s // KT + 1))
                                slowly(v.tensor_scalar(high[i][:, :, :], high[i][:, :, :], keep[:, 0:1], None, ALU.mult))
                            dve.wait_ge(scores_done, u + 1)
                            if u >= 2:
                                dve.wait_ge(exp_done, u - 1)
                            slowly(v.tensor_scalar(clip[i][:, :, :], sc[u % 3][:, :, :], SCALE, CLAMP, ALU.mult, ALU.min))
                            slowly(v.tensor_scalar(clip[i][:, :, :], clip[i][:, :, :], -CLAMP, keep[:, 0:1],
                                                   ALU.max, ALU.mult))
                            v.tensor_tensor(clip[i][:, :, :], clip[i][:, :, :], high[i][:, :, :],
                                            ALU.subtract).then_inc(slow_logits, 1)
                        if w == B * WS - 1:
                            w1_low(0)
                            split_x(0)
                        if s % KT == KT - 1:
                            heads_out(b, s // KT)
                    if b < B - 1:
                        for i in range(len(POST)):
                            if i == EARLY:
                                norm_mlp(b)
                            post(b, i)

            dve.wait_ge(flag_done, 1)
            held = dve.value_load(flag[0:1, 0:1], min_val=0, max_val=CHECKS)
            counts = count[0], fill[0], stat_rounds[0]
            with dve.If(held < CHECKS):
                general_attention()
                general = count[0], fill[0], stat_rounds[0]
            with dve.Else():
                count[0], fill[0], stat_rounds[0] = counts
                fast_attention()
                assert general == (count[0], fill[0], stat_rounds[0])
            def weights_of_two():
                dve.wait_ge(exp_z, 1)
                step(v.tensor_scalar(s_top[:, :, :], s_top[:, :, :], 1.0, None, ALU.add))
                settle()
                step(v.reciprocal(w_top[:, :, :], s_top[:, :, :]))
                settle()
                step(v.tensor_tensor(s_sum[:, :], w_top[:, :, 0], w_top[:, :, 1], ALU.add))
                settle()
                step(v.tensor_scalar(s_sum[:, :], s_sum[:, :], TOP_EPS, None, ALU.add))
                settle()
                step(v.reciprocal(s_sum[:, :], s_sum[:, :]))
                settle()
                step(v.scalar_tensor_tensor(w_top[:, :, :], w_top[:, :, :], tanh_g[:, 1:2],
                                            s_sum[:, :].unsqueeze(2).to_broadcast([P, T, 2]), ALU.mult, ALU.mult))

            def split_h(i, q):
                f = i * (HM // 2) + q
                dve.wait_ge(relu_done, f + 1)
                hi, lo = (h_p[i % 2][k][:, 2 * q:2 * q + 2, :] for k in range(2))
                if CHUNKS[i][0] == R:
                    last = split(hi, lo, h_f[f % 2][:, :, :])
                else:
                    last = v.tensor_tensor(lo, h_f[f % 2][:, :, :], hi.bitcast(F32), ALU.subtract)
                last.then_inc(h_split, 1)

            def read_y(i):
                dve.wait_ge(y_done, i + 1)
                y = result_bank(i).rearrange("p (t n) -> p t n", t=2)
                chunk, c = CHUNKS[i]
                s = set_of(i)
                dve.wait_ge(biases_in[s % 3], 32 * (s // 3 + 1))
                dve.wait_ge(y_out[i % 2], 32 * stores(i % 2, i))
                b2 = b2_sb[s % 3][:, :].unsqueeze(1).to_broadcast([P, 2, D])
                if chunk == R:
                    settle()
                    v.tensor_tensor(y_sb[i % 2][:, :, :], y, b2, ALU.add).then_inc(y_read, 1)
                else:
                    step(v.tensor_tensor(y_sb[i % 2][:, :, :], y, b2, ALU.add))
                    settle()
                    v.scalar_tensor_tensor(x_sb[:, 2 * c:2 * c + 2, :], y_sb[i % 2][:, :, :], tanh_g[:, 1:2],
                                           x_sb[:, 2 * c:2 * c + 2, :], ALU.mult, ALU.add).then_inc(y_read, 1)
                dve.wait_ge(y_read, i + 1)

            def combine(t):
                dve.wait_ge(gathered[t // 4], 32)
                for i in range(2):
                    if i == 1:
                        dve.wait_ge(dve_step, count[0] - 1)
                    for u in (t, t + 1):
                        if (i, u) == (1, t + 1):
                            dve.wait_ge(dve_step, count[0])
                        last = v.scalar_tensor_tensor(x_sb[:, u, :], y_all[i][:, u, :], w_top[:, u, i:i + 1],
                                                      x_sb[:, u, :], ALU.mult, ALU.add)
                        if i == 0:
                            step(last)
                        else:
                            last.then_inc(combined, 1)

            step(v.memset(zero_rows[:, :, :], 0.0))
            settle()
            for t in range(2):
                step(v.tensor_scalar(zero_rows[:, t, D:D + 1].bitcast(I32), normed[:, t, D:D + 1].bitcast(I32),
                                     2 * B * NQ, None, ALU.add))
            tiles = 0
            for i in range(len(CHUNKS)):
                s = set_of(i)
                for q in range(EIGHTHS):
                    at_e = EIGHTHS * i + q
                    if at_e == LAST_NORM:
                        norm_mlp(B - 1)
                    for k, when in enumerate(LAST_AT):
                        if when == at_e:
                            post(B - 1, k)
                    if at_e == SLOTS_AT:
                        dve.wait_ge(dest_done, B)
                        slots()
                    if q == turn_at(i) and i + 1 < len(CHUNKS):
                        split_x(i + 1)
                    if q < HM // 2:
                        split_h(i, q)
                    if q == (7 if s == 0 else W1_LOW_AT) and i == last_of(s) and s + 1 < SETS:
                        w1_low(s + 1)
                    if i == AHEAD + 1 and q == 4:
                        weights_of_two()
                    for _ in range(COMBINE_AT.count(at_e)):
                        combine(tiles)
                        tiles += 2
                if i >= 1:
                    read_y(i - 1)
            for t in range(tiles, T, 2):
                combine(t)
            dve.wait_ge(combined, T)
            read_y(len(CHUNKS) - 1)

            used = dve.value_load(n_used[0:1, 0:1], min_val=0, max_val=SLOTS)
            with dve.If(used > MAIN):
                for k in range(LATE):
                    dve.wait_ge(late_in, 80 * (k + 1))
                    dve.wait_ge(late_hi, 2 * k + 1)
                    v.tensor_tensor(w1_p[0][1][:, :, :], w1_raw[0], w1_p[0][0][:, :, :].bitcast(F32),
                                    ALU.subtract).then_inc(late_w1, 1)
                    step(v.tensor_copy(y_row[0][:, :], x_in[0][:, :, D].bitcast(U32)))
                    dve.wait_ge(late_turned, k + 1)
                    split(xt_p[0][0][:, :, :], xt_p[0][1][:, :, :],
                          mb[:, :].rearrange("p (k n) -> p k n", k=KD)).then_inc(late_x, 1)
                    for q in range(HM // 2):
                        dve.wait_ge(late_relu, 4 * k + q + 1)
                        split(h_p[0][0][:, 2 * q:2 * q + 2, :], h_p[0][1][:, 2 * q:2 * q + 2, :],
                              h_f[q % 2][:, :, :]).then_inc(late_split, 1)
                    dve.wait_ge(late_y, k + 1)
                    v.tensor_tensor(y_sb[0][:, :, :], pv[:, :].rearrange("p (t n) -> p t n", t=2),
                                    b2_sb[0][:, :].unsqueeze(1).to_broadcast([P, 2, D]), ALU.add).then_inc(late_result, 1)
                dve.wait_ge(late_back, 32)
                for t in range(T):
                    step(v.scalar_tensor_tensor(x_sb[:, t, :], y_all[0][:, t, :], w_top[:, t, 0:1],
                                                x_sb[:, t, :], ALU.mult, ALU.add))
                    settle()
                    v.scalar_tensor_tensor(x_sb[:, t, :], y_all[1][:, t, :], w_top[:, t, 1:2],
                                           x_sb[:, t, :], ALU.mult, ALU.add).then_inc(late_combined, 1)
            with dve.Else():
                pass

        @block.tensor
        def _(pe):
            mm = nc.tensor.matmul

            def product(dst, lhs, rhs, parts=KD):
                todo = [(k, a, b) for k in range(parts) for a, b in PASSES]
                for i, (k, a, b) in enumerate(todo):
                    last = mm(dst, lhs(a, k), rhs(b, k), start=(i == 0), stop=(i == len(todo) - 1))
                return last

            fill = [0]

            def bank():
                fill[0] += 1
                last = fill[0] - (1 if fill[0] <= FIRST_X else 2)
                if last > 0 and fill[0] != FIRST_X + 1:
                    pe.wait_ge(post_read, last)
                return mb_bank(fill[0])

            def prep(f):
                n, kind, j = PREP[f]
                dst = prep_bank(f)
                if f >= 8:
                    pe.wait_ge(dve_read, f - 7)
                if kind == TX:
                    pe.wait_ge(xn_done, n + 1)
                    for t in range(QT):
                        last = nc.tensor.transpose(dst[:, t * P:(t + 1) * P],
                                                   normed[:, n * QT + t, j * P:(j + 1) * P], ident[:, :])
                elif kind == TC:
                    k, half = j % 2, j // 2
                    pe.wait_ge(loaded_ctx, 16 * (n + 1))
                    for t in range(4):
                        last = nc.tensor.transpose(dst[0:CH, t * P:(t + 1) * P],
                                                   ctx_raw[:, 4 * half + t, k * CH:(k + 1) * CH], ident[:, :])
                elif kind == Q:
                    pe.wait_ge(w_split, 3)
                    pe.wait_ge(dve_read, at(n, TX, KD - 1) + 1)
                    last = product(dst, lambda a, k: wq_p[a][:, k, j * P:(j + 1) * P], lambda a, k: xn_p[a][:, k, :])
                elif kind == K:
                    m, half = j % 2, j // 2
                    pe.wait_ge(w_split, 1)
                    pe.wait_ge(dve_read, at(n, TC, 2 * half + 1) + 1)
                    last = product(dst, lambda a, k: wk_p[a][:, k, m * P:(m + 1) * P],
                                   lambda a, k: ctx_p[a][:, k, half * 512:half * 512 + 512])
                elif kind == V:
                    pe.wait_ge(w_split, 2)
                    for u in range(2):
                        kt = 2 * j + u
                        last = product(dst[:, u * D:(u + 1) * D],
                                       lambda a, k: ctx_p[a][:, k, kt * P:(kt + 1) * P],
                                       lambda a, k: wv_p[a][:, k, :])
                else:
                    pe.wait_ge(heads_set, 1)
                    for m, s in enumerate(norm_staged(n, j)):
                        pe.wait_ge(act_read, acts(at(*STAGED[s])))
                        first_col = PH * (KD - 1 - m)
                        last = mm(dst[0:HEADS, :], head_of[:, first_col:first_col + HEADS], stage_s[s % DEEP][:, :],
                                  start=(m == 0), stop=(m == KD - 1))
                last.then_inc(fill_done, 1)

            def post(n, i):
                kind, t = POST[i]
                dst = bank()
                if kind == T1:
                    pe.wait_ge(pv_read, GROUPS * (n + 1))
                    for g in range(GROUPS):
                        last = nc.tensor.transpose(dst[:, g * P:(g + 1) * P], o_t[:, g, t * P:(t + 1) * P], ident[:, :])
                elif kind == T2:
                    pe.wait_ge(post_read, after(n, T1, t))
                    o = on[t % 2][:, :, :].rearrange("p h d -> p (h d)")
                    for k in range(KD):
                        last = nc.tensor.transpose(dst[:, k * P:(k + 1) * P], o[:, k * P:(k + 1) * P], ident[:, :])
                elif kind == T3:
                    pe.wait_ge(post_read, after(n, T2, t))
                    last = product(dst[:, 0:D], lambda a, k: on_p[t % 2][a][:, k, :], lambda a, k: wo_p[a][:, k, :])
                elif kind == T4:
                    pe.wait_ge(normed_done, n + 1)
                    for u in range(2):
                        for k in range(KD):
                            at = (u * KD + k) * P
                            last = nc.tensor.transpose(dst[:, at:at + P],
                                                       normed[:, n * QT + 2 * t + u, k * P:(k + 1) * P], ident[:, :])
                elif kind == T6:
                    pe.wait_ge(masks_done, n + 1)
                    m = mask_s[:, :, :].rearrange("p t e -> p (t e)")
                    mm(dst[:, 0:QT * E], before[:, :], m, start=True, stop=True)
                    last = mm(dst[:, QT * E:2 * QT * E], ones[:, :], m, start=True, stop=True)
                else:
                    pe.wait_ge(post_read, after(n, T4, t))
                    for u in range(2):
                        for k in range(KD):
                            last = mm(dst[:, u * E:(u + 1) * E], n_t[:, 2 * t + u, k, :], rw_t[:, k, :],
                                      start=(k == 0), stop=(k == KD - 1))
                last.then_inc(post_done, 1)

            def score(dst, i, a, g, kt):
                return mm(dst[:, a, :], k_stack[0:ROWS, 2 * g + i, kt * P:(kt + 1) * P],
                          q_stack[0:ROWS, 2 * g + i, a, :], start=True, stop=True)

            def slow_at(b, g, i, kt):
                pair = (b * GROUPS + g) * 2 + i
                return 1 + pair * (1 + 5 * KT - 1) + 1 + 5 * (kt - 1) + 1

            def scores(w):
                b, g, kt = w // WS, w % WS // KT, w % KT
                if kt == 0:
                    pe.wait_ge(stack_in[g // 2], STACK * (b + 1))
                for i in range(2):
                    u = 2 * w + i
                    if u >= 3:
                        pe.wait_ge(exp_done, u - 2)
                    for a in range(2):
                        last = score(sc[u % 3], i, a, g, kt)
                    last.then_inc(scores_done, 1)

            def values(w):
                b, g, kt = w // WS, w % WS // KT, w % KT
                gg = b * GROUPS + g
                if kt == 0 and gg >= 1:
                    pe.wait_ge(pv_read, gg)
                pe.wait_ge(exp_done, 2 * w + 2)
                for j in range(4):
                    last = mm(pv[32 * j:32 * j + DH + 1, :], v_sb[b][:, kt, 4 * g + j, :],
                              prob[w % 2][j // 2][:, j % 2, :], start=(kt == 0), stop=(kt == KT - 1))
                last.then_inc(pv_done, 1)

            pe.wait_ge(ident_set, 1)
            pe.wait_ge(loaded_bias, 80)
            nrows = HM * (E + 1) + 2 * KD
            nc.tensor.transpose(pv[:, 0:nrows], bias_rows[0:nrows, :], ident[0:nrows, 0:nrows])
            for k in range(KD):
                last = nc.tensor.transpose(pv[:, P + k * E:P + (k + 1) * E], rw_rows[:, k * P:(k + 1) * P], ident[0:E, 0:E])
            last.then_inc(b1_read, 1)

            pe.wait_ge(b1_read, 2)
            for f in range(FILLS):
                prep(f)
            pe.wait_ge(consts_set, 1)
            pe.wait_ge(checks_done, 1)
            mm(mb[0:1, 0:2], ones[:, 0:1], checks[:, :], start=True, stop=True).then_inc(checks_sum, 1)

            def turn_x(i):
                dst = bank()
                chunk, c = CHUNKS[i]
                if chunk == R:
                    pe.wait_ge(x_in_done[c % 2], 16 * (c // 2 + 1))
                else:
                    pe.wait_ge(normed_done, (2 * c + 1) // QT + 1)
                for k in range(KD):
                    for t in range(2):
                        src = (normed[:, 2 * c + t, k * P:(k + 1) * P] if chunk == S
                               else x_in[c % 2][:, t, k * P:(k + 1) * P])
                        at = (2 * k + t) * P
                        last = nc.tensor.transpose(dst[:, at:at + P], src, ident[:, :])
                last.then_inc(post_done, 1)

            def fast_attention():
                scores(0)
                for b in range(B):
                    for s in range(WS):
                        w = b * WS + s
                        if w + 1 < B * WS:
                            scores(w + 1)
                        values(w)
                        if (i := post_slot(b, s)) is not None:
                            post(b - 1, i)
                        if w == B * WS - 2:
                            turn_x(0)

            def general_attention():
                u = 0
                for b in range(B):
                    for g in range(GROUPS):
                        if b:
                            pe.wait_ge(slow_stack, STACK * ((b - 1) * 2 + g // 2 + 1))
                        else:
                            pe.wait_ge(stack_in[g // 2], STACK)
                        for i in range(2):
                            for kt in range(KT):
                                if kt:
                                    pe.wait_ge(slow_step, slow_at(b, g, i, kt))
                                elif i or g or b:
                                    pe.wait_ge(slow_high, (b * GROUPS + g) * 2 + i)
                                for a in range(2):
                                    last = score(sc[i], i, a, g, kt)
                                last.then_inc(slow_scores, 1)
                pe.wait_ge(slow_stack, STACK * B * 2)
                pe.wait_ge(slow_keep, 1)
                for b in range(B):
                    for s in range(WS):
                        scores(b * WS + s)
                        if b * WS + s == B * WS - 1:
                            turn_x(0)
                        values(b * WS + s)
                    if b < B - 1:
                        for i in range(len(POST)):
                            post(b, i)

            pe.wait_ge(flag_done, 1)
            held = pe.value_load(flag[0:1, 0:1], min_val=0, max_val=CHECKS)
            fills = fill[0]
            with pe.If(held < CHECKS):
                general_attention()
            with pe.Else():
                fill[0] = fills
                fast_attention()
            def hidden(i, q):
                s = set_of(i)
                f = i * (HM // 2) + q
                if q == 0:
                    pe.wait_ge(post_read, mb_count((X, i)))
                    pe.wait_ge(w1_lo, s + 1)
                if f >= 4:
                    pe.wait_ge(relu_done, f - 3)
                for r in range(2):
                    m = 2 * q + r
                    last = product(hps(f)[:, r, :], lambda a, k: w1_p[s % 2][a][:, k, m * P:(m + 1) * P],
                                   lambda a, k: xt_p[i % 2][a][:, k, :])
                last.then_inc(h_done, 1)

            def results(i, e):
                s = set_of(i)
                if e == 0:
                    pe.wait_ge(w2_lo, s + 1)
                    pe.wait_ge(h_split, (i + 1) * HM // 2)
                    if i >= 2:
                        pe.wait_ge(y_read, i - 1)
                t, half = e // 2, e % 2
                for k in range(half * HM // 2, (half + 1) * HM // 2):
                    for a, b in PASSES:
                        last = mm(result_bank(i)[:, t * D:(t + 1) * D], h_p[i % 2][a][:, k, t * P:(t + 1) * P],
                                  w2_p[s % 2][b][:, k, :], start=((k, a, b) == (0, 0, 0)),
                                  stop=((k, a, b) == (HM - 1, 1, 0)))
                if e == 3:
                    last.then_inc(y_done, 1)

            pe.wait_ge(pv_read, B * GROUPS)
            for i in range(len(CHUNKS)):
                for q in range(EIGHTHS):
                    for k, when in enumerate(LAST_AT):
                        if when == EIGHTHS * i + q:
                            post(B - 1, k)
                    if q == turn_at(i) and i + 1 < len(CHUNKS):
                        turn_x(i + 1)
                    if q < HM // 2:
                        hidden(i, q)
                    elif i >= 1:
                        results(i - 1, q - HM // 2)
            for e in range(4):
                results(len(CHUNKS) - 1, e)

            used = pe.value_load(n_used[0:1, 0:1], min_val=0, max_val=SLOTS)
            with pe.If(used > MAIN):
                for k in range(LATE):
                    pe.wait_ge(late_in, 80 * (k + 1))
                    for part in range(KD):
                        for t in range(2):
                            cols = slice((2 * part + t) * P, (2 * part + t + 1) * P)
                            last = nc.tensor.transpose(mb[:, cols], x_in[0][:, t, part * P:(part + 1) * P], ident[:, :])
                    last.then_inc(late_turned, 1)
                    pe.wait_ge(late_x, k + 1)
                    pe.wait_ge(late_w1, k + 1)
                    for q in range(HM // 2):
                        for m in (2 * q, 2 * q + 1):
                            last = product(hps(q)[:, m % 2, :], lambda a, k: w1_p[0][a][:, k, m * P:(m + 1) * P],
                                           lambda a, k: xt_p[0][a][:, k, :])
                        last.then_inc(late_h, 1)
                    pe.wait_ge(late_split, 4 * (k + 1))
                    pe.wait_ge(late_w2, k + 1)
                    for t in range(2):
                        last = product(pv[:, t * D:(t + 1) * D], lambda a, k: h_p[0][a][:, k, t * P:(t + 1) * P],
                                       lambda a, k: w2_p[0][a][:, k, :], HM)
                    last.then_inc(late_y, 1)
            with pe.Else():
                pass


_INS = ['x', 'ctx_768', 'g_xattn', 'g_ffn', 'L0_xattn_Wq', 'L0_xattn_bq', 'L0_xattn_Wk', 'L0_xattn_bk',
        'L0_xattn_Wv', 'L0_xattn_bv', 'L0_xattn_Wo', 'L0_xattn_bo', 'L0_ffn_norm_weight', 'L0_ffn_router_w',
        'L0_ffn_sw1', 'L0_ffn_sb1', 'L0_ffn_sw2', 'L0_ffn_sb2', 'L0_ffn_ew1', 'L0_ffn_eb1', 'L0_ffn_ew2',
        'L0_ffn_eb2']


def kernel(**inputs):
    import numpy as np
    import concourse.bacc as bacc
    from concourse.bass_utils import run_bass_kernel_spmd

    nc = bacc.Bacc("TRN2", target_bir_lowering=False, num_devices=1)
    arrays, args = {}, []
    for name in _INS:
        a = np.ascontiguousarray(inputs[name])
        arrays[f"in_{name}"] = a
        args.append(nc.dram_tensor(f"in_{name}", a.shape, mybir.dt.from_np(a.dtype), kind="ExternalInput").ap())
    out = nc.dram_tensor("out", inputs["x"].shape, F32, kind="ExternalOutput").ap()
    flamingo_block(nc, *args, out)
    r = run_bass_kernel_spmd(nc, [arrays], core_ids=[0])
    return r.results[0]["out"]
```
